# Optimizing a Trainium2 kernel written in Bass

```python
import numpy as np
import jax
import jax.numpy as jnp

def _softmax(x, axis=-1):
    return jax.nn.softmax(x, axis=axis)

def _gelu(x):
    return jax.nn.gelu(x, approximate=True)

def _silu(x):
    return jax.nn.silu(x)

def _sigmoid(x):
    return jax.nn.sigmoid(x)

def _layernorm(x, axis=-1, eps=1e-05):
    m = jnp.mean(x, axis=axis, keepdims=True)
    v = jnp.var(x, axis=axis, keepdims=True)
    return (x - m) / jnp.sqrt(v + eps)

def _scatter_add(tgt, idx, src, axis=0):
    return tgt.at[idx].add(src)

def _segment_sum(src, seg, n):
    return jax.ops.segment_sum(src, seg, n)
kernel_name = 'mk_decoder_postln_d1_seqx_r2_85cf12'

def setup_inputs(seed: int=0):
    np.random.seed(seed)
    _w = jnp.asarray

    def _rec_inputs():
        import jax
        import jax.numpy as jnp
        _rk = jax.random.key(seed)
        x = 0.0002417 + 0.9998 * jax.random.normal(jax.random.fold_in(_rk, 1), (8, 512, 512), jnp.float32)
        _lenS = 512 - jax.random.randint(jax.random.fold_in(_rk, 7), (8,), 0, max(1, 512 // 4) + 1, jnp.int32)
        _lenS2 = 512 - jax.random.randint(jax.random.fold_in(_rk, 8), (8,), 0, max(1, 512 // 4) + 1, jnp.int32)
        _ctx_1024P = jax.random.normal(jax.random.fold_in(_rk, 11), (8, 16, 512), jnp.float32)
        _ctx_1024c = jax.random.dirichlet(jax.random.fold_in(_rk, 511), 0.3 * jnp.ones((16,), jnp.float32), (8, 512))
        _ctx_1024t = jnp.einsum('bsk,bkd->bsd', _ctx_1024c, _ctx_1024P)
        _ctx_1024t = _ctx_1024t * jax.lax.rsqrt(jnp.mean(jnp.square(_ctx_1024t)) + 1e-12) * 0.953939
        ctx_1024 = 7.22013e-05 + 1.00017 * (_ctx_1024t + 0.3 * jax.random.normal(jax.random.fold_in(_rk, 611), (8, 512, 512), jnp.float32))
        return (x, ctx_1024)
    x, ctx_1024 = _rec_inputs()

    def _L0_attn_setup():
        import math
        import jax, jax.numpy as jnp
        import numpy as np
        N_EMBD = 512
        N_HEAD = 16
        B, T = (2, 1024)

        def _heads(t):
            b, s, d = t.shape
            return t.reshape(b, s, N_HEAD, d // N_HEAD).transpose(0, 2, 1, 3)
        key = jax.random.key(seed)
        ks = jax.random.split(key, 7)
        D = N_EMBD
        s = 0.02
        return {'x': jax.random.normal(ks[0], (B, T, D), dtype=jnp.float32), 'w_attn': jax.random.normal(ks[1], (2 * D, D), dtype=jnp.float32) * s, 'b_attn': jnp.zeros((2 * D,), dtype=jnp.float32), 'w_k2': jax.random.normal(ks[2], (D, D), dtype=jnp.float32) * s, 'b_k2': jnp.zeros((D,), dtype=jnp.float32), 'w_proj': jax.random.normal(ks[3], (D, D), dtype=jnp.float32) * s, 'b_proj': jnp.zeros((D,), dtype=jnp.float32)}
    _L0_attn_all = _L0_attn_setup()
    _L0_attn_in = {k: v for k, v in _L0_attn_all.items() if k in ('w_attn', 'b_attn', 'w_k2', 'b_k2', 'w_proj', 'b_proj')}
    del _L0_attn_all

    def _L0_xattn_setup():
        import jax, jax.numpy as jnp
        import numpy as np
        EMBED = 512
        HEADS = 16
        HEAD_DIM = EMBED // HEADS
        key = jax.random.key(seed)
        ks = jax.random.split(key, 8)
        N, L = (4, 1024)
        inp = {'values': jax.random.normal(ks[0], (N, L, EMBED), dtype=jnp.float32), 'keys': jax.random.normal(ks[1], (N, L, EMBED), dtype=jnp.float32), 'query': jax.random.normal(ks[2], (N, L, EMBED), dtype=jnp.float32), 'Wv': jax.random.normal(ks[3], (HEAD_DIM, HEAD_DIM), dtype=jnp.float32) * (1.0 / np.sqrt(HEAD_DIM)), 'Wk': jax.random.normal(ks[4], (HEAD_DIM, HEAD_DIM), dtype=jnp.float32) * (1.0 / np.sqrt(HEAD_DIM)), 'Wq': jax.random.normal(ks[5], (HEAD_DIM, HEAD_DIM), dtype=jnp.float32) * (1.0 / np.sqrt(HEAD_DIM)), 'Wo': jax.random.normal(ks[6], (EMBED, EMBED), dtype=jnp.float32) * (1.0 / np.sqrt(EMBED)), 'bo': jax.random.normal(ks[7], (EMBED,), dtype=jnp.float32) * 0.01}
        return inp
    _L0_xattn_all = _L0_xattn_setup()
    _L0_xattn_in = {k: v for k, v in _L0_xattn_all.items() if k in ('Wv', 'Wk', 'Wq', 'Wo', 'bo')}
    del _L0_xattn_all

    def _L0_ffn_setup():
        import jax, jax.numpy as jnp
        import numpy as np
        B, S, D, E = (4, 2048, 512, 8)
        key = jax.random.key(seed)
        ks = jax.random.split(key, 6)
        scale = 1.0 / np.sqrt(D)
        return {'tokens': jax.random.normal(ks[0], (B, S, D), dtype=jnp.float32), 'gate_w': jax.random.normal(ks[1], (D, E), dtype=jnp.float32) * scale, 'w0': jax.random.normal(ks[2], (D, D), dtype=jnp.float32) * scale, 'b0': jax.random.normal(ks[3], (D,), dtype=jnp.float32) * 0.01, 'w1': jax.random.normal(ks[4], (D, D), dtype=jnp.float32) * scale, 'b1': jax.random.normal(ks[5], (D,), dtype=jnp.float32) * 0.01}
    _L0_ffn_all = _L0_ffn_setup()
    _L0_ffn_in = {k: v for k, v in _L0_ffn_all.items() if k in ('gate_w', 'w0', 'b0', 'w1', 'b1')}
    del _L0_ffn_all
    return {'x': x, 'ctx_1024': ctx_1024, 'L0_attn_w_attn': _L0_attn_in['w_attn'], 'L0_attn_b_attn': _L0_attn_in['b_attn'], 'L0_attn_w_k2': _L0_attn_in['w_k2'], 'L0_attn_b_k2': _L0_attn_in['b_k2'], 'L0_attn_w_proj': _L0_attn_in['w_proj'], 'L0_attn_b_proj': _L0_attn_in['b_proj'], 'L0_xattn_Wv': _L0_xattn_in['Wv'], 'L0_xattn_Wk': _L0_xattn_in['Wk'], 'L0_xattn_Wq': _L0_xattn_in['Wq'], 'L0_xattn_Wo': _L0_xattn_in['Wo'], 'L0_xattn_bo': _L0_xattn_in['bo'], 'L0_ffn_gate_w': _L0_ffn_in['gate_w'], 'L0_ffn_w0': _L0_ffn_in['w0'], 'L0_ffn_b0': _L0_ffn_in['b0'], 'L0_ffn_w1': _L0_ffn_in['w1'], 'L0_ffn_b1': _L0_ffn_in['b1']}

def reference(x, ctx_1024, L0_attn_w_attn, L0_attn_b_attn, L0_attn_w_k2, L0_attn_b_k2, L0_attn_w_proj, L0_attn_b_proj, L0_xattn_Wv, L0_xattn_Wk, L0_xattn_Wq, L0_xattn_Wo, L0_xattn_bo, L0_ffn_gate_w, L0_ffn_w0, L0_ffn_b0, L0_ffn_w1, L0_ffn_b1):
    import jax
    import jax.numpy as jnp

    def _L0_attn_ref(x, w_attn, b_attn, w_k2, b_k2, w_proj, b_proj):
        import math
        import jax, jax.numpy as jnp
        import numpy as np
        N_EMBD = 512
        N_HEAD = 16
        B, T = (2, 1024)

        def _heads(t):
            b, s, d = t.shape
            return t.reshape(b, s, N_HEAD, d // N_HEAD).transpose(0, 2, 1, 3)
        b, t, d = x.shape
        hd = d // N_HEAD
        scale = 1.0 / math.sqrt(hd)
        qk = x @ w_attn.T + b_attn
        q, k = jnp.split(qk, 2, axis=-1)
        q, k, v = (_heads(q), _heads(k), _heads(x))
        scores = jnp.einsum('bhqd,bhkd->bhqk', q, k) * scale
        causal = jnp.tril(jnp.ones((t, t), dtype=bool))
        scores = jnp.where(causal, scores, -jnp.inf)
        y_ar = jnp.einsum('bhqk,bhkd->bhqd', jax.nn.softmax(scores, axis=-1), v)
        e = v[:, :, 1:, :] - y_ar[:, :, :-1, :]
        q2 = q[:, :, 1:, :]
        k2 = _heads(x[:, :-1] @ w_k2.T + b_k2)
        qa = -jax.nn.leaky_relu(-q2 * scale, negative_slope=0.02)
        ka = jax.nn.sigmoid(k2 * scale * 0.02)
        ma = jnp.einsum('bhqd,bhkd->bhqk', qa, ka)
        ma = jnp.where(jnp.tril(jnp.ones((t - 1, t - 1), dtype=bool)), ma, 0.0)
        y_ma = jnp.einsum('bhqk,bhkd->bhqd', ma, e)
        y_ma = jnp.concatenate([jnp.zeros_like(y_ma[:, :, :1, :]), y_ma], axis=2)

        def merge(z):
            return z.transpose(0, 2, 1, 3).reshape(b, t, d)
        out = merge(y_ar) @ w_proj.T + b_proj + (merge(y_ma) @ w_proj.T + b_proj)
        return out

    def _L0_xattn_ref(values, keys, query, Wv, Wk, Wq, Wo, bo):
        import jax, jax.numpy as jnp
        import numpy as np
        EMBED = 512
        HEADS = 16
        HEAD_DIM = EMBED // HEADS
        N, Lq, _ = query.shape
        Lv = values.shape[1]
        Lk = keys.shape[1]
        v = values.reshape(N, Lv, HEADS, HEAD_DIM)
        k = keys.reshape(N, Lk, HEADS, HEAD_DIM)
        q = query.reshape(N, Lq, HEADS, HEAD_DIM)
        v = jnp.einsum('nlhd,ed->nlhe', v, Wv)
        k = jnp.einsum('nlhd,ed->nlhe', k, Wk)
        q = jnp.einsum('nlhd,ed->nlhe', q, Wq)
        energy = jnp.einsum('nqhd,nkhd->nhqk', q, k)
        attention = jax.nn.softmax(energy / jnp.sqrt(jnp.float32(EMBED)), axis=-1)
        out = jnp.einsum('nhql,nlhd->nqhd', attention, v).reshape(N, Lq, EMBED)
        return out @ Wo.T + bo

    def _L0_ffn_ref(tokens, gate_w, w0, b0, w1, b1):
        import jax, jax.numpy as jnp
        import numpy as np
        B, S, D, E = (4, 2048, 512, 8)
        b, s, d = tokens.shape
        logits = jnp.einsum('bsd,de->bse', tokens, gate_w)
        weights = jax.nn.softmax(logits, axis=-1)
        topk_w, topk_idx = jax.lax.top_k(weights, 2)
        x = tokens.reshape(b * s, d)
        fw = topk_w.reshape(b * s, 2)
        fidx = topk_idx.reshape(b * s, 2)
        e0 = jax.nn.silu(x @ w0.T + b0)
        e1 = jax.nn.silu(x @ w1.T + b1)
        m0 = (fidx[:, 0:1] == 0).astype(x.dtype)
        m1 = (fidx[:, 1:2] == 1).astype(x.dtype)
        out = e0 * fw[:, 0:1] * m0 + e1 * fw[:, 1:2] * m1
        return out.reshape(b, s, d)
    x = _layernorm(x + _L0_attn_ref(x, L0_attn_w_attn, L0_attn_b_attn, L0_attn_w_k2, L0_attn_b_k2, L0_attn_w_proj, L0_attn_b_proj), axis=-1)
    x = _layernorm(x + _L0_xattn_ref(ctx_1024, ctx_1024, x, L0_xattn_Wv, L0_xattn_Wk, L0_xattn_Wq, L0_xattn_Wo, L0_xattn_bo), axis=-1)
    x = _layernorm(x + _L0_ffn_ref(x, L0_ffn_gate_w, L0_ffn_w0, L0_ffn_b0, L0_ffn_w1, L0_ffn_b1), axis=-1)
    return x

_drawn_inputs = setup_inputs


def setup_inputs(seed=0):
    import zlib

    import numpy as np

    out = dict(_drawn_inputs(seed))
    spreads = {'L0_attn_b_attn': (0.0, 0.1), 'L0_attn_b_k2': (0.0, 2.0), 'L0_attn_b_proj': (0.0, 0.1)}
    factors = {'L0_attn_w_k2': 200.0, 'L0_xattn_bo': 5.686, 'L0_ffn_b0': 64.0, 'L0_ffn_b1': 64.0}
    for name, (base, spread) in spreads.items():
        noise = np.random.default_rng([zlib.crc32(name.encode()), seed]).standard_normal(out[name].shape)
        drawn = base * np.exp(spread * noise) if base else spread * noise
        out[name] = jnp.asarray(drawn.astype(out[name].dtype))
    for name, factor in factors.items():
        out[name] = (out[name] * factor).astype(out[name].dtype)
    return out
```

```python
from contextlib import ExitStack

import numpy as np

import concourse.bass as bass
from concourse import mybir

F32 = mybir.dt.float32
F32R = mybir.dt.float32r
BF16 = mybir.dt.bfloat16
I32 = mybir.dt.int32
U32 = mybir.dt.uint32
ALU = mybir.AluOpType
ACT = mybir.ActivationFunctionType
AX = mybir.AxisListType.X

BATCH, SEQ, DIM, HEADS, EXPERTS = 8, 512, 512, 16, 8
P = 128
HEAD_DIM = DIM // HEADS
TILES = SEQ // P
GROUPS = DIM // P
PER = P // HEAD_DIM
NG = BATCH * GROUPS
SCALE_SELF = float(HEAD_DIM) ** -0.5
SCALE_CROSS = float(DIM) ** -0.5
LEAK = 0.02
EPS = 1e-5
NEG = -1.0e30
RSQRT_MAGIC = float(0x5F3759DF)


class Flag:

    def __init__(self, sem):
        self.sem, self.count = sem, 0


class Program:

    ENGINES = ("tensor", "vector", "scalar", "gpsimd", "sync")

    def __init__(self, nc, ctx):
        self.nc, self.ctx = nc, ctx
        self.queue = {e: [] for e in self.ENGINES}
        self.waited = {e: {} for e in self.ENGINES}

    def flag(self, name):
        return Flag(self.ctx.enter_context(self.nc.semaphore(name)))

    def put(self, engine, build, waits=(), flag=None, by=1):
        seen, need = self.waited[engine], {}
        for w in waits:
            if w is not None and seen.get(w[0], 0) < w[1]:
                need[w[0]] = max(need.get(w[0], 0), w[1])
        seen.update(need)
        self.queue[engine].append((list(need.items()), build, flag, by))
        if flag is None:
            return None
        flag.count += by
        return (flag, flag.count)

    def emit(self, engine, eng):
        for need, build, flag, by in self.queue[engine]:
            for f, value in need:
                eng.wait_ge(f.sem, value)
            ins = build(eng)
            if flag is not None:
                ins.then_inc(flag.sem, by)


def build(nc, t):
    sems = ExitStack()
    with sems:
        prog = Program(nc, sems)
        shared = Shared(nc, sems, prog)
        for phase in (self_softmax_phase, self_memory_phase, cross_phase):
            with ExitStack() as ctx:
                phase(nc, ctx, prog, shared, t)
        prog.put("sync", lambda e: e.nop(), waits=shared.stores)
        with nc.Block() as block:
            for engine in Program.ENGINES:
                bind(block, prog, engine)


def bind(block, prog, engine):
    def body(eng):
        prog.emit(engine, eng)

    {"tensor": block.tensor, "vector": block.vector, "scalar": block.scalar,
     "gpsimd": block.gpsimd, "sync": block.sync}[engine](body)


class Shared:

    def __init__(self, nc, ctx, prog):
        def sb(name, shape, dt=F32):
            return ctx.enter_context(nc.sbuf_tensor(name, shape, dt))

        self.bank = [ctx.enter_context(nc.psum_tensor(f"bank{i}", [P, 512], F32)) for i in range(8)]
        self.bank_read = [None] * 8
        self.ident = sb("ident", [P, P])
        self.identb = sb("identb", [P, P], BF16)
        self.future = sb("future", [P, P], BF16)
        self.ones = sb("ones", [P, HEAD_DIM])
        self.prog, self.pool_last = prog, None
        self.wall = []
        self.stores = []
        names = ("scores", "scores_t", "pv", "dense", "small_t")
        self.pe = {n: prog.flag(f"pe_{n}") for n in names}
        self.dve = {n: prog.flag(f"dve_{n}") for n in ("max", "split", "norm", "ln", "misc", "ffn")}
        self.act = {n: prog.flag(f"act_{n}") for n in ("exp", "evac", "misc")}
        self.pool = {n: prog.flag(f"pool_{n}") for n in ("mask", "const")}

        const = self.pool["const"]
        on_pool(self, lambda e: e.memset(self.ident[:, :], 0.0), [], const)
        on_pool(self, lambda e: e.memset(self.identb[:, :], 0.0), [], const)
        on_pool(self, lambda e: e.memset(self.future[:, :], 0.0), [], const)
        on_pool(self, lambda e: e.memset(self.ones[:, :], 1.0), [], const)
        for m in (self.ident, self.identb):
            on_pool(self, lambda e, m=m: e.affine_select(
                out=m[:, :], in_=m[:, :], compare_op=ALU.not_equal, fill=1.0, base=0,
                pattern=[[-1, P]], channel_multiplier=1), [], const)
        self.const = on_pool(self, lambda e: e.affine_select(
            out=self.future[:, :], in_=self.future[:, :], compare_op=ALU.is_ge, fill=NEG, base=0,
            pattern=[[-1, P]], channel_multiplier=1), [], const)


def on_pool(sh, build, waits, flag):
    sh.pool_last = sh.prog.put("gpsimd", build, waits=[*waits, sh.pool_last], flag=flag)
    return sh.pool_last


def split(prog, engine_hi, hi, lo, x, waits, flag, act_flag=None):
    if engine_hi == "scalar":
        got = prog.put("scalar", lambda e: e.activation(hi, x, ACT.Copy), waits=waits, flag=act_flag)
    else:
        got = prog.put("vector", lambda e: e.tensor_copy(hi, x), waits=waits, flag=flag)
    return prog.put("vector", lambda e: e.tensor_tensor(lo, x, hi.bitcast(F32), ALU.subtract),
                    waits=[*waits, got], flag=flag)


class Stacks:

    def __init__(self, nc, ctx, prog, name, operands, ring):
        self.prog, self.ring = prog, ring
        self.tile = [ctx.enter_context(nc.sbuf_tensor(f"{name}{r}", [P, operands, PER, SEQ], F32R))
                     for r in range(ring)]
        self.landed = [prog.flag(f"{name}_landed{r}") for r in range(ring)]
        self.ready = {}
        self.read = [None] * ring

    def load(self, group, stage, staged):
        slot = group % self.ring
        dst, flag = self.tile[slot], self.landed[slot]
        h = HEAD_DIM
        for j in range(PER):
            rows = slice(h * j, h * j + h)
            for band, first, step in ((0, 0, 2), (1, 1, 1), (2, 0, 3)):
                src = stage[rows, first:first + step + 1:step, :]
                out = dst[h * band:h * band + h, :, j, :].bitcast(F32)
                got = self.prog.put("sync", lambda e, src=src, out=out: e.dma_start(out, src),
                                    waits=[staged, self.read[slot]], flag=flag, by=16)
        self.ready[group] = got
        return got


def softmax_attention(sh, prog, stacks, group, kt, causal, scale, ptile, p_free):
    slot = group % stacks.ring
    first = kt * P if causal else 0
    q0 = min(first, SEQ - 256)
    for j in range(PER):
        b = 2 + sh.st_next
        sh.st_next ^= 1
        bank = sh.bank[b]
        kq = stacks.tile[slot]
        done = prog.put("tensor", lambda e, bank=bank, j=j: e.matmul(
            bank[:, 0:SEQ - q0], kq[0:98, 1, j, kt * P:kt * P + P], kq[0:98, 0, j, q0:SEQ],
            start=True, stop=True),
            waits=[stacks.ready[group], sh.shift_ready[group], sh.bank_read[b]], flag=sh.pe["scores_t"])
        if kt == TILES - 1 and j == PER - 1:
            stacks.read[slot] = done
        got = prog.put("scalar", lambda e, bank=bank, j=j: e.activation(
            ptile[:, j, 0:SEQ - first], bank[:, first - q0:SEQ - q0], ACT.Exp, scale=scale),
            waits=[done, p_free], flag=sh.act["exp"])
        sh.bank_read[b] = got
    if causal:
        got = on_pool(sh, lambda e: e.affine_select(
            out=ptile[:, :, 0:P], in_=ptile[:, :, 0:P], compare_op=ALU.is_ge, fill=0.0, base=0,
            pattern=[[0, PER], [1, P]], channel_multiplier=-1), [got], sh.pool["mask"])
    return got


def weighted_sum(sh, prog, ptile, ready, v, v_ready, kt, causal, out_bank, flag):
    first = kt * P if causal else 0
    for j in range(PER):
        rows = slice(HEAD_DIM * j, HEAD_DIM * j + HEAD_DIM)
        got = prog.put("tensor", lambda e, j=j, rows=rows: e.matmul(
            sh.bank[out_bank][rows, first:SEQ], v(j), ptile[:, j, 0:SEQ - first],
            start=(kt == 0), stop=(kt == TILES - 1), skip_group_check=True),
            waits=[ready, v_ready, sh.bank_read[out_bank] if kt == 0 else None], flag=flag)
    return got


def head_max(sh, prog, stacks, group, j, causal):
    slot, m = group % stacks.ring, sh.negmax[group % 2]
    kq = stacks.tile[slot]
    for qt in range(TILES):
        b = sh.sm_next
        sh.sm_next ^= 1
        bank = sh.bank[b]
        keys = P * (qt + 1) if causal else SEQ
        done = prog.put("tensor", lambda e, bank=bank, qt=qt, keys=keys: e.matmul(
            bank[:, 0:max(keys, 256)], kq[0:96, 0, j, qt * P:qt * P + P], kq[0:96, 1, j, 0:max(keys, 256)],
            start=True, stop=not causal, skip_group_check=True),
            waits=[stacks.ready[group], sh.bank_read[b]], flag=sh.pe["scores"])
        if causal:
            done = prog.put("tensor", lambda e, bank=bank, qt=qt: e.matmul(
                bank[:, qt * P:qt * P + P], sh.identb[:, :], sh.future[:, :],
                start=False, stop=True, skip_group_check=True),
                waits=[sh.const], flag=sh.pe["scores"])
        col = j * TILES + qt
        got = prog.put("vector", lambda e, bank=bank, keys=keys, col=col: e.reduce_max(
            m[:, col:col + 1], bank[:, 0:keys], AX, negate=True),
            waits=[done, sh.negmax_read[group % 2]], flag=sh.dve["max"])
        sh.bank_read[b] = got
    return got


def shift_rows(sh, prog, stacks, group, maxed, bank):
    m, hl, slot = sh.negmax[group % 2], sh.shift[group % 2], group % stacks.ring
    n = PER * TILES
    done = prog.put("tensor", lambda e: e.transpose(sh.bank[bank][0:n, 0:P], m[:, :], sh.ident[:, :]),
                    waits=[maxed, sh.const, sh.bank_read[bank]], flag=sh.pe["small_t"])
    sh.negmax_read[group % 2] = done
    x = sh.bank[bank][0:n, 0:P]
    free = sh.shift_free[group % 2]
    hi = prog.put("scalar", lambda e: e.activation(hl[:, 0, :].bitcast(F32R), x, ACT.Copy),
                  waits=[done, free], flag=sh.act["misc"])
    lo = prog.put("vector", lambda e: e.tensor_tensor(hl[:, 1, :].bitcast(F32R), x, hl[:, 0, :], ALU.subtract),
                  waits=[hi, free], flag=sh.dve["misc"])
    sh.bank_read[bank] = lo
    for part in range(2):
        row = stacks.tile[slot][96 + part:97 + part, 0, :, :].rearrange("p j (t q) -> p (j t) q", q=P)
        got = prog.put("sync", lambda e, row=row, part=part: e.dma_start(row.bitcast(F32), hl[:, part, :]),
                       waits=[hi, lo, stacks.read[slot]], flag=stacks.landed[slot], by=16)
    sh.shift_free[group % 2] = got
    sh.shift_ready[group] = got


def open_softmax(nc, ctx, prog, sh, stacks, name):
    sh.negmax = [ctx.enter_context(nc.sbuf_tensor(f"{name}_negmax{i}", [P, PER * TILES], F32)) for i in range(2)]
    sh.shift = [ctx.enter_context(nc.sbuf_tensor(f"{name}_shift{i}", [PER * TILES, 2, P], F32)) for i in range(2)]
    sh.negmax_read, sh.shift_free, sh.shift_ready = [None] * 2, [None] * 2, {}
    sh.sm_next = sh.st_next = 0
    for r in range(stacks.ring):
        got = on_pool(sh, lambda e, r=r: e.memset(stacks.tile[r][96:128, 1, :, :].bitcast(F32), 1.0),
                      sh.wall, sh.pool["const"])
    return got


def rsqrt(sh, prog, ws, var, n, ready, flag):
    y, a, b = (w[:, 0:n] for w in ws[:3])
    v = ws[3][:, 0:n]
    put = lambda f, waits: prog.put("vector", f, waits=waits, flag=flag)
    g = put(lambda e: e.tensor_scalar(v, var, EPS, None, ALU.add), [ready])
    g = put(lambda e: e.tensor_scalar(a.bitcast(I32), v.bitcast(I32), 1, None, ALU.logical_shift_right), [g])
    g = put(lambda e: e.tensor_scalar(y.bitcast(I32), a.bitcast(I32), -1.0, RSQRT_MAGIC, ALU.mult, ALU.add), [g])
    for _ in range(4):
        g = put(lambda e: e.tensor_tensor(a, y, y, ALU.mult), [g])
        g = put(lambda e: e.tensor_tensor(b, a, v, ALU.mult), [g])
        g = put(lambda e: e.tensor_scalar(a, b, -0.5, 1.5, ALU.mult, ALU.add), [g])
        g = put(lambda e: e.tensor_tensor(y, y, a, ALU.mult), [g])
    return g


class LayerNorm:

    def __init__(self, nc, ctx, sh, prog, name):
        sb = lambda n, s: ctx.enter_context(nc.sbuf_tensor(f"{name}_{n}", s, F32))
        self.sh, self.prog = sh, prog
        self.stats, self.mv = sb("stats", [P, 6]), sb("mv", [P, 2])
        self.ws = [sb(f"ws{i}", [P, 1]) for i in range(4)]
        self.last = None

    def run(self, out, r, ready, out_free):
        put, flag = self.prog.put, self.sh.dve["ln"]
        g = put("vector", lambda e: e.bn_stats(self.stats[:, :], r), waits=[ready, self.last], flag=flag)
        g = put("vector", lambda e: e.bn_aggr(self.mv[:, :], self.stats[:, :]), waits=[g], flag=flag)
        g = rsqrt(self.sh, self.prog, self.ws, self.mv[:, 1:2], 1, g, flag)
        self.last = put("vector", lambda e: e.tensor_scalar(
            out, r, self.mv[:, 0:1], self.ws[0][:, 0:1], ALU.subtract, ALU.mult),
            waits=[g, out_free], flag=flag)
        return self.last


def matmul3(prog, out, pairs, waits, flag, start=True, stop=True):
    passes = [(a[x], b[y]) for a, b in pairs for x, y in ((0, 0), (1, 0), (0, 1))]
    for i, (a, b) in enumerate(passes):
        got = prog.put("tensor", lambda e, a=a, b=b, i=i: e.matmul(
            out, a, b, start=start and i == 0, stop=stop and i == len(passes) - 1),
            waits=waits, flag=flag if i == len(passes) - 1 else None)
    return got


def load_split_weights(prog, sh, raw, raw_flags, jobs):
    free, got = [None] * len(raw), {}
    for i, (key, hi, lo, src) in enumerate(jobs):
        r = i % len(raw)
        n = hi.shape[-1]
        tile = raw[r][:, 0:n]
        landed = prog.put("sync", lambda e, tile=tile, src=src: e.dma_start(tile, src),
                          waits=[free[r], *sh.wall], flag=raw_flags[r], by=16)
        got[key] = split(prog, "vector", hi, lo, tile, [landed, *sh.wall], sh.dve["split"])
        free[r] = got[key]
    return got, free



def self_softmax_phase(nc, ctx, prog, sh, t):
    sb = lambda name, shape, dt=F32: ctx.enter_context(nc.sbuf_tensor(name, shape, dt))
    put = prog.put
    w_hi, w_lo = sb("wqk_hi", [P, GROUPS, 2 * DIM], F32R), sb("wqk_lo", [P, GROUPS, 2 * DIM], F32R)
    bias = sb("bqk", [P, 2 * GROUPS])
    xt_hi = [sb(f"xt_hi{i}", [P, GROUPS, SEQ], F32R) for i in range(2)]
    xt_lo = [sb(f"xt_lo{i}", [P, GROUPS, SEQ], F32R) for i in range(2)]
    raw = [sb(f"raw{i}", [P, SEQ]) for i in range(2)]
    raw_landed = [prog.flag(f"raw_landed{i}") for i in range(2)]
    stage = [sb(f"stage{i}", [P, 4, SEQ]) for i in range(2)]
    qa = [sb(f"qa_out{i}", [P, SEQ]) for i in range(2)]
    stacks = Stacks(nc, ctx, prog, "qk", 2, 3)
    pt = [sb(f"pt{i}", [P, PER, SEQ]) for i in range(2)]
    v = [sb(f"v{i}", [P, TILES, P]) for i in range(2)]
    v_landed = [prog.flag(f"v_landed{i}") for i in range(2)]
    recip = sb("recip", [P, SEQ])
    y_ar = [sb(f"y_ar{i}", [P, SEQ]) for i in range(2)]
    y_stored = [prog.flag(f"y_stored{i}") for i in range(2)]
    qa_stored = [prog.flag(f"qa_stored{i}") for i in range(2)]
    bias_landed = prog.flag("bqk_landed")
    ones_ready = open_softmax(nc, ctx, prog, sh, stacks, "self")
    Y, L, DENSE = 4, 5, (6, 7)
    dense_next = [0]

    def dense_bank():
        dense_next[0] ^= 1
        return DENSE[dense_next[0]]

    bias_ready = put("sync", lambda e: e.dma_start(bias[:, :], t["b_attn"]), flag=bias_landed, by=16)
    jobs = [((half, c), w_hi[:, c, half * DIM:(half + 1) * DIM], w_lo[:, c, half * DIM:(half + 1) * DIM],
             t["w_attn_t"][c * P:c * P + P, half * DIM:(half + 1) * DIM]) for half in range(2) for c in range(GROUPS)]
    w_ready, raw_free = load_split_weights(prog, sh, raw, raw_landed, jobs)
    w_all = w_ready[(1, GROUPS - 1)]

    xt_ready, xt_free = {}, [None, None]

    def load_xt(b, c):
        r = c % 2
        landed = put("sync", lambda e: e.dma_start(raw[r][:, :], t["x_t"][b, c * P:c * P + P, :]),
                     waits=[raw_free[r]], flag=raw_landed[r], by=16)
        xt_ready[b] = split(prog, "vector", xt_hi[b % 2][:, c, :], xt_lo[b % 2][:, c, :], raw[r][:, :],
                            [landed, xt_free[b % 2]], sh.dve["split"])
        raw_free[r] = xt_ready[b]

    qa_free = [None, None]

    def project(g, which):
        b, h = divmod(g, GROUPS)
        bank, st = dense_bank(), stage[g % 2]
        col = which * DIM + h * P
        pairs = [((w_hi[:, c, col:col + P], w_lo[:, c, col:col + P]),
                  (xt_hi[b % 2][:, c, :], xt_lo[b % 2][:, c, :])) for c in range(GROUPS)]
        done = matmul3(prog, sh.bank[bank][:, :], pairs, [w_all, xt_ready[b], sh.bank_read[bank]], sh.pe["dense"])
        if which == 1 and h == GROUPS - 1:
            xt_free[b % 2] = done
        hi, lo = st[:, 2 * which, :], st[:, 2 * which + 1, :]
        x = put("scalar", lambda e: e.activation(lo, sh.bank[bank][:, :], ACT.Identity,
                                                 bias=bias[:, which * GROUPS + h:which * GROUPS + h + 1]),
                waits=[done, bias_ready, stage_free[g % 2]], flag=sh.act["evac"])
        sh.bank_read[bank] = x
        if which == 0:
            out = qa[g % 2]
            got = put("vector", lambda e: e.scalar_tensor_tensor(
                out=out[:, :], in0=lo, scalar=LEAK, in1=lo, op0=ALU.mult, op1=ALU.min),
                waits=[x, qa_free[g % 2]], flag=sh.dve["misc"])
            qa_free[g % 2] = put("sync", lambda e: e.dma_start(t["qa"][b, h * P:h * P + P, :], out[:, :]),
                                 waits=[got], flag=qa_stored[g % 2], by=16)
            x = got
        staged = split(prog, "vector", hi.bitcast(F32R), lo.bitcast(F32R), lo, [x], sh.dve["split"])
        if which == 1:
            stage_free[g % 2] = stacks.load(g, st, staged)

    stage_free = [None, None]
    v_ready, v_free = {}, [None, None]

    def load_v(g):
        b, h = divmod(g, GROUPS)
        src = t["x"][b].rearrange("(k p) d -> p k d", p=P)[:, :, h * P:h * P + P]
        v_ready[g] = put("sync", lambda e: e.dma_start(v[g % 2][:, :, :], src), waits=[v_free[g % 2]],
                         flag=v_landed[g % 2], by=16)

    p_free, p_ready = [None, None], {}
    y_free = [None, None]

    def sums(g, kt):
        u = (g * TILES + kt) % 2
        got = weighted_sum(sh, prog, pt[u], p_ready[(g, kt)],
                           lambda j: v[g % 2][:, kt, HEAD_DIM * j:HEAD_DIM * j + HEAD_DIM],
                           v_ready[g], kt, True, Y, sh.pe["pv"])
        got = weighted_sum(sh, prog, pt[u], p_ready[(g, kt)], lambda j: sh.ones[:, :], sh.const, kt, True, L,
                           sh.pe["pv"])
        p_free[u] = got
        if kt < TILES - 1:
            return
        v_free[g % 2] = got
        b, h = divmod(g, GROUPS)
        r = put("vector", lambda e: e.reciprocal(recip[:, :], sh.bank[L][:, :]), waits=[got], flag=sh.dve["norm"])
        sh.bank_read[L] = r
        n = put("vector", lambda e: e.tensor_tensor(y_ar[g % 2][:, :], sh.bank[Y][:, :], recip[:, :], ALU.mult),
                waits=[r, y_free[g % 2]], flag=sh.dve["norm"])
        sh.bank_read[Y] = n
        y_free[g % 2] = put("sync", lambda e: e.dma_start(t["y_ar"][b, h * P:h * P + P, :], y_ar[g % 2][:, :]),
                            waits=[n], flag=y_stored[g % 2], by=16)

    def maxima(g, j):
        maxed = head_max(sh, prog, stacks, g, j, True)
        if j == PER - 1:
            shift_rows(sh, prog, stacks, g, maxed, dense_bank())

    for c in range(GROUPS):
        load_xt(0, c)
    put("tensor", lambda e: e.nop(), waits=[ones_ready])
    for g in range(2):
        project(g, 0)
        project(g, 1)
        load_v(g)
    for j in range(PER):
        maxima(0, j)
    last = None
    for g in range(NG):
        for kt in range(TILES):
            u = (g * TILES + kt) % 2
            p_ready[(g, kt)] = softmax_attention(sh, prog, stacks, g, kt, True, SCALE_SELF, pt[u], p_free[u])
            if kt < 2 and g + 2 < NG:
                project(g + 2, kt)
            last, prev = (g, kt), last
            if prev is not None:
                sums(*prev)
            if kt == 1 and 1 <= g and g + 1 < NG:
                load_v(g + 1)
            if g + 1 < NG:
                maxima(g + 1, kt)
            nb = g // GROUPS + 1
            if nb < BATCH and kt >= 2 and g % GROUPS < 2:
                load_xt(nb, (g % GROUPS) * 2 + kt - 2)
    sums(*last)
    tail = [f for f in (y_free + qa_free)]
    sh.wall = [(f, f.count) for f in (*sh.pe.values(), *sh.dve.values(), *sh.act.values(), *sh.pool.values(),
                                      *stacks.landed, *raw_landed, *v_landed) if f.count] + tail



def self_memory_phase(nc, ctx, prog, sh, t):
    sb = lambda name, shape, dt=F32: ctx.enter_context(nc.sbuf_tensor(name, shape, dt))
    put = prog.put
    w_hi, w_lo = sb("wk2_hi", [P, GROUPS, DIM], F32R), sb("wk2_lo", [P, GROUPS, DIM], F32R)
    wp = sb("wproj", [P, GROUPS, DIM])
    b2, b2c, bproj = sb("bk2", [P, GROUPS]), sb("bk2_scaled", [P, GROUPS]), sb("bproj", [P, DIM])
    xt_hi = [sb(f"mxt_hi{i}", [P, GROUPS, SEQ], F32R) for i in range(2)]
    xt_lo = [sb(f"mxt_lo{i}", [P, GROUPS, SEQ], F32R) for i in range(2)]
    raw = [sb(f"mraw{i}", [P, SEQ]) for i in range(2)]
    raw_landed = [prog.flag(f"mraw_landed{i}") for i in range(2)]
    stage = sb("mstage", [P, 4, SEQ])
    stacks = Stacks(nc, ctx, prog, "ma", 2, 2)
    mt = [sb(f"mt{i}", [P, PER, SEQ]) for i in range(2)]
    y_ar = [sb(f"my_ar{i}", [P, SEQ]) for i in range(3)]
    xs = [sb(f"x_next{i}", [P, TILES, P]) for i in range(2)]
    ev = [sb(f"e{i}", [P, TILES, P]) for i in range(2)]
    y = [sb(f"y{i}", [P, GROUPS, SEQ]) for i in range(2)]
    xr = [sb(f"mxr{i}", [P, DIM]) for i in range(2)]
    x1 = [sb(f"mx1_{i}", [P, DIM]) for i in range(2)]
    ln = LayerNorm(nc, ctx, sh, prog, "ln1")
    small = prog.flag("m_small_landed")
    qa_landed = prog.flag("m_qa_landed")
    y_landed = [prog.flag(f"m_y_landed{i}") for i in range(3)]
    xs_landed = [prog.flag(f"m_xs_landed{i}") for i in range(2)]
    xr_landed = [prog.flag(f"m_xr_landed{i}") for i in range(2)]
    x1_stored = [prog.flag(f"x1_stored{i}") for i in range(2)]
    Y2, DENSE = 4, (5, 6, 7)
    dense_next = [0]

    def dense_bank():
        dense_next[0] = (dense_next[0] + 1) % len(DENSE)
        return DENSE[dense_next[0]]

    wall = sh.wall
    put("sync", lambda e: e.dma_start(b2[:, :], t["b_k2"]), waits=wall, flag=small, by=16)
    put("sync", lambda e: e.dma_start(bproj[:, :], t["b_proj"].partition_broadcast(P)), flag=small, by=16)
    small_ready = put("sync", lambda e: e.dma_start(
        wp[:, :, :], t["w_proj_t"].rearrange("(c p) n -> p c n", p=P)), flag=small, by=16)
    kscale = 0.5 * LEAK * SCALE_SELF
    b2_ready = put("vector", lambda e: e.tensor_scalar(b2c[:, :], b2[:, :], kscale, None, ALU.mult),
                   waits=[small_ready], flag=sh.dve["misc"])
    for i in range(2):
        xs_zero = on_pool(sh, lambda e, i=i: e.memset(xs[i][:, :, :], 0.0), wall, sh.pool["const"])
    jobs = [(c, w_hi[:, c, :], w_lo[:, c, :], t["w_k2_t"][c * P:c * P + P, :]) for c in range(GROUPS)]
    w_ready, raw_free = load_split_weights(prog, sh, raw, raw_landed, jobs)
    w_all = w_ready[GROUPS - 1]
    xt_ready, xt_free = {}, [None, None]

    def load_xt(b, c):
        r = c % 2
        landed = put("sync", lambda e: e.dma_start(raw[r][:, :], t["x_t"][b, c * P:c * P + P, :]),
                     waits=[raw_free[r]], flag=raw_landed[r], by=16)
        xt_ready[b] = split(prog, "vector", xt_hi[b % 2][:, c, :], xt_lo[b % 2][:, c, :], raw[r][:, :],
                            [landed, xt_free[b % 2], *wall], sh.dve["split"])
        raw_free[r] = xt_ready[b]

    stage_free = [None]

    def project(g):
        b, h = divmod(g, GROUPS)
        bank = dense_bank()
        pairs = [((w_hi[:, c, h * P:h * P + P], w_lo[:, c, h * P:h * P + P]),
                  (xt_hi[b % 2][:, c, :], xt_lo[b % 2][:, c, :])) for c in range(GROUPS)]
        done = matmul3(prog, sh.bank[bank][:, :], pairs, [w_all, xt_ready[b], sh.bank_read[bank]], sh.pe["dense"])
        if h == GROUPS - 1:
            xt_free[b % 2] = done
        q_hi, q_lo, k_hi, k_lo = (stage[:, i, :] for i in range(4))
        landed = put("sync", lambda e: e.dma_start(q_lo, t["qa"][b, h * P:h * P + P, :]),
                     waits=[stage_free[0], *wall], flag=qa_landed, by=16)
        th = put("scalar", lambda e: e.activation(k_lo, sh.bank[bank][:, :], ACT.Tanh,
                                                  bias=b2c[:, h:h + 1], scale=kscale),
                 waits=[done, b2_ready, stage_free[0], *wall], flag=sh.act["evac"])
        sh.bank_read[bank] = th
        hi = put("vector", lambda e: e.tensor_scalar(k_hi.bitcast(F32R), k_lo, 1.0, None, ALU.add),
                 waits=[th], flag=sh.dve["split"])
        put("vector", lambda e: e.scalar_tensor_tensor(out=k_lo.bitcast(F32R), in0=k_lo, scalar=1.0, in1=k_hi,
                                                       op0=ALU.add, op1=ALU.subtract),
            waits=[hi], flag=sh.dve["split"])
        staged = split(prog, "vector", q_hi.bitcast(F32R), q_lo.bitcast(F32R), q_lo, [landed], sh.dve["split"])
        stage_free[0] = stacks.load(g, stage, staged)

    y_ready, y_free, xs_ready, xs_free = {}, [None] * 3, {}, [None] * 2

    def load_y(g):
        b, h = divmod(g, GROUPS)
        ry = g % 3
        y_ready[g] = put("sync", lambda e: e.dma_start(y_ar[ry][:, :], t["y_ar"][b, h * P:h * P + P, :]),
                         waits=[y_free[ry], *wall], flag=y_landed[ry], by=16)
        r = g % 2
        cols = slice(h * P, h * P + P)
        body = t["x"][b, 1:1 + (TILES - 1) * P, cols].rearrange("(k p) d -> p k d", p=P)
        put("sync", lambda e: e.dma_start(xs[r][:, 0:TILES - 1, :], body),
            waits=[xs_free[r], xs_zero], flag=xs_landed[r], by=16)
        rest = t["x"][b, 1 + (TILES - 1) * P:SEQ, cols]
        xs_ready[g] = put("sync", lambda e: e.dma_start(xs[r][0:P - 1, TILES - 1, :], rest),
                          waits=[xs_free[r]], flag=xs_landed[r], by=16)

    e_ready, e_free = {}, [None] * 2

    def values(g):
        bank = dense_bank()
        for k in range(TILES):
            done = put("tensor", lambda e, k=k: e.transpose(
                sh.bank[bank][:, k * P:k * P + P], y_ar[g % 3][:, k * P:k * P + P], sh.ident[:, :]),
                waits=[y_ready[g], sh.bank_read[bank]], flag=sh.pe["small_t"])
        e_ready[g] = put("vector", lambda e: e.tensor_tensor(
            ev[g % 2][:, :, :].rearrange("p k d -> p (k d)"), xs[g % 2][:, :, :].rearrange("p k d -> p (k d)"),
            sh.bank[bank][:, :], ALU.subtract),
            waits=[done, xs_ready[g], e_free[g % 2], *wall], flag=sh.dve["misc"])
        sh.bank_read[bank] = xs_free[g % 2] = e_ready[g]

    m_ready, m_free = {}, [None] * 2
    st_next = [0]

    def memory_scores(g, kt):
        u, slot, first = (g * TILES + kt) % 2, g % stacks.ring, kt * P
        q0 = min(first, SEQ - 256)
        kq = stacks.tile[slot]
        for j in range(PER):
            b = st_next[0]
            st_next[0] = (b + 1) % 4
            done = put("tensor", lambda e, b=b, j=j: e.matmul(
                sh.bank[b][:, 0:SEQ - q0], kq[0:96, 1, j, first:first + P], kq[0:96, 0, j, q0:SEQ],
                start=True, stop=True),
                waits=[stacks.ready[g], sh.bank_read[b]], flag=sh.pe["scores_t"])
            got = put("scalar", lambda e, b=b, j=j: e.activation(
                mt[u][:, j, 0:SEQ - first], sh.bank[b][:, first - q0:SEQ - q0], ACT.Copy, scale=0.5 * SCALE_SELF),
                waits=[done, m_free[u], *wall], flag=sh.act["exp"])
            sh.bank_read[b] = got
        if kt == TILES - 1:
            stacks.read[slot] = done
        m_ready[(g, kt)] = on_pool(sh, lambda e: e.affine_select(
            out=mt[u][:, :, 0:P], in_=mt[u][:, :, 0:P], compare_op=ALU.is_ge, fill=0.0, base=-1,
            pattern=[[0, PER], [1, P]], channel_multiplier=-1), [got], sh.pool["mask"])

    ysum_ready, ysum_free = {}, [None] * 2

    def memory_sums(g, kt):
        b, h = divmod(g, GROUPS)
        u = (g * TILES + kt) % 2
        got = weighted_sum(sh, prog, mt[u], m_ready[(g, kt)],
                           lambda j: ev[g % 2][:, kt, HEAD_DIM * j:HEAD_DIM * j + HEAD_DIM],
                           e_ready[g], kt, True, Y2, sh.pe["pv"])
        m_free[u] = got
        if kt < TILES - 1:
            return
        e_free[g % 2] = got
        n = put("vector", lambda e: e.tensor_tensor(y[b % 2][:, h, :], sh.bank[Y2][:, :], y_ar[g % 3][:, :], ALU.add),
                waits=[got, y_ready[g], ysum_free[b % 2], *wall], flag=sh.dve["norm"])
        sh.bank_read[Y2] = y_free[g % 3] = ysum_ready[b] = n

    xr_free, x1_free = [None] * 2, [None] * 2

    def project_out(b, k):
        bank, r = dense_bank(), k % 2
        landed = put("sync", lambda e: e.dma_start(xr[r][:, :], t["x"][b, k * P:k * P + P, :]),
                     waits=[xr_free[r], *wall], flag=xr_landed[r], by=16)
        for c in range(GROUPS):
            done = put("tensor", lambda e, c=c: e.matmul(
                sh.bank[bank][:, :], y[b % 2][:, c, k * P:k * P + P], wp[:, c, :],
                start=(c == 0), stop=(c == GROUPS - 1)),
                waits=[ysum_ready[b], small_ready, sh.bank_read[bank]], flag=sh.pe["dense"])
        if k == TILES - 1:
            ysum_free[b % 2] = done
        got = put("vector", lambda e: e.scalar_tensor_tensor(
            out=xr[r][:, :], in0=bproj[:, :], scalar=2.0, in1=xr[r][:, :], op0=ALU.mult, op1=ALU.add),
            waits=[landed, small_ready], flag=sh.dve["misc"])
        got = put("vector", lambda e: e.tensor_tensor(xr[r][:, :], sh.bank[bank][:, :], xr[r][:, :], ALU.add),
                  waits=[done, got], flag=sh.dve["misc"])
        sh.bank_read[bank] = got
        got = ln.run(x1[r][:, :], xr[r][:, :], got, x1_free[r])
        xr_free[r] = got
        x1_free[r] = put("sync", lambda e: e.dma_start(t["x1"][b, k * P:k * P + P, :], x1[r][:, :]),
                         waits=[got], flag=x1_stored[r], by=16)

    for c in range(GROUPS):
        load_xt(0, c)
    load_y(0)
    project(0)
    values(0)
    last = None
    for g in range(NG):
        b, h = divmod(g, GROUPS)
        for kt in range(TILES):
            memory_scores(g, kt)
            if kt == 0 and g + 1 < NG:
                load_y(g + 1)
                project(g + 1)
            if kt == 2 and g + 1 < NG:
                values(g + 1)
            last, prev = (g, kt), last
            if prev is not None:
                memory_sums(*prev)
            if kt == 1 and b > 0:
                project_out(b - 1, h)
            if b + 1 < BATCH and kt >= 2 and h < 2:
                load_xt(b + 1, 2 * h + kt - 2)
    memory_sums(*last)
    for k in range(TILES):
        project_out(BATCH - 1, k)
    sh.wall = [(f, f.count) for f in (*sh.pe.values(), *sh.dve.values(), *sh.act.values(), *sh.pool.values(),
                                      *stacks.landed, *raw_landed, *y_landed, *xs_landed, *xr_landed, *x1_stored,
                                      qa_landed, small) if f.count]



def cross_phase(nc, ctx, prog, sh, t):
    sb = lambda name, shape, dt=F32: ctx.enter_context(nc.sbuf_tensor(name, shape, dt))
    put = prog.put
    wall = sh.wall
    wo = sb("wo", [P, GROUPS, DIM])
    fold = sb("fold", [P, 3, P])
    a_hi, a_lo = sb("a_hi", [P, P], F32R), sb("a_lo", [P, P], F32R)
    e_hi = sb("exp_hi", [P, 2, GROUPS, DIM], F32R)
    e_lo = sb("exp_lo", [P, 2, GROUPS, DIM], F32R)
    gate_hi, gate_lo = sb("gate_hi", [P, GROUPS, EXPERTS], F32R), sb("gate_lo", [P, GROUPS, EXPERTS], F32R)
    gate_raw = sb("gate_raw", [P, GROUPS, EXPERTS])
    bo = sb("bo", [P, DIM])
    be = sb("bias_exp", [P, 2, DIM])
    raw = [sb(f"craw{i}", [P, SEQ]) for i in range(2)]
    raw_landed = [prog.flag(f"craw_landed{i}") for i in range(2)]
    stacks = Stacks(nc, ctx, prog, "cqk", 2, 2)
    stage = sb("cstage", [P, 4, SEQ])
    pt = [sb(f"cpt{i}", [P, PER, SEQ]) for i in range(2)]
    v = [sb(f"cv{i}", [P, TILES, P]) for i in range(2)]
    v_landed = [prog.flag(f"cv_landed{i}") for i in range(2)]
    recip = sb("crecip", [P, SEQ])
    y = sb("cy", [P, GROUPS, SEQ])
    x1 = [sb(f"cx1_{i}", [P, TILES, DIM]) for i in range(2)]
    x1_landed = [prog.flag(f"cx1_landed{i}") for i in range(2)]
    x1t = sb("x1t", [P, 2, SEQ], F32R)
    x2 = sb("x2", [P, TILES, DIM])
    x2t_hi, x2t_lo = sb("x2t_hi", [P, GROUPS, SEQ], F32R), sb("x2t_lo", [P, GROUPS, SEQ], F32R)
    tanh = sb("tanh", [P, DIM])
    lt = sb("logits_t", [EXPERTS, SEQ])
    lg = sb("logits", [P, TILES, EXPERTS])
    gs = {n: sb(f"gate_{n}", [P, TILES]) for n in ("max", "sum", "rest", "keep0", "keep1", "w0", "w1")}
    ge = sb("gate_exp", [P, TILES, EXPERTS])
    gb = sb("gate_beats", [P, TILES, EXPERTS])
    ln2 = LayerNorm(nc, ctx, sh, prog, "ln2")
    ln3 = LayerNorm(nc, ctx, sh, prog, "ln3")
    out_stored = prog.flag("out_stored")
    small = prog.flag("c_small_landed")
    k_landed = prog.flag("c_keys_landed")
    ones_ready = open_softmax(nc, ctx, prog, sh, stacks, "cross")
    Y, L, DENSE = 4, 5, (6, 7)
    dense_next = [0]

    def dense_bank():
        dense_next[0] ^= 1
        return DENSE[dense_next[0]]

    zero = on_pool(sh, lambda e: e.memset(fold[:, :, :], 0.0), wall, sh.pool["const"])
    for i, name in enumerate(("wq", "wk", "wv")):
        for j in range(PER):
            d = slice(HEAD_DIM * j, HEAD_DIM * j + HEAD_DIM)
            put("sync", lambda e, i=i, d=d, name=name: e.dma_start(fold[d, i, d], t[name]),
                waits=[zero, *wall], flag=small, by=16)
    put("sync", lambda e: e.dma_start(bo[:, :], t["bo"].partition_broadcast(P)), flag=small, by=16)
    put("sync", lambda e: e.dma_start(be[:, 0, :], t["b0"].partition_broadcast(P)), flag=small, by=16)
    put("sync", lambda e: e.dma_start(be[:, 1, :], t["b1"].partition_broadcast(P)), flag=small, by=16)
    small_ready = put("sync", lambda e: e.dma_start(
        gate_raw[:, :, :], t["gate_w"].rearrange("(c p) n -> p c n", p=P)), flag=small, by=16)
    bank = dense_bank()
    done = put("tensor", lambda e, bank=bank: e.matmul(sh.bank[bank][:, 0:P], fold[:, 0, :], fold[:, 1, :],
                                                       start=True, stop=True),
               waits=[small_ready, *wall], flag=sh.pe["dense"])
    a_ready = split(prog, "vector", a_hi[:, :], a_lo[:, :], sh.bank[bank][:, 0:P], [done, *wall], sh.dve["split"])
    sh.bank_read[bank] = a_ready
    raw_free = [None, None]
    for c in range(GROUPS):
        bank, r = dense_bank(), c % 2
        landed = put("sync", lambda e, r=r, c=c: e.dma_start(raw[r][:, :], t["wo_t"][c * P:c * P + P, :]),
                     waits=[raw_free[r], *wall], flag=raw_landed[r], by=16)
        done = put("tensor", lambda e, bank=bank, r=r: e.matmul(sh.bank[bank][:, :], fold[:, 2, :], raw[r][:, :],
                                                                start=True, stop=True),
                   waits=[small_ready, landed, sh.bank_read[bank]], flag=sh.pe["dense"])
        raw_free[r] = done
        wo_ready = put("vector", lambda e, bank=bank, c=c: e.tensor_copy(wo[:, c, :], sh.bank[bank][:, :]),
                       waits=[done], flag=sh.dve["misc"])
        sh.bank_read[bank] = wo_ready
    gate_ready = split(prog, "vector", gate_hi[:, :, :], gate_lo[:, :, :], gate_raw[:, :, :], [small_ready],
                       sh.dve["split"])

    def load_expert(i, c):
        r = c % 2
        landed = put("sync", lambda e: e.dma_start(raw[r][:, :], t[f"w{i}_t"][c * P:c * P + P, :]),
                     waits=[raw_free[r], *wall], flag=raw_landed[r], by=16)
        raw_free[r] = split(prog, "vector", e_hi[:, i, c, :], e_lo[:, i, c, :], raw[r][:, :], [landed],
                            sh.dve["split"])
        return raw_free[r]

    x1_ready, x1_free = {}, [None, None]

    def load_x1(b):
        x1_ready[b] = put("sync", lambda e: e.dma_start(
            x1[b % 2][:, :, :], t["x1"][b].rearrange("(k p) d -> p k d", p=P)),
            waits=[x1_free[b % 2], *wall], flag=x1_landed[b % 2], by=16)

    stage_free, x1t_free = [None], [None]
    v_ready, v_free = {}, [None, None]

    def keys(g):
        b, h = divmod(g, GROUPS)
        k_hi, k_lo = stage[:, 2, :], stage[:, 3, :]
        landed = put("sync", lambda e: e.dma_start(k_lo, t["ctx_t"][b, h * P:h * P + P, :]),
                     waits=[stage_free[0], *wall], flag=k_landed, by=16)
        split(prog, "vector", k_hi.bitcast(F32R), k_lo.bitcast(F32R), k_lo, [landed], sh.dve["split"])
        src = t["ctx"][b].rearrange("(k p) d -> p k d", p=P)[:, :, h * P:h * P + P]
        v_ready[g] = put("sync", lambda e: e.dma_start(v[g % 2][:, :, :], src), waits=[v_free[g % 2], *wall],
                         flag=v_landed[g % 2], by=16)

    def queries(g):
        b, h = divmod(g, GROUPS)
        bank = dense_bank()
        for k in range(TILES):
            done = put("tensor", lambda e, k=k: e.transpose(
                sh.bank[bank][:, k * P:k * P + P], x1[b % 2][:, k, h * P:h * P + P], sh.ident[:, :]),
                waits=[x1_ready[b], sh.bank_read[bank]], flag=sh.pe["small_t"])
        got = put("scalar", lambda e: e.activation(x1t[:, 0, :], sh.bank[bank][:, :], ACT.Copy),
                  waits=[done, x1t_free[0], *wall], flag=sh.act["evac"])
        got = put("vector", lambda e: e.tensor_tensor(x1t[:, 1, :], sh.bank[bank][:, :],
                                                      x1t[:, 0, :].bitcast(F32), ALU.subtract),
                  waits=[got, x1t_free[0]], flag=sh.dve["split"])
        sh.bank_read[bank] = got
        bank2 = dense_bank()
        done = matmul3(prog, sh.bank[bank2][:, :], [((a_hi[:, :], a_lo[:, :]), (x1t[:, 0, :], x1t[:, 1, :]))],
                       [a_ready, got, sh.bank_read[bank2]], sh.pe["dense"])
        x1t_free[0] = done
        q_hi, q_lo = stage[:, 0, :], stage[:, 1, :]
        hi = put("scalar", lambda e: e.activation(q_hi.bitcast(F32R), sh.bank[bank2][:, :], ACT.Copy),
                 waits=[done, stage_free[0]], flag=sh.act["evac"])
        staged = put("vector", lambda e: e.tensor_tensor(q_lo.bitcast(F32R), sh.bank[bank2][:, :], q_hi, ALU.subtract),
                     waits=[hi, stage_free[0]], flag=sh.dve["split"])
        sh.bank_read[bank2] = staged
        stage_free[0] = stacks.load(g, stage, staged)

    p_free, p_ready = [None, None], {}
    y_ready, y_free = {}, [None]

    def sums(g, kt):
        u = (g * TILES + kt) % 2
        got = weighted_sum(sh, prog, pt[u], p_ready[(g, kt)],
                           lambda j: v[g % 2][:, kt, HEAD_DIM * j:HEAD_DIM * j + HEAD_DIM],
                           v_ready[g], kt, False, Y, sh.pe["pv"])
        got = weighted_sum(sh, prog, pt[u], p_ready[(g, kt)], lambda j: sh.ones[:, :], sh.const, kt, False, L,
                           sh.pe["pv"])
        p_free[u] = got
        if kt < TILES - 1:
            return
        v_free[g % 2] = got
        b, h = divmod(g, GROUPS)
        r = put("vector", lambda e: e.reciprocal(recip[:, :], sh.bank[L][:, :]), waits=[got], flag=sh.dve["norm"])
        sh.bank_read[L] = r
        y_ready[b] = put("vector", lambda e: e.tensor_tensor(y[:, h, :], sh.bank[Y][:, :], recip[:, :], ALU.mult),
                         waits=[r, y_free[0]], flag=sh.dve["norm"])
        sh.bank_read[Y] = y_ready[b]

    def maxima(g, j):
        maxed = head_max(sh, prog, stacks, g, j, False)
        if j == PER - 1:
            shift_rows(sh, prog, stacks, g, maxed, dense_bank())

    x2_ready, x2_free, x2t_ready, x2t_free = {}, [None], {}, [None]

    def project_out(b, k):
        bank = dense_bank()
        for c in range(GROUPS):
            done = put("tensor", lambda e, c=c: e.matmul(
                sh.bank[bank][:, :], y[:, c, k * P:k * P + P], wo[:, c, :],
                start=(c == 0), stop=(c == GROUPS - 1)),
                waits=[y_ready[b], wo_ready, sh.bank_read[bank]], flag=sh.pe["dense"])
        if k == TILES - 1:
            y_free[0] = done
        x = x1[b % 2][:, k, :]
        got = put("vector", lambda e: e.tensor_tensor(x, x, bo[:, :], ALU.add), waits=[small_ready],
                  flag=sh.dve["misc"])
        got = put("vector", lambda e: e.tensor_tensor(x, sh.bank[bank][:, :], x, ALU.add),
                  waits=[done, got], flag=sh.dve["misc"])
        sh.bank_read[bank] = got
        x2_ready[(b, k)] = ln2.run(x2[:, k, :], x, got, x2_free[0])
        if k == TILES - 1:
            x1_free[b % 2] = x2_ready[(b, k)]

    def transpose_x2(b, c):
        bank = dense_bank()
        for k in range(TILES):
            done = put("tensor", lambda e, k=k: e.transpose(
                sh.bank[bank][:, k * P:k * P + P], x2[:, k, c * P:c * P + P], sh.ident[:, :]),
                waits=[x2_ready[(b, TILES - 1)], sh.bank_read[bank]], flag=sh.pe["small_t"])
        hi = put("scalar", lambda e: e.activation(x2t_hi[:, c, :], sh.bank[bank][:, :], ACT.Copy),
                 waits=[done, x2t_free[0], *wall], flag=sh.act["evac"])
        x2t_ready[b] = put("vector", lambda e: e.tensor_tensor(
            x2t_lo[:, c, :], sh.bank[bank][:, :], x2t_hi[:, c, :].bitcast(F32), ALU.subtract),
            waits=[hi, x2t_free[0]], flag=sh.dve["split"])
        sh.bank_read[bank] = x2t_ready[b]

    gates_ready = {}
    gate_last = [None]

    def gates(b):
        bank = dense_bank()
        pairs = [((gate_hi[:, c, :], gate_lo[:, c, :]), (x2t_hi[:, c, :], x2t_lo[:, c, :])) for c in range(GROUPS)]
        done = matmul3(prog, sh.bank[bank][0:EXPERTS, :], pairs, [gate_ready, x2t_ready[b], sh.bank_read[bank]],
                       sh.pe["dense"])
        got = put("scalar", lambda e: e.activation(lt[:, :], sh.bank[bank][0:EXPERTS, :], ACT.Copy),
                  waits=[done, gate_last[0], *wall], flag=sh.act["evac"])
        sh.bank_read[bank] = got
        bank2 = dense_bank()
        for k in range(TILES):
            done = put("tensor", lambda e, k=k: e.transpose(
                sh.bank[bank2][:, k * EXPERTS:(k + 1) * EXPERTS], lt[:, k * P:k * P + P],
                sh.ident[0:EXPERTS, 0:EXPERTS]),
                waits=[got, sh.bank_read[bank2]], flag=sh.pe["small_t"])
        dv = lambda f, *w: put("vector", f, waits=w, flag=sh.dve["ffn"])
        g = dv(lambda e: e.tensor_copy(lg[:, :, :].rearrange("p k x -> p (k x)"),
                                       sh.bank[bank2][:, 0:TILES * EXPERTS]), done, ffn_last[0])
        sh.bank_read[bank2] = g
        col = lambda n: gs[n][:, :]
        wide = lambda ap, n=EXPERTS: ap.unsqueeze(2).to_broadcast([P, TILES, n])
        g = dv(lambda e: e.reduce_max(col("max"), lg[:, :, :], AX), g)
        g = dv(lambda e: e.tensor_tensor(ge[:, :, :], lg[:, :, :], wide(col("max")), ALU.subtract), g)
        x = put("scalar", lambda e: e.activation(ge[:, :, :], ge[:, :, :], ACT.Exp), waits=[g], flag=sh.act["misc"])
        g = dv(lambda e: e.reduce_sum(col("rest"), ge[:, :, :], AX), x)
        g = dv(lambda e: e.reciprocal(col("sum"), col("rest")), g)
        g = dv(lambda e: e.reduce_max(col("rest"), lg[:, :, 1:EXPERTS], AX), g)
        g = dv(lambda e: e.tensor_tensor(col("keep0"), lg[:, :, 0], col("rest"), ALU.is_ge), g)
        g = dv(lambda e: e.tensor_tensor(gb[:, :, :], lg[:, :, :], wide(lg[:, :, 1]), ALU.is_gt), g)
        g = dv(lambda e: e.tensor_tensor(gb[:, :, 0], lg[:, :, 0], lg[:, :, 1], ALU.is_ge), g)
        g = dv(lambda e: e.reduce_sum(col("rest"), gb[:, :, :], AX), g)
        g = dv(lambda e: e.tensor_scalar(col("keep1"), col("rest"), 1.0, 0.5, ALU.is_equal, ALU.mult), g)
        g = dv(lambda e: e.tensor_scalar(col("keep0"), col("keep0"), 0.5, None, ALU.mult), g)
        for i in (0, 1):
            g = dv(lambda e, i=i: e.tensor_tensor(col(f"w{i}"), ge[:, :, i], col("sum"), ALU.mult), g)
            g = dv(lambda e, i=i: e.tensor_tensor(col(f"w{i}"), col(f"w{i}"), col(f"keep{i}"), ALU.mult), g)
        gates_ready[b] = gate_last[0] = g

    ffn_last = [None]
    ffn_bank = [None]
    tanh_free = [None]

    def expert(b, k, i):
        bank = dense_bank()
        pairs = [((x2t_hi[:, c, k * P:k * P + P], x2t_lo[:, c, k * P:k * P + P]),
                  (e_hi[:, i, c, :], e_lo[:, i, c, :])) for c in range(GROUPS)]
        done = matmul3(prog, sh.bank[bank][:, :], pairs, [exp_ready, x2t_ready[b], sh.bank_read[bank]], sh.pe["dense"])
        if k == TILES - 1 and i == 1:
            x2t_free[0] = done
        z = zt[:, :]
        dv = lambda f, *w: put("vector", f, waits=w, flag=sh.dve["ffn"])
        g = dv(lambda e: e.tensor_tensor(z, sh.bank[bank][:, :], be[:, i, :], ALU.add), done, small_ready, tanh_free[0])
        sh.bank_read[bank] = g
        a = put("scalar", lambda e: e.activation(tanh[:, :], z, ACT.Tanh, scale=0.5), waits=[g, tanh_free[0]],
                flag=sh.act["evac"])
        g = dv(lambda e: e.scalar_tensor_tensor(out=tanh[:, :], in0=tanh[:, :], scalar=1.0, in1=z,
                                                op0=ALU.add, op1=ALU.mult), a)
        w = gs[f"w{i}"][:, k:k + 1]
        g = dv(lambda e: e.scalar_tensor_tensor(out=x2[:, k, :], in0=tanh[:, :], scalar=w, in1=x2[:, k, :],
                                                op0=ALU.mult, op1=ALU.add), g, gates_ready[b])
        tanh_free[0] = ffn_last[0] = g
        if i == 1:
            g = ln3.run(x2[:, k, :], x2[:, k, :], g, None)
            x2_free[0] = put("sync", lambda e: e.dma_start(t["out"][b, k * P:k * P + P, :], x2[:, k, :]),
                             waits=[g], flag=out_stored, by=16)

    zt = sb("z", [P, DIM])

    def after(b, step):
        if step < 4:
            project_out(b, step)
        elif step < 6:
            transpose_x2(b, 2 * step - 8)
            transpose_x2(b, 2 * step - 7)
        elif step == 6:
            gates(b)
        elif step < 15:
            expert(b, (step - 7) // 2, (step - 7) % 2)

    load_x1(0)
    put("tensor", lambda e: e.nop(), waits=[ones_ready])
    keys(0)
    queries(0)
    for j in range(PER):
        maxima(0, j)
    last = None
    for g in range(NG):
        b, h = divmod(g, GROUPS)
        for kt in range(TILES):
            u = (g * TILES + kt) % 2
            p_ready[(g, kt)] = softmax_attention(sh, prog, stacks, g, kt, False, SCALE_CROSS, pt[u],
                                                 p_free[u] if g or kt > 1 else wall[0])
            last, prev = (g, kt), last
            if prev is not None:
                sums(*prev)
            if kt == 0:
                if h == 2 and b + 1 < BATCH:
                    load_x1(b + 1)
                if g + 1 < NG:
                    keys(g + 1)
                    queries(g + 1)
            if kt >= 1 and g + 1 < NG:
                maxima(g + 1, kt - 1)
                if kt == TILES - 1:
                    maxima(g + 1, kt)
            if b == 0 and h < 2:
                exp_ready = load_expert(h, kt)
            if b > 0:
                after(b - 1, h * TILES + kt)
    sums(*last)
    for step in range(15):
        after(BATCH - 1, step)
    sh.stores = [(out_stored, out_stored.count)]



SCRATCH = ("y_ar", "qa", "x1")


def kernel(x, ctx_1024, L0_attn_w_attn, L0_attn_b_attn, L0_attn_w_k2, L0_attn_b_k2, L0_attn_w_proj,
           L0_attn_b_proj, L0_xattn_Wv, L0_xattn_Wk, L0_xattn_Wq, L0_xattn_Wo, L0_xattn_bo,
           L0_ffn_gate_w, L0_ffn_w0, L0_ffn_b0, L0_ffn_w1, L0_ffn_b1):
    import concourse.bacc as bacc
    from concourse.bass_utils import run_bass_kernel_spmd

    def c(a):
        return np.ascontiguousarray(a)

    def columns(bias):
        return c(np.asarray(bias).reshape(-1, P).T)

    x, ctx_1024 = np.asarray(x), np.asarray(ctx_1024)
    arrays = {
        "x": c(x), "x_t": c(x.transpose(0, 2, 1)),
        "ctx": c(ctx_1024), "ctx_t": c(ctx_1024.transpose(0, 2, 1)),
        "w_attn_t": c(np.asarray(L0_attn_w_attn).T), "b_attn": columns(L0_attn_b_attn),
        "w_k2_t": c(np.asarray(L0_attn_w_k2).T), "b_k2": columns(L0_attn_b_k2),
        "w_proj_t": c(np.asarray(L0_attn_w_proj).T), "b_proj": c(np.asarray(L0_attn_b_proj)),
        "wv": c(L0_xattn_Wv), "wk": c(L0_xattn_Wk), "wq": c(L0_xattn_Wq),
        "wo_t": c(np.asarray(L0_xattn_Wo).T), "bo": c(np.asarray(L0_xattn_bo)),
        "gate_w": c(L0_ffn_gate_w),
        "w0_t": c(np.asarray(L0_ffn_w0).T), "b0": c(np.asarray(L0_ffn_b0)),
        "w1_t": c(np.asarray(L0_ffn_w1).T), "b1": c(np.asarray(L0_ffn_b1)),
    }
    nc = bacc.Bacc("TRN2", target_bir_lowering=False, num_devices=1)
    t = {n: nc.dram_tensor(f"in_{n}", list(a.shape), F32, kind="ExternalInput").ap() for n, a in arrays.items()}
    for n in SCRATCH:
        t[n] = nc.dram_tensor(f"scratch_{n}", [BATCH, SEQ, DIM], F32, kind="Internal").ap()
    t["out"] = nc.dram_tensor("out", [BATCH, SEQ, DIM], F32, kind="ExternalOutput").ap()
    build(nc, t)
    r = run_bass_kernel_spmd(nc, [{f"in_{n}": a for n, a in arrays.items()}], core_ids=[0])
    return r.results[0]["out"]
```

```python
from contextlib import ExitStack

import numpy as np

import concourse.bass as bass
from concourse import mybir

F32 = mybir.dt.float32
F32R = mybir.dt.float32r
BF16 = mybir.dt.bfloat16
ALU = mybir.AluOpType
ACT = mybir.ActivationFunctionType
AX = mybir.AxisListType.X

BATCH, SEQ, DIM, HEADS, EXPERTS = 8, 512, 512, 16, 8
P = 128
HEAD_DIM = DIM // HEADS
TILES = SEQ // P
GROUPS = DIM // P
PER = P // HEAD_DIM
NG = BATCH * GROUPS
SCALE_SELF = float(HEAD_DIM) ** -0.5
SCALE_CROSS = float(DIM) ** -0.5
LEAK = 0.02
EPS = 1e-5
NEG = -1.0e30
LEAD = 5


class Flag:

    def __init__(self, sem):
        self.sem, self.count = sem, 0


class Program:

    ENGINES = ("tensor", "vector", "scalar", "gpsimd", "sync")

    def __init__(self, nc, ctx):
        self.nc, self.ctx = nc, ctx
        self.queue = {e: [] for e in self.ENGINES}
        self.waited = {e: {} for e in self.ENGINES}

    def flag(self, name):
        return Flag(self.ctx.enter_context(self.nc.semaphore(name)))

    def put(self, engine, build, waits=(), flag=None, by=1):
        seen, need = self.waited[engine], {}
        for w in waits:
            if w is not None and seen.get(w[0], 0) < w[1]:
                need[w[0]] = max(need.get(w[0], 0), w[1])
        seen.update(need)
        self.queue[engine].append((list(need.items()), build, flag, by))
        if flag is None:
            return None
        flag.count += by
        return (flag, flag.count)

    def emit(self, engine, eng):
        for need, build, flag, by in self.queue[engine]:
            for f, value in need:
                eng.wait_ge(f.sem, value)
            ins = build(eng)
            if flag is not None:
                ins.then_inc(flag.sem, by)


def build(nc, t):
    sems = ExitStack()
    with sems:
        prog = Program(nc, sems)
        shared = Shared(nc, sems, prog)
        for phase in (self_softmax_phase, self_memory_phase, cross_phase):
            with ExitStack() as ctx:
                phase(nc, ctx, prog, shared, t)
        prog.put("sync", lambda e: e.nop(), waits=shared.stores)
        with nc.Block() as block:
            for engine in Program.ENGINES:
                bind(block, prog, engine)


def bind(block, prog, engine):
    def body(eng):
        prog.emit(engine, eng)

    {"tensor": block.tensor, "vector": block.vector, "scalar": block.scalar,
     "gpsimd": block.gpsimd, "sync": block.sync}[engine](body)


class Shared:

    def __init__(self, nc, ctx, prog):
        def sb(name, shape, dt=F32):
            return ctx.enter_context(nc.sbuf_tensor(name, shape, dt))

        self.bank = [ctx.enter_context(nc.psum_tensor(f"bank{i}", [P, 512], F32)) for i in range(8)]
        self.bank_read = [None] * 8
        self.ident = sb("ident", [P, P])
        self.identb = sb("identb", [P, P], BF16)
        self.future = sb("future", [P, P], BF16)
        self.ones = sb("ones", [P, HEAD_DIM])
        self.prog, self.pool_last = prog, None
        self.wall = []
        self.stores = []
        names = ("scores", "scores_t", "pv", "dense", "small_t")
        self.pe = {n: prog.flag(f"pe_{n}") for n in names}
        self.dve = {n: prog.flag(f"dve_{n}") for n in ("max", "split", "norm", "ln", "misc", "ffn")}
        self.act = {n: prog.flag(f"act_{n}") for n in ("exp", "evac", "misc", "ln")}
        self.pool = {n: prog.flag(f"pool_{n}") for n in ("mask", "const")}

        const = self.pool["const"]
        on_pool(self, lambda e: e.memset(self.ident[:, :], 0.0), [], const)
        on_pool(self, lambda e: e.memset(self.identb[:, :], 0.0), [], const)
        on_pool(self, lambda e: e.memset(self.future[:, :], 0.0), [], const)
        on_pool(self, lambda e: e.memset(self.ones[:, :], 1.0), [], const)
        for m in (self.ident, self.identb):
            on_pool(self, lambda e, m=m: e.affine_select(
                out=m[:, :], in_=m[:, :], compare_op=ALU.not_equal, fill=1.0, base=0,
                pattern=[[-1, P]], channel_multiplier=1), [], const)
        self.const = on_pool(self, lambda e: e.affine_select(
            out=self.future[:, :], in_=self.future[:, :], compare_op=ALU.is_ge, fill=NEG, base=0,
            pattern=[[-1, P]], channel_multiplier=1), [], const)


def weave(*tasks):
    live = [[gen, 0.0, float(total)] for gen, total in tasks if gen is not None]
    while live:
        task = min(live, key=lambda x: x[1] / x[2])
        try:
            task[1] += next(task[0])
        except StopIteration:
            live.remove(task)


def chain(*gens):
    for gen in gens:
        yield from gen


def run(gen):
    for _ in gen:
        pass


def on_pool(sh, build, waits, flag):
    sh.pool_last = sh.prog.put("gpsimd", build, waits=[*waits, sh.pool_last], flag=flag)
    return sh.pool_last


def split(prog, engine_hi, hi, lo, x, waits, flag, act_flag=None):
    if engine_hi == "scalar":
        got = prog.put("scalar", lambda e: e.activation(hi, x, ACT.Copy), waits=waits, flag=act_flag)
    else:
        got = prog.put("vector", lambda e: e.tensor_copy(hi, x), waits=waits, flag=flag)
    return prog.put("vector", lambda e: e.tensor_tensor(lo, x, hi.bitcast(F32), ALU.subtract),
                    waits=[*waits, got], flag=flag)


class Banks:

    def __init__(self, *numbers):
        self.idle = list(numbers)

    def turn(self):
        self.idle.append(self.idle.pop(0))
        return self.idle[-1]

    def hold(self):
        return self.idle.pop(0)

    def release(self, bank):
        self.idle.append(bank)


class Stacks:

    def __init__(self, nc, ctx, prog, name, operands, ring):
        self.prog, self.ring = prog, ring
        self.tile = [ctx.enter_context(nc.sbuf_tensor(f"{name}{r}", [P, operands, PER, SEQ], F32R))
                     for r in range(ring)]
        self.landed = [prog.flag(f"{name}_landed{r}") for r in range(ring)]
        self.ready = {}
        self.read = [None] * ring

    def load(self, group, stage, staged):
        slot = group % self.ring
        dst, flag = self.tile[slot], self.landed[slot]
        h = HEAD_DIM
        for j in range(PER):
            rows = slice(h * j, h * j + h)
            for band, first, step in ((0, 0, 2), (1, 1, 1), (2, 0, 3)):
                src = stage[rows, first:first + step + 1:step, :]
                out = dst[h * band:h * band + h, :, j, :].bitcast(F32)
                got = self.prog.put("sync", lambda e, src=src, out=out: e.dma_start(out, src),
                                    waits=[staged, self.read[slot]], flag=flag, by=16)
        self.ready[group] = got
        return got


def softmax_attention(sh, prog, stacks, group, kt, causal, scale, ptile, p_free, p_ready):
    slot = group % stacks.ring
    first = kt * P if causal else 0
    q0 = min(first, SEQ - 256)
    for j in range(PER):
        b = 2 + sh.st_next
        sh.st_next ^= 1
        bank = sh.bank[b]
        kq = stacks.tile[slot]
        done = prog.put("tensor", lambda e, bank=bank, j=j: e.matmul(
            bank[:, 0:SEQ - q0], kq[0:98, 1, j, kt * P:kt * P + P], kq[0:98, 0, j, q0:SEQ],
            start=True, stop=True),
            waits=[stacks.ready[group], sh.shift_ready[group], sh.bank_read[b]], flag=sh.pe["scores_t"])
        if kt == TILES - 1 and j == PER - 1:
            stacks.read[slot] = done
        got = prog.put("scalar", lambda e, bank=bank, j=j: e.activation(
            ptile[:, j, 0:SEQ - first], bank[:, first - q0:SEQ - q0], ACT.Exp, scale=scale),
            waits=[done, p_free], flag=sh.act["exp"])
        sh.bank_read[b] = got
        if j < PER - 1:
            yield (SEQ - q0) / 2.4
    if causal:
        got = on_pool(sh, lambda e: e.affine_select(
            out=ptile[:, :, 0:P], in_=ptile[:, :, 0:P], compare_op=ALU.is_ge, fill=0.0, base=0,
            pattern=[[0, PER], [1, P]], channel_multiplier=-1), [got], sh.pool["mask"])
    p_ready[(group, kt)] = got
    yield (SEQ - q0) / 2.4


def weighted_sum(sh, prog, ptile, ready, v, v_ready, kt, causal, out_bank, flag):
    first = kt * P if causal else 0
    for j in range(PER):
        rows = slice(HEAD_DIM * j, HEAD_DIM * j + HEAD_DIM)
        got = prog.put("tensor", lambda e, j=j, rows=rows: e.matmul(
            sh.bank[out_bank][rows, first:SEQ], v(j), ptile[:, j, 0:SEQ - first],
            start=(kt == 0), stop=(kt == TILES - 1), skip_group_check=True),
            waits=[ready, v_ready, sh.bank_read[out_bank] if kt == 0 else None], flag=flag)
    return got


def head_max(sh, prog, stacks, group, j, causal):
    slot, m = group % stacks.ring, sh.negmax[group % 2]
    kq = stacks.tile[slot]
    for qt in range(TILES):
        b = sh.sm_next
        sh.sm_next ^= 1
        bank = sh.bank[b]
        keys = P * (qt + 1) if causal else SEQ
        done = prog.put("tensor", lambda e, bank=bank, qt=qt, keys=keys: e.matmul(
            bank[:, 0:max(keys, 256)], kq[0:96, 0, j, qt * P:qt * P + P], kq[0:96, 1, j, 0:max(keys, 256)],
            start=True, stop=not causal, skip_group_check=True),
            waits=[stacks.ready[group], sh.bank_read[b]], flag=sh.pe["scores"])
        if causal:
            done = prog.put("tensor", lambda e, bank=bank, qt=qt: e.matmul(
                bank[:, qt * P:qt * P + P], sh.identb[:, :], sh.future[:, :],
                start=False, stop=True, skip_group_check=True),
                waits=[sh.const], flag=sh.pe["scores"])
        col = j * TILES + qt
        got = prog.put("vector", lambda e, bank=bank, keys=keys, col=col: e.reduce_max(
            m[:, col:col + 1], bank[:, 0:keys], AX, negate=True),
            waits=[done, sh.negmax_read[group % 2]], flag=sh.dve["max"])
        sh.bank_read[b] = got
        yield max(keys, 256) / 2.4 + (60 if causal else 0)
    sh.maxed[group] = got


def shift_rows(sh, prog, stacks, group, maxed, bank):
    m, hl, slot = sh.negmax[group % 2], sh.shift[group % 2], group % stacks.ring
    n = PER * TILES
    done = prog.put("tensor", lambda e: e.transpose(sh.bank[bank][0:n, 0:P], m[:, :], sh.ident[:, :]),
                    waits=[maxed, sh.const, sh.bank_read[bank]], flag=sh.pe["small_t"])
    sh.negmax_read[group % 2] = done
    x = sh.bank[bank][0:n, 0:P]
    free = sh.shift_free[group % 2]
    hi = prog.put("scalar", lambda e: e.activation(hl[:, 0, :].bitcast(F32R), x, ACT.Copy),
                  waits=[done, free], flag=sh.act["misc"])
    lo = prog.put("vector", lambda e: e.tensor_tensor(hl[:, 1, :].bitcast(F32R), x, hl[:, 0, :], ALU.subtract),
                  waits=[hi, free], flag=sh.dve["misc"])
    sh.bank_read[bank] = lo
    for part in range(2):
        row = stacks.tile[slot][96 + part:97 + part, 0, :, :].rearrange("p j (t q) -> p (j t) q", q=P)
        got = prog.put("sync", lambda e, row=row, part=part: e.dma_start(row.bitcast(F32), hl[:, part, :]),
                       waits=[hi, lo, stacks.read[slot]], flag=stacks.landed[slot], by=16)
    sh.shift_free[group % 2] = got
    sh.shift_ready[group] = got


def open_softmax(nc, ctx, prog, sh, stacks, name):
    sh.negmax = [ctx.enter_context(nc.sbuf_tensor(f"{name}_negmax{i}", [P, PER * TILES], F32)) for i in range(2)]
    sh.shift = [ctx.enter_context(nc.sbuf_tensor(f"{name}_shift{i}", [PER * TILES, 2, P], F32)) for i in range(2)]
    sh.negmax_read, sh.shift_free, sh.shift_ready = [None] * 2, [None] * 2, {}
    sh.sm_next = sh.st_next = 0
    sh.maxed = {}
    for r in range(stacks.ring):
        got = on_pool(sh, lambda e, r=r: e.memset(stacks.tile[r][96:128, 1, :, :].bitcast(F32), 1.0),
                      sh.wall, sh.pool["const"])
    return got


class LayerNorm:

    def __init__(self, nc, ctx, sh, prog, name):
        sb = lambda n, s: ctx.enter_context(nc.sbuf_tensor(f"{name}_{n}", s, F32))
        self.sh, self.prog = sh, prog
        self.stats, self.mv = sb("stats", [P, TILES, 6]), sb("mv", [P, TILES, 2])
        self.rstd, self.shift, self.power = sb("rstd", [P, TILES]), sb("shift", [P, TILES]), sb("power", [P, TILES])
        self.power_ready = on_pool(sh, lambda e: e.memset(self.power[:, :], -0.5), sh.wall, sh.pool["const"])
        self.applied = None

    def statistics(self, k, r, ready):
        put, flag = self.prog.put, self.sh.dve["ln"]
        g = put("vector", lambda e: e.bn_stats(self.stats[:, k, :], r), waits=[ready, self.applied, *self.sh.wall],
                flag=flag)
        self.last = put("vector", lambda e: e.bn_aggr(self.mv[:, k, :], self.stats[:, k, :]), waits=[g], flag=flag)

    def scales(self):
        put, flag = self.prog.put, self.sh.dve["ln"]
        g = put("vector", lambda e: e.tensor_scalar(self.rstd[:, :], self.mv[:, :, 1], EPS, None, ALU.add),
                waits=[self.last], flag=flag)
        g = on_pool(self.sh, lambda e: e.tensor_tensor(self.rstd[:, :], self.rstd[:, :], self.power[:, :], ALU.pow),
                    [g], self.sh.pool["mask"])
        self.ready = put("vector", lambda e: e.scalar_tensor_tensor(
            out=self.shift[:, :], in0=self.mv[:, :, 0], scalar=-1.0, in1=self.rstd[:, :],
            op0=ALU.mult, op1=ALU.mult), waits=[g], flag=flag)

    def apply(self, k, out, r, waits=()):
        self.applied = self.prog.put("scalar", lambda e: e.activation(
            out, r, ACT.Identity, bias=self.shift[:, k:k + 1], scale=self.rstd[:, k:k + 1]),
            waits=[self.ready, *waits], flag=self.sh.act["ln"])
        return self.applied


def matmul3(prog, out, pairs, waits, flag, start=True, stop=True):
    passes = [(a[x], b[y]) for a, b in pairs for x, y in ((0, 0), (1, 0), (0, 1))]
    for i, (a, b) in enumerate(passes):
        got = prog.put("tensor", lambda e, a=a, b=b, i=i: e.matmul(
            out, a, b, start=start and i == 0, stop=stop and i == len(passes) - 1),
            waits=waits, flag=flag if i == len(passes) - 1 else None)
        if i % 3 == 2 and i < len(passes) - 1:
            yield 3 * SEQ / 2.4
    return got


def load_split_weights(prog, sh, raw, raw_flags, jobs):
    free, got = [None] * len(raw), {}
    for i, (key, hi, lo, src) in enumerate(jobs):
        r = i % len(raw)
        n = hi.shape[-1]
        tile = raw[r][:, 0:n]
        landed = prog.put("sync", lambda e, tile=tile, src=src: e.dma_start(tile, src),
                          waits=[free[r], *sh.wall], flag=raw_flags[r], by=16)
        got[key] = split(prog, "vector", hi, lo, tile, [landed, *sh.wall], sh.dve["split"])
        free[r] = got[key]
    return got, free



def self_softmax_phase(nc, ctx, prog, sh, t):
    sb = lambda name, shape, dt=F32: ctx.enter_context(nc.sbuf_tensor(name, shape, dt))
    put = prog.put
    w_hi, w_lo = sb("wqk_hi", [P, GROUPS, 2 * DIM], F32R), sb("wqk_lo", [P, GROUPS, 2 * DIM], F32R)
    bias = sb("bqk", [P, 2 * GROUPS])
    xt_hi = [sb(f"xt_hi{i}", [P, GROUPS, SEQ], F32R) for i in range(2)]
    xt_lo = [sb(f"xt_lo{i}", [P, GROUPS, SEQ], F32R) for i in range(2)]
    raw = [sb(f"raw{i}", [P, SEQ]) for i in range(2)]
    raw_landed = [prog.flag(f"raw_landed{i}") for i in range(2)]
    stage = [sb(f"stage{i}", [P, 4, SEQ]) for i in range(2)]
    qa = [sb(f"qa_out{i}", [P, SEQ]) for i in range(2)]
    stacks = Stacks(nc, ctx, prog, "qk", 2, 3)
    pt = [sb(f"pt{i}", [P, PER, SEQ]) for i in range(2)]
    v = [sb(f"v{i}", [P, TILES, P]) for i in range(2)]
    v_landed = [prog.flag(f"v_landed{i}") for i in range(2)]
    recip, y_raw = sb("recip", [P, SEQ]), sb("y_raw", [P, SEQ])
    y_ar = [sb(f"y_ar{i}", [P, SEQ]) for i in range(2)]
    y_stored = [prog.flag(f"y_stored{i}") for i in range(2)]
    qa_stored = [prog.flag(f"qa_stored{i}") for i in range(2)]
    bias_landed = prog.flag("bqk_landed")
    ones_ready = open_softmax(nc, ctx, prog, sh, stacks, "self")
    Y, L, dense = 4, 5, Banks(6, 7)

    bias_ready = put("sync", lambda e: e.dma_start(bias[:, :], t["b_attn"]), flag=bias_landed, by=16)
    jobs = [((half, c), w_hi[:, c, half * DIM:(half + 1) * DIM], w_lo[:, c, half * DIM:(half + 1) * DIM],
             t["w_attn_t"][c * P:c * P + P, half * DIM:(half + 1) * DIM]) for half in range(2) for c in range(GROUPS)]
    w_ready, raw_free = load_split_weights(prog, sh, raw, raw_landed, jobs)
    w_all = w_ready[(1, GROUPS - 1)]

    xt_ready, xt_free = {}, [None, None]

    def load_xt(b, c):
        r = c % 2
        landed = put("sync", lambda e: e.dma_start(raw[r][:, :], t["x_t"][b, c * P:c * P + P, :]),
                     waits=[raw_free[r]], flag=raw_landed[r], by=16)
        xt_ready[b] = split(prog, "vector", xt_hi[b % 2][:, c, :], xt_lo[b % 2][:, c, :], raw[r][:, :],
                            [landed, xt_free[b % 2]], sh.dve["split"])
        raw_free[r] = xt_ready[b]

    qa_free = [None, None]

    def project(g, which):
        b, h = divmod(g, GROUPS)
        bank, st = dense.hold(), stage[g % 2]
        col = which * DIM + h * P
        pairs = [((w_hi[:, c, col:col + P], w_lo[:, c, col:col + P]),
                  (xt_hi[b % 2][:, c, :], xt_lo[b % 2][:, c, :])) for c in range(GROUPS)]
        done = yield from matmul3(prog, sh.bank[bank][:, :], pairs, [w_all, xt_ready[b], sh.bank_read[bank]], sh.pe["dense"])
        if which == 1 and h == GROUPS - 1:
            xt_free[b % 2] = done
        hi, lo = st[:, 2 * which, :], st[:, 2 * which + 1, :]
        x = put("scalar", lambda e: e.activation(lo, sh.bank[bank][:, :], ACT.Identity,
                                                 bias=bias[:, which * GROUPS + h:which * GROUPS + h + 1]),
                waits=[done, bias_ready, stage_free[g % 2]], flag=sh.act["evac"])
        sh.bank_read[bank] = x
        dense.release(bank)
        if which == 0:
            out = qa[g % 2]
            got = put("vector", lambda e: e.scalar_tensor_tensor(
                out=out[:, :], in0=lo, scalar=LEAK, in1=lo, op0=ALU.mult, op1=ALU.min),
                waits=[x, qa_free[g % 2]], flag=sh.dve["misc"])
            qa_free[g % 2] = put("sync", lambda e: e.dma_start(t["qa"][b, h * P:h * P + P, :], out[:, :]),
                                 waits=[got], flag=qa_stored[g % 2], by=16)
            x = got
        staged = split(prog, "vector", hi.bitcast(F32R), lo.bitcast(F32R), lo, [x], sh.dve["split"])
        if which == 1:
            stage_free[g % 2] = stacks.load(g, st, staged)
        yield 3 * SEQ / 2.4

    stage_free = [None, None]
    v_ready, v_free = {}, [None, None]

    def load_v(g):
        b, h = divmod(g, GROUPS)
        src = t["x"][b].rearrange("(k p) d -> p k d", p=P)[:, :, h * P:h * P + P]
        v_ready[g] = put("sync", lambda e: e.dma_start(v[g % 2][:, :, :], src), waits=[v_free[g % 2]],
                         flag=v_landed[g % 2], by=16)

    p_free, p_ready = [None, None], {}
    y_free = [None, None]

    norm_last = [None]

    def sums(g, kt):
        u = (g * TILES + kt) % 2
        cost = PER * (SEQ - kt * P) / 2.4
        got = weighted_sum(sh, prog, pt[u], p_ready[(g, kt)],
                           lambda j: v[g % 2][:, kt, HEAD_DIM * j:HEAD_DIM * j + HEAD_DIM],
                           v_ready[g], kt, True, Y, sh.pe["pv"])
        if kt == TILES - 1:
            v_free[g % 2] = got
            raw_ready = put("scalar", lambda e: e.activation(y_raw[:, :], sh.bank[Y][:, :], ACT.Copy),
                            waits=[got, norm_last[0]], flag=sh.act["misc"])
            sh.bank_read[Y] = raw_ready
        yield cost
        got = weighted_sum(sh, prog, pt[u], p_ready[(g, kt)], lambda j: sh.ones[:, :], sh.const, kt, True, L,
                           sh.pe["pv"])
        p_free[u] = got
        yield cost
        if kt < TILES - 1:
            return
        b, h = divmod(g, GROUPS)
        got = put("scalar", lambda e: e.activation(recip[:, :], sh.bank[L][:, :], ACT.Copy),
                  waits=[got, norm_last[0]], flag=sh.act["misc"])
        sh.bank_read[L] = got
        for q in range(TILES):
            cols = slice(q * P, q * P + P)
            r = put("vector", lambda e, cols=cols: e.reciprocal(recip[:, cols], recip[:, cols]), waits=[got],
                    flag=sh.dve["norm"])
            yield 1
        n = put("vector", lambda e: e.tensor_tensor(y_ar[g % 2][:, :], y_raw[:, :], recip[:, :], ALU.mult),
                waits=[r, raw_ready, y_free[g % 2]], flag=sh.dve["norm"])
        norm_last[0] = n
        y_free[g % 2] = put("sync", lambda e: e.dma_start(t["y_ar"][b, h * P:h * P + P, :], y_ar[g % 2][:, :]),
                            waits=[n], flag=y_stored[g % 2], by=16)

    def maxima(g, j):
        yield from head_max(sh, prog, stacks, g, j, True)
        if j == PER - 1:
            shift_rows(sh, prog, stacks, g, sh.maxed[g], dense.turn())
            yield 53

    for c in range(GROUPS):
        load_xt(0, c)
    put("tensor", lambda e: e.nop(), waits=[ones_ready])
    for g in range(2):
        run(project(g, 0))
        run(project(g, 1))
        load_v(g)
    for n in range(LEAD):
        run(maxima(*divmod(n, PER)))
    last = None
    for g in range(NG):
        for kt in range(TILES):
            u = (g * TILES + kt) % 2
            ahead = g * TILES + kt + LEAD
            nb = g // GROUPS + 1
            if nb < BATCH and kt >= 2 and g % GROUPS < 2:
                load_xt(nb, (g % GROUPS) * 2 + kt - 2)
            if kt == 1 and 1 <= g and g + 1 < NG:
                load_v(g + 1)
            weave(
                (softmax_attention(sh, prog, stacks, g, kt, True, SCALE_SELF, pt[u], p_free[u], p_ready), 700),
                (sums(*last) if last else None, 1800),
                (maxima(*divmod(ahead, PER)) if ahead < NG * PER else None, 900),
                (project(g + 2, kt) if kt < 2 and g + 2 < NG else None, 2560),
            )
            last = (g, kt)
    run(sums(*last))
    tail = [f for f in (y_free + qa_free)]
    sh.wall = [(f, f.count) for f in (*sh.pe.values(), *sh.dve.values(), *sh.act.values(), *sh.pool.values(),
                                      *stacks.landed, *raw_landed, *v_landed) if f.count] + tail



def self_memory_phase(nc, ctx, prog, sh, t):
    sb = lambda name, shape, dt=F32: ctx.enter_context(nc.sbuf_tensor(name, shape, dt))
    put = prog.put
    w_hi, w_lo = sb("wk2_hi", [P, GROUPS, DIM], F32R), sb("wk2_lo", [P, GROUPS, DIM], F32R)
    wp = sb("wproj", [P, GROUPS, DIM])
    b2, b2c, bproj = sb("bk2", [P, GROUPS]), sb("bk2_scaled", [P, GROUPS]), sb("bproj", [P, DIM])
    xt_hi = [sb(f"mxt_hi{i}", [P, GROUPS, SEQ], F32R) for i in range(2)]
    xt_lo = [sb(f"mxt_lo{i}", [P, GROUPS, SEQ], F32R) for i in range(2)]
    raw = [sb(f"mraw{i}", [P, SEQ]) for i in range(2)]
    raw_landed = [prog.flag(f"mraw_landed{i}") for i in range(2)]
    stage = sb("mstage", [P, 4, SEQ])
    stacks = Stacks(nc, ctx, prog, "ma", 2, 2)
    mt = [sb(f"mt{i}", [P, PER, SEQ]) for i in range(2)]
    y_ar = [sb(f"my_ar{i}", [P, SEQ]) for i in range(3)]
    xs = [sb(f"x_next{i}", [P, TILES, P]) for i in range(2)]
    ev = [sb(f"e{i}", [P, TILES, P]) for i in range(2)]
    y = [sb(f"y{i}", [P, GROUPS, SEQ]) for i in range(2)]
    xr = sb("mxr", [P, TILES, DIM])
    xr_ready = [None]
    ln = LayerNorm(nc, ctx, sh, prog, "ln1")
    small = prog.flag("m_small_landed")
    qa_landed = prog.flag("m_qa_landed")
    y_landed = [prog.flag(f"m_y_landed{i}") for i in range(3)]
    xs_landed = [prog.flag(f"m_xs_landed{i}") for i in range(2)]
    xr_landed, x1_stored = prog.flag("m_xr_landed"), prog.flag("x1_stored")
    Y2, dense = 4, Banks(5, 6, 7)

    wall = sh.wall
    put("sync", lambda e: e.dma_start(b2[:, :], t["b_k2"]), waits=wall, flag=small, by=16)
    put("sync", lambda e: e.dma_start(bproj[:, :], t["b_proj"].partition_broadcast(P)), flag=small, by=16)
    small_ready = put("sync", lambda e: e.dma_start(
        wp[:, :, :], t["w_proj_t"].rearrange("(c p) n -> p c n", p=P)), flag=small, by=16)
    kscale = 0.5 * LEAK * SCALE_SELF
    b2_ready = put("vector", lambda e: e.tensor_scalar(b2c[:, :], b2[:, :], kscale, None, ALU.mult),
                   waits=[small_ready], flag=sh.dve["misc"])
    for i in range(2):
        xs_zero = on_pool(sh, lambda e, i=i: e.memset(xs[i][:, :, :], 0.0), wall, sh.pool["const"])
    jobs = [(c, w_hi[:, c, :], w_lo[:, c, :], t["w_k2_t"][c * P:c * P + P, :]) for c in range(GROUPS)]
    w_ready, raw_free = load_split_weights(prog, sh, raw, raw_landed, jobs)
    w_all = w_ready[GROUPS - 1]
    xt_ready, xt_free = {}, [None, None]

    def load_xt(b, c):
        r = c % 2
        landed = put("sync", lambda e: e.dma_start(raw[r][:, :], t["x_t"][b, c * P:c * P + P, :]),
                     waits=[raw_free[r]], flag=raw_landed[r], by=16)
        xt_ready[b] = split(prog, "vector", xt_hi[b % 2][:, c, :], xt_lo[b % 2][:, c, :], raw[r][:, :],
                            [landed, xt_free[b % 2], *wall], sh.dve["split"])
        raw_free[r] = xt_ready[b]

    stage_free = [None]

    def project(g):
        b, h = divmod(g, GROUPS)
        bank = dense.hold()
        pairs = [((w_hi[:, c, h * P:h * P + P], w_lo[:, c, h * P:h * P + P]),
                  (xt_hi[b % 2][:, c, :], xt_lo[b % 2][:, c, :])) for c in range(GROUPS)]
        done = yield from matmul3(prog, sh.bank[bank][:, :], pairs, [w_all, xt_ready[b], sh.bank_read[bank]], sh.pe["dense"])
        if h == GROUPS - 1:
            xt_free[b % 2] = done
        q_hi, q_lo, k_hi, k_lo = (stage[:, i, :] for i in range(4))
        landed = put("sync", lambda e: e.dma_start(q_lo, t["qa"][b, h * P:h * P + P, :]),
                     waits=[stage_free[0], *wall], flag=qa_landed, by=16)
        th = put("scalar", lambda e: e.activation(k_lo, sh.bank[bank][:, :], ACT.Tanh,
                                                  bias=b2c[:, h:h + 1], scale=kscale),
                 waits=[done, b2_ready, stage_free[0], *wall], flag=sh.act["evac"])
        sh.bank_read[bank] = th
        dense.release(bank)
        hi = put("vector", lambda e: e.tensor_scalar(k_hi.bitcast(F32R), k_lo, 1.0, None, ALU.add),
                 waits=[th], flag=sh.dve["split"])
        put("vector", lambda e: e.scalar_tensor_tensor(out=k_lo.bitcast(F32R), in0=k_lo, scalar=1.0, in1=k_hi,
                                                       op0=ALU.add, op1=ALU.subtract),
            waits=[hi], flag=sh.dve["split"])
        staged = split(prog, "vector", q_hi.bitcast(F32R), q_lo.bitcast(F32R), q_lo, [landed], sh.dve["split"])
        stage_free[0] = stacks.load(g, stage, staged)
        yield 3 * SEQ / 2.4

    y_ready, y_free, xs_ready, xs_free = {}, [None] * 3, {}, [None] * 2

    def load_y(g):
        b, h = divmod(g, GROUPS)
        ry = g % 3
        y_ready[g] = put("sync", lambda e: e.dma_start(y_ar[ry][:, :], t["y_ar"][b, h * P:h * P + P, :]),
                         waits=[y_free[ry], *wall], flag=y_landed[ry], by=16)
        r = g % 2
        cols = slice(h * P, h * P + P)
        body = t["x"][b, 1:1 + (TILES - 1) * P, cols].rearrange("(k p) d -> p k d", p=P)
        put("sync", lambda e: e.dma_start(xs[r][:, 0:TILES - 1, :], body),
            waits=[xs_free[r], xs_zero], flag=xs_landed[r], by=16)
        rest = t["x"][b, 1 + (TILES - 1) * P:SEQ, cols]
        xs_ready[g] = put("sync", lambda e: e.dma_start(xs[r][0:P - 1, TILES - 1, :], rest),
                          waits=[xs_free[r]], flag=xs_landed[r], by=16)

    e_ready, e_free = {}, [None] * 2

    def values(g):
        bank = dense.turn()
        for k in range(TILES):
            done = put("tensor", lambda e, k=k: e.transpose(
                sh.bank[bank][:, k * P:k * P + P], y_ar[g % 3][:, k * P:k * P + P], sh.ident[:, :]),
                waits=[y_ready[g], sh.bank_read[bank]], flag=sh.pe["small_t"])
        e_ready[g] = put("vector", lambda e: e.tensor_tensor(
            ev[g % 2][:, :, :].rearrange("p k d -> p (k d)"), xs[g % 2][:, :, :].rearrange("p k d -> p (k d)"),
            sh.bank[bank][:, :], ALU.subtract),
            waits=[done, xs_ready[g], e_free[g % 2], *wall], flag=sh.dve["misc"])
        sh.bank_read[bank] = xs_free[g % 2] = e_ready[g]
        yield TILES * 53

    m_ready, m_free = {}, [None] * 2
    st_next = [0]

    def memory_scores(g, kt):
        u, slot, first = (g * TILES + kt) % 2, g % stacks.ring, kt * P
        q0 = min(first, SEQ - 256)
        kq = stacks.tile[slot]
        for j in range(PER):
            b = st_next[0]
            st_next[0] = (b + 1) % 4
            done = put("tensor", lambda e, b=b, j=j: e.matmul(
                sh.bank[b][:, 0:SEQ - q0], kq[0:96, 1, j, first:first + P], kq[0:96, 0, j, q0:SEQ],
                start=True, stop=True),
                waits=[stacks.ready[g], sh.bank_read[b]], flag=sh.pe["scores_t"])
            got = put("scalar", lambda e, b=b, j=j: e.activation(
                mt[u][:, j, 0:SEQ - first], sh.bank[b][:, first - q0:SEQ - q0], ACT.Copy, scale=0.5 * SCALE_SELF),
                waits=[done, m_free[u], *wall], flag=sh.act["exp"])
            sh.bank_read[b] = got
            if j < PER - 1:
                yield (SEQ - q0) / 2.4
        if kt == TILES - 1:
            stacks.read[slot] = done
        m_ready[(g, kt)] = on_pool(sh, lambda e: e.affine_select(
            out=mt[u][:, :, 0:P], in_=mt[u][:, :, 0:P], compare_op=ALU.is_ge, fill=0.0, base=-1,
            pattern=[[0, PER], [1, P]], channel_multiplier=-1), [got], sh.pool["mask"])
        yield (SEQ - q0) / 2.4

    ysum_ready, ysum_free = {}, [None] * 2

    def memory_sums(g, kt):
        b, h = divmod(g, GROUPS)
        u = (g * TILES + kt) % 2
        got = weighted_sum(sh, prog, mt[u], m_ready[(g, kt)],
                           lambda j: ev[g % 2][:, kt, HEAD_DIM * j:HEAD_DIM * j + HEAD_DIM],
                           e_ready[g], kt, True, Y2, sh.pe["pv"])
        m_free[u] = got
        yield PER * (SEQ - kt * P) / 2.4
        if kt < TILES - 1:
            return
        e_free[g % 2] = got
        n = put("vector", lambda e: e.tensor_tensor(y[b % 2][:, h, :], sh.bank[Y2][:, :], y_ar[g % 3][:, :], ALU.add),
                waits=[got, y_ready[g], ysum_free[b % 2], *wall], flag=sh.dve["norm"])
        sh.bank_read[Y2] = y_free[g % 3] = ysum_ready[b] = n

    xr_free = [None]

    def project_out(b, k):
        bank = dense.hold()
        x = xr[:, k, :]
        if k == 0:
            xr_ready[0] = put("sync", lambda e: e.dma_start(
                xr[:, :, :], t["x"][b].rearrange("(k p) d -> p k d", p=P)),
                waits=[xr_free[0], *wall], flag=xr_landed, by=16)
        for c in range(GROUPS):
            done = put("tensor", lambda e, c=c: e.matmul(
                sh.bank[bank][:, :], y[b % 2][:, c, k * P:k * P + P], wp[:, c, :],
                start=(c == 0), stop=(c == GROUPS - 1)),
                waits=[ysum_ready[b], small_ready, sh.bank_read[bank]], flag=sh.pe["dense"])
            if c < GROUPS - 1:
                yield 4 * SEQ / 2.4
        if k == TILES - 1:
            ysum_free[b % 2] = done
        got = put("vector", lambda e: e.scalar_tensor_tensor(
            out=x, in0=bproj[:, :], scalar=2.0, in1=x, op0=ALU.mult, op1=ALU.add),
            waits=[xr_ready[0], small_ready], flag=sh.dve["misc"])
        got = put("vector", lambda e: e.tensor_tensor(x, sh.bank[bank][:, :], x, ALU.add),
                  waits=[done, got], flag=sh.dve["misc"])
        sh.bank_read[bank] = got
        dense.release(bank)
        ln.statistics(k, x, got)
        yield 4 * SEQ / 2.4
        if k < TILES - 1:
            return
        ln.scales()
        for i in range(TILES):
            got = ln.apply(i, xr[:, i, :], xr[:, i, :])
            yield 1
        xr_free[0] = put("sync", lambda e: e.dma_start(t["x1"][b].rearrange("(k p) d -> p k d", p=P), xr[:, :, :]),
                         waits=[got], flag=x1_stored, by=16)

    for c in range(GROUPS):
        load_xt(0, c)
    load_y(0)
    run(project(0))
    run(values(0))
    last = None
    for g in range(NG):
        b, h = divmod(g, GROUPS)
        for kt in range(TILES):
            if kt == 0 and g + 1 < NG:
                load_y(g + 1)
            if b + 1 < BATCH and kt >= 2 and h < 2:
                load_xt(b + 1, 2 * h + kt - 2)
            weave(
                (memory_scores(g, kt), 700),
                (memory_sums(*last) if last else None, 900),
                (project(g + 1) if kt == 0 and g + 1 < NG else None, 2560),
                (values(g + 1) if kt == 2 and g + 1 < NG else None, 200),
                (project_out(b - 1, h) if kt in (1,) and b > 0 else None, 3400),
            )
            last = (g, kt)
    run(memory_sums(*last))
    for k in range(TILES):
        run(project_out(BATCH - 1, k))
    sh.wall = [(f, f.count) for f in (*sh.pe.values(), *sh.dve.values(), *sh.act.values(), *sh.pool.values(),
                                      *stacks.landed, *raw_landed, *y_landed, *xs_landed, xr_landed, x1_stored,
                                      qa_landed, small) if f.count]



def cross_phase(nc, ctx, prog, sh, t):
    sb = lambda name, shape, dt=F32: ctx.enter_context(nc.sbuf_tensor(name, shape, dt))
    put = prog.put
    wall = sh.wall
    wo = sb("wo", [P, GROUPS, DIM])
    fold = sb("fold", [P, 3, P])
    a_hi, a_lo = sb("a_hi", [P, P], F32R), sb("a_lo", [P, P], F32R)
    e_hi = sb("exp_hi", [P, 2, GROUPS, DIM], F32R)
    e_lo = sb("exp_lo", [P, 2, GROUPS, DIM], F32R)
    gate_hi, gate_lo = sb("gate_hi", [P, GROUPS, EXPERTS], F32R), sb("gate_lo", [P, GROUPS, EXPERTS], F32R)
    gate_raw = sb("gate_raw", [P, GROUPS, EXPERTS])
    bo = sb("bo", [P, DIM])
    be = sb("bias_exp", [P, 2, DIM])
    raw = [sb(f"craw{i}", [P, SEQ]) for i in range(2)]
    raw_landed = [prog.flag(f"craw_landed{i}") for i in range(2)]
    stacks = Stacks(nc, ctx, prog, "cqk", 2, 3)
    stage = sb("cstage", [P, 4, SEQ])
    pt = [sb(f"cpt{i}", [P, PER, SEQ]) for i in range(2)]
    v = [sb(f"cv{i}", [P, TILES, P]) for i in range(2)]
    v_landed = [prog.flag(f"cv_landed{i}") for i in range(2)]
    rowsum, y_raw = sb("crowsum", [P, SEQ]), sb("cy_raw", [P, SEQ])
    recip = sb("crecip", [P, TILES * PER])
    y = [sb(f"cy{i}", [P, GROUPS, SEQ]) for i in range(2)]
    x1 = [sb(f"cx1_{i}", [P, TILES, DIM]) for i in range(2)]
    x1_landed = [prog.flag(f"cx1_landed{i}") for i in range(2)]
    x1t = sb("x1t", [P, 2, SEQ], F32R)
    x2 = sb("x2", [P, TILES, DIM])
    x2t_hi, x2t_lo = sb("x2t_hi", [P, GROUPS, SEQ], F32R), sb("x2t_lo", [P, GROUPS, SEQ], F32R)
    tanh = [sb(f"tanh{i}", [P, DIM]) for i in range(2)]
    lt = sb("logits_t", [EXPERTS, SEQ])
    lg = sb("logits", [P, TILES, EXPERTS])
    gs = {n: sb(f"gate_{n}", [P, TILES]) for n in ("max", "sum", "rest", "keep0", "keep1", "w0", "w1")}
    ge = sb("gate_exp", [P, TILES, EXPERTS])
    gb = sb("gate_beats", [P, TILES, EXPERTS])
    ln2 = LayerNorm(nc, ctx, sh, prog, "ln2")
    ln3 = LayerNorm(nc, ctx, sh, prog, "ln3")
    out_stored = prog.flag("out_stored")
    small = prog.flag("c_small_landed")
    k_landed = prog.flag("c_keys_landed")
    ones_ready = open_softmax(nc, ctx, prog, sh, stacks, "cross")
    Y, L, dense = 4, 5, Banks(6, 7)

    zero = on_pool(sh, lambda e: e.memset(fold[:, :, :], 0.0), wall, sh.pool["const"])
    for i, name in enumerate(("wq", "wk", "wv")):
        for j in range(PER):
            d = slice(HEAD_DIM * j, HEAD_DIM * j + HEAD_DIM)
            put("sync", lambda e, i=i, d=d, name=name: e.dma_start(fold[d, i, d], t[name]),
                waits=[zero, *wall], flag=small, by=16)
    put("sync", lambda e: e.dma_start(bo[:, :], t["bo"].partition_broadcast(P)), flag=small, by=16)
    put("sync", lambda e: e.dma_start(be[:, 0, :], t["b0"].partition_broadcast(P)), flag=small, by=16)
    put("sync", lambda e: e.dma_start(be[:, 1, :], t["b1"].partition_broadcast(P)), flag=small, by=16)
    small_ready = put("sync", lambda e: e.dma_start(
        gate_raw[:, :, :], t["gate_w"].rearrange("(c p) n -> p c n", p=P)), flag=small, by=16)
    bank = dense.turn()
    done = put("tensor", lambda e, bank=bank: e.matmul(sh.bank[bank][:, 0:P], fold[:, 0, :], fold[:, 1, :],
                                                       start=True, stop=True),
               waits=[small_ready, *wall], flag=sh.pe["dense"])
    a_ready = split(prog, "vector", a_hi[:, :], a_lo[:, :], sh.bank[bank][:, 0:P], [done, *wall], sh.dve["split"])
    sh.bank_read[bank] = a_ready
    raw_free = [None, None]
    for c in range(GROUPS):
        bank, r = dense.turn(), c % 2
        landed = put("sync", lambda e, r=r, c=c: e.dma_start(raw[r][:, :], t["wo_t"][c * P:c * P + P, :]),
                     waits=[raw_free[r], *wall], flag=raw_landed[r], by=16)
        done = put("tensor", lambda e, bank=bank, r=r: e.matmul(sh.bank[bank][:, :], fold[:, 2, :], raw[r][:, :],
                                                                start=True, stop=True),
                   waits=[small_ready, landed, sh.bank_read[bank]], flag=sh.pe["dense"])
        raw_free[r] = done
        wo_ready = put("vector", lambda e, bank=bank, c=c: e.tensor_copy(wo[:, c, :], sh.bank[bank][:, :]),
                       waits=[done], flag=sh.dve["misc"])
        sh.bank_read[bank] = wo_ready
    gate_ready = split(prog, "vector", gate_hi[:, :, :], gate_lo[:, :, :], gate_raw[:, :, :], [small_ready],
                       sh.dve["split"])

    def load_expert(i, c):
        r = c % 2
        landed = put("sync", lambda e: e.dma_start(raw[r][:, :], t[f"w{i}_t"][c * P:c * P + P, :]),
                     waits=[raw_free[r], *wall], flag=raw_landed[r], by=16)
        raw_free[r] = split(prog, "vector", e_hi[:, i, c, :], e_lo[:, i, c, :], raw[r][:, :], [landed],
                            sh.dve["split"])
        return raw_free[r]

    x1_ready, x1_used, x1_free = {}, {}, [None, None]

    def load_x1(b):
        x1_ready[b] = put("sync", lambda e: e.dma_start(
            x1[b % 2][:, :, :], t["x1"][b].rearrange("(k p) d -> p k d", p=P)),
            waits=[x1_free[b % 2], *wall], flag=x1_landed[b % 2], by=16)

    stage_free, x1t_free = [None], [None]
    v_ready, v_free = {}, [None, None]

    def keys(g):
        b, h = divmod(g, GROUPS)
        k_hi, k_lo = stage[:, 2, :], stage[:, 3, :]
        landed = put("sync", lambda e: e.dma_start(k_lo, t["ctx_t"][b, h * P:h * P + P, :]),
                     waits=[stage_free[0], *wall], flag=k_landed, by=16)
        split(prog, "vector", k_hi.bitcast(F32R), k_lo.bitcast(F32R), k_lo, [landed], sh.dve["split"])

    def load_values(g):
        b, h = divmod(g, GROUPS)
        src = t["ctx"][b].rearrange("(k p) d -> p k d", p=P)[:, :, h * P:h * P + P]
        v_ready[g] = put("sync", lambda e: e.dma_start(v[g % 2][:, :, :], src), waits=[v_free[g % 2], *wall],
                         flag=v_landed[g % 2], by=16)

    def queries(g):
        b, h = divmod(g, GROUPS)
        bank = dense.turn()
        for k in range(TILES):
            done = put("tensor", lambda e, k=k: e.transpose(
                sh.bank[bank][:, k * P:k * P + P], x1[b % 2][:, k, h * P:h * P + P], sh.ident[:, :]),
                waits=[x1_ready[b], sh.bank_read[bank]], flag=sh.pe["small_t"])
        x1_used[b] = done
        got = put("scalar", lambda e: e.activation(x1t[:, 0, :], sh.bank[bank][:, :], ACT.Copy),
                  waits=[done, x1t_free[0], *wall], flag=sh.act["evac"])
        got = put("vector", lambda e: e.tensor_tensor(x1t[:, 1, :], sh.bank[bank][:, :],
                                                      x1t[:, 0, :].bitcast(F32), ALU.subtract),
                  waits=[got, x1t_free[0]], flag=sh.dve["split"])
        sh.bank_read[bank] = got
        yield TILES * 53
        bank2 = dense.turn()
        done = yield from matmul3(prog, sh.bank[bank2][:, :], [((a_hi[:, :], a_lo[:, :]), (x1t[:, 0, :], x1t[:, 1, :]))],
                       [a_ready, got, sh.bank_read[bank2]], sh.pe["dense"])
        x1t_free[0] = done
        q_hi, q_lo = stage[:, 0, :], stage[:, 1, :]
        hi = put("scalar", lambda e: e.activation(q_hi.bitcast(F32R), sh.bank[bank2][:, :], ACT.Copy),
                 waits=[done, stage_free[0]], flag=sh.act["evac"])
        staged = put("vector", lambda e: e.tensor_tensor(q_lo.bitcast(F32R), sh.bank[bank2][:, :], q_hi, ALU.subtract),
                     waits=[hi, stage_free[0]], flag=sh.dve["split"])
        sh.bank_read[bank2] = staged
        stage_free[0] = stacks.load(g, stage, staged)
        yield 3 * SEQ / 2.4

    p_free, p_ready = [None, None], {}
    y_ready, y_free, norm_last = {}, [None, None], [None]

    def sums(g, kt):
        u = (g * TILES + kt) % 2
        got = weighted_sum(sh, prog, pt[u], p_ready[(g, kt)],
                           lambda j: v[g % 2][:, kt, HEAD_DIM * j:HEAD_DIM * j + HEAD_DIM],
                           v_ready[g], kt, False, Y, sh.pe["pv"])
        if kt == TILES - 1:
            v_free[g % 2] = got
            raw_ready = put("scalar", lambda e: e.activation(y_raw[:, :], sh.bank[Y][:, :], ACT.Copy),
                            waits=[got, norm_last[0]], flag=sh.act["misc"])
            sh.bank_read[Y] = raw_ready
        yield PER * SEQ / 2.4
        got = weighted_sum(sh, prog, pt[u], p_ready[(g, kt)], lambda j: sh.ones[:, :], sh.const, kt, False, L,
                           sh.pe["pv"])
        p_free[u] = got
        if kt == TILES - 1:
            norm_jobs.append((g, raw_ready, put(
                "scalar", lambda e: e.activation(rowsum[:, :], sh.bank[L][:, :], ACT.Copy),
                waits=[got, norm_last[0]], flag=sh.act["misc"])))
            sh.bank_read[L] = norm_jobs[-1][2]
        yield PER * SEQ / 2.4

    norm_jobs = []

    def normalise():
        g, raw_ready, sum_ready = norm_jobs.pop()
        b, h = divmod(g, GROUPS)
        bank = dense.turn()
        for k in range(TILES):
            done = put("tensor", lambda e, k=k: e.transpose(
                sh.bank[bank][:, k * P:k * P + P], rowsum[:, k * P:k * P + P], sh.ident[:, :]),
                waits=[sum_ready, sh.bank_read[bank]], flag=sh.pe["small_t"])
        inv = put("vector", lambda e: e.reciprocal(
            recip[:, :], sh.bank[bank][:, :].rearrange("p (a r) -> p a r", r=HEAD_DIM)[:, :, 0]),
            waits=[done, norm_last[0]], flag=sh.dve["norm"])
        sh.bank_read[bank] = inv
        wide = put("vector", lambda e: e.tensor_copy(
            rowsum[:, :].rearrange("p (a r) -> p a r", r=HEAD_DIM),
            recip[:, :].unsqueeze(2).to_broadcast([P, TILES * PER, HEAD_DIM])), waits=[inv, done], flag=sh.dve["norm"])
        yield TILES * 53
        bank2 = dense.turn()
        for k in range(TILES):
            done = put("tensor", lambda e, k=k: e.transpose(
                sh.bank[bank2][:, k * P:k * P + P], rowsum[:, k * P:k * P + P], sh.ident[:, :]),
                waits=[wide, sh.bank_read[bank2]], flag=sh.pe["small_t"])
        y_ready[b] = put("vector", lambda e: e.tensor_tensor(
            y[b % 2][:, h, :], sh.bank[bank2][:, :], y_raw[:, :], ALU.mult),
            waits=[done, raw_ready, y_free[b % 2]], flag=sh.dve["norm"])
        norm_last[0] = sh.bank_read[bank2] = y_ready[b]
        yield TILES * 53

    def maxima(g, j):
        yield from head_max(sh, prog, stacks, g, j, False)
        if j == PER - 1:
            shift_rows(sh, prog, stacks, g, sh.maxed[g], dense.turn())
            yield 53

    x2_ready, x2_free, x2t_ready, x2t_free = {}, [None], {}, [None]

    def project_out(b, k):
        bank = dense.hold()
        x = x1[b % 2][:, k, :]
        biased = on_pool(sh, lambda e: e.tensor_tensor(x, x, bo[:, :], ALU.add), [small_ready, x1_used[b]],
                         sh.pool["mask"])
        for c in range(GROUPS):
            done = put("tensor", lambda e, c=c: e.matmul(
                sh.bank[bank][:, :], y[b % 2][:, c, k * P:k * P + P], wo[:, c, :],
                start=(c == 0), stop=(c == GROUPS - 1)),
                waits=[y_ready[b], wo_ready, sh.bank_read[bank]], flag=sh.pe["dense"])
            if c < GROUPS - 1:
                yield 4 * SEQ / 2.4
        if k == TILES - 1:
            y_free[b % 2] = done
        got = put("vector", lambda e: e.tensor_tensor(x, sh.bank[bank][:, :], x, ALU.add),
                  waits=[done, biased], flag=sh.dve["misc"])
        sh.bank_read[bank] = got
        dense.release(bank)
        ln2.statistics(k, x, got)
        yield 4 * SEQ / 2.4
        if k < TILES - 1:
            return
        ln2.scales()
        for i in range(TILES):
            got = ln2.apply(i, x2[:, i, :], x1[b % 2][:, i, :], [x2_free[0]])
            yield 1
        x2_ready[b] = x1_free[b % 2] = got

    def transpose_x2(b, c):
        bank = dense.turn()
        for k in range(TILES):
            done = put("tensor", lambda e, k=k: e.transpose(
                sh.bank[bank][:, k * P:k * P + P], x2[:, k, c * P:c * P + P], sh.ident[:, :]),
                waits=[x2_ready[b], sh.bank_read[bank]], flag=sh.pe["small_t"])
        hi = put("scalar", lambda e: e.activation(x2t_hi[:, c, :], sh.bank[bank][:, :], ACT.Copy),
                 waits=[done, x2t_free[0], *wall], flag=sh.act["evac"])
        x2t_ready[b] = put("vector", lambda e: e.tensor_tensor(
            x2t_lo[:, c, :], sh.bank[bank][:, :], x2t_hi[:, c, :].bitcast(F32), ALU.subtract),
            waits=[hi, x2t_free[0]], flag=sh.dve["split"])
        sh.bank_read[bank] = x2t_ready[b]
        yield TILES * 53

    gates_ready = {}
    gate_last, gate_used = [None], [None]

    def gates(b):
        bank = dense.hold()
        pairs = [((gate_hi[:, c, :], gate_lo[:, c, :]), (x2t_hi[:, c, :], x2t_lo[:, c, :])) for c in range(GROUPS)]
        done = yield from matmul3(prog, sh.bank[bank][0:EXPERTS, :], pairs, [gate_ready, x2t_ready[b], sh.bank_read[bank]],
                       sh.pe["dense"])
        got = put("scalar", lambda e: e.activation(lt[:, :], sh.bank[bank][0:EXPERTS, :], ACT.Copy),
                  waits=[done, gate_last[0], *wall], flag=sh.act["evac"])
        sh.bank_read[bank] = got
        dense.release(bank)
        bank2 = dense.turn()
        for k in range(TILES):
            done = put("tensor", lambda e, k=k: e.transpose(
                sh.bank[bank2][:, k * EXPERTS:(k + 1) * EXPERTS], lt[:, k * P:k * P + P],
                sh.ident[0:EXPERTS, 0:EXPERTS]),
                waits=[got, sh.bank_read[bank2]], flag=sh.pe["small_t"])
        dv = lambda f, *w: put("vector", f, waits=w, flag=sh.dve["ffn"])
        g = dv(lambda e: e.tensor_copy(lg[:, :, :].rearrange("p k x -> p (k x)"),
                                       sh.bank[bank2][:, 0:TILES * EXPERTS]), done, gate_used[0])
        sh.bank_read[bank2] = g
        col = lambda n: gs[n][:, :]
        wide = lambda ap, n=EXPERTS: ap.unsqueeze(2).to_broadcast([P, TILES, n])
        g = dv(lambda e: e.reduce_max(col("max"), lg[:, :, :], AX), g)
        g = dv(lambda e: e.tensor_tensor(ge[:, :, :], lg[:, :, :], wide(col("max")), ALU.subtract), g)
        x = put("scalar", lambda e: e.activation(ge[:, :, :], ge[:, :, :], ACT.Exp), waits=[g], flag=sh.act["misc"])
        g = dv(lambda e: e.reduce_sum(col("rest"), ge[:, :, :], AX), x)
        g = dv(lambda e: e.reciprocal(col("sum"), col("rest")), g)
        g = dv(lambda e: e.reduce_max(col("rest"), lg[:, :, 1:EXPERTS], AX), g)
        g = dv(lambda e: e.tensor_tensor(col("keep0"), lg[:, :, 0], col("rest"), ALU.is_ge), g)
        g = dv(lambda e: e.tensor_tensor(gb[:, :, :], lg[:, :, :], wide(lg[:, :, 1]), ALU.is_gt), g)
        g = dv(lambda e: e.tensor_tensor(gb[:, :, 0], lg[:, :, 0], lg[:, :, 1], ALU.is_ge), g)
        g = dv(lambda e: e.reduce_sum(col("rest"), gb[:, :, :], AX), g)
        g = dv(lambda e: e.tensor_scalar(col("keep1"), col("rest"), 1.0, 0.5, ALU.is_equal, ALU.mult), g)
        g = dv(lambda e: e.tensor_scalar(col("keep0"), col("keep0"), 0.5, None, ALU.mult), g)
        for i in (0, 1):
            g = dv(lambda e, i=i: e.tensor_tensor(col(f"w{i}"), ge[:, :, i], col("sum"), ALU.mult), g)
            g = dv(lambda e, i=i: e.tensor_tensor(col(f"w{i}"), col(f"w{i}"), col(f"keep{i}"), ALU.mult), g)
        gates_ready[b] = gate_last[0] = g
        yield 3 * SEQ / 2.4

    z_free, tanh_free = [None], [None, None]

    def expert(b, k, i):
        bank = dense.hold()
        pairs = [((x2t_hi[:, c, k * P:k * P + P], x2t_lo[:, c, k * P:k * P + P]),
                  (e_hi[:, i, c, :], e_lo[:, i, c, :])) for c in range(GROUPS)]
        done = yield from matmul3(prog, sh.bank[bank][:, :], pairs, [exp_ready, x2t_ready[b], sh.bank_read[bank]], sh.pe["dense"])
        if k == TILES - 1 and i == 1:
            x2t_free[0] = done
        z, r = zt[:, :], i
        g = put("vector", lambda e: e.tensor_tensor(z, sh.bank[bank][:, :], be[:, i, :], ALU.add),
                waits=[done, small_ready, z_free[0]], flag=sh.dve["ffn"])
        sh.bank_read[bank] = g
        dense.release(bank)
        a = put("scalar", lambda e: e.activation(tanh[r][:, :], z, ACT.Tanh, scale=0.5), waits=[g, tanh_free[r]],
                flag=sh.act["evac"])
        g = put("vector", lambda e: e.scalar_tensor_tensor(out=tanh[r][:, :], in0=tanh[r][:, :], scalar=1.0, in1=z,
                                                           op0=ALU.add, op1=ALU.mult), waits=[a], flag=sh.dve["ffn"])
        z_free[0] = g
        w = gs[f"w{i}"][:, k:k + 1]
        g = put("scalar", lambda e: e.activation(tanh[r][:, :], tanh[r][:, :], ACT.Copy, scale=w),
                waits=[g, gates_ready[b]], flag=sh.act["evac"])
        gate_used[0] = g
        tanh_free[r] = g = on_pool(sh, lambda e: e.tensor_tensor(x2[:, k, :], x2[:, k, :], tanh[r][:, :], ALU.add),
                                   [g, x2t_ready[b]], sh.pool["mask"])
        yield 3 * SEQ / 2.4
        if i == 1:
            ln3.statistics(k, x2[:, k, :], g)
        if i == 1 and k == TILES - 1:
            ln3.scales()
            for n in range(TILES):
                got = ln3.apply(n, x2[:, n, :], x2[:, n, :])
                yield 1
            x2_free[0] = put("sync", lambda e: e.dma_start(t["out"][b].rearrange("(k p) d -> p k d", p=P), x2[:, :, :]),
                             waits=[got], flag=out_stored, by=16)

    zt = sb("z", [P, DIM])

    def after(b, step):
        if 1 <= step <= 4:
            return project_out(b, step - 1), 3400
        if step in (5, 6):
            return chain(transpose_x2(b, 2 * step - 10), transpose_x2(b, 2 * step - 9)), 420
        if step == 7:
            return gates(b), 2560
        if step >= 8:
            return expert(b, (step - 8) // 2, step % 2), 2560
        return None, 0

    load_x1(0)
    put("tensor", lambda e: e.nop(), waits=[ones_ready])
    for g in range(2):
        load_values(g)
        keys(g)
        run(queries(g))
    for n in range(LEAD):
        run(maxima(*divmod(n, PER)))
    last = None
    for g in range(NG):
        b, h = divmod(g, GROUPS)
        for kt in range(TILES):
            step, ahead = h * TILES + kt, g * TILES + kt + LEAD
            u = (g * TILES + kt) % 2
            if b == 0 and h < 2:
                exp_ready = load_expert(h, kt)
            if kt == 1 and g >= 1 and g + 1 < NG:
                load_values(g + 1)
            if kt == 1 and g + 2 < NG:
                keys(g + 2)
            if step == 5 and b + 1 < BATCH:
                load_x1(b + 1)
            weave(
                (softmax_attention(sh, prog, stacks, g, kt, False, SCALE_CROSS, pt[u],
                                   p_free[u] if g or kt > 1 else wall[0], p_ready), 860),
                (sums(*last) if last else None, 1900),
                (normalise() if kt == 1 and g > 0 else None, 450),
                (maxima(*divmod(ahead, PER)) if ahead < NG * PER else None, 900),
                (queries(g + 2) if kt == 1 and g + 2 < NG else None, 900),
                after(b - 1, step) if b > 0 else (None, 0),
            )
            last = (g, kt)
    run(sums(*last))
    run(normalise())
    for step in range(1, 16):
        run(after(BATCH - 1, step)[0])
    sh.stores = [(out_stored, out_stored.count)]



SCRATCH = ("y_ar", "qa", "x1")


def kernel(x, ctx_1024, L0_attn_w_attn, L0_attn_b_attn, L0_attn_w_k2, L0_attn_b_k2, L0_attn_w_proj,
           L0_attn_b_proj, L0_xattn_Wv, L0_xattn_Wk, L0_xattn_Wq, L0_xattn_Wo, L0_xattn_bo,
           L0_ffn_gate_w, L0_ffn_w0, L0_ffn_b0, L0_ffn_w1, L0_ffn_b1):
    import concourse.bacc as bacc
    from concourse.bass_utils import run_bass_kernel_spmd

    def c(a):
        return np.ascontiguousarray(a)

    def columns(bias):
        return c(np.asarray(bias).reshape(-1, P).T)

    x, ctx_1024 = np.asarray(x), np.asarray(ctx_1024)
    arrays = {
        "x": c(x), "x_t": c(x.transpose(0, 2, 1)),
        "ctx": c(ctx_1024), "ctx_t": c(ctx_1024.transpose(0, 2, 1)),
        "w_attn_t": c(np.asarray(L0_attn_w_attn).T), "b_attn": columns(L0_attn_b_attn),
        "w_k2_t": c(np.asarray(L0_attn_w_k2).T), "b_k2": columns(L0_attn_b_k2),
        "w_proj_t": c(np.asarray(L0_attn_w_proj).T), "b_proj": c(np.asarray(L0_attn_b_proj)),
        "wv": c(L0_xattn_Wv), "wk": c(L0_xattn_Wk), "wq": c(L0_xattn_Wq),
        "wo_t": c(np.asarray(L0_xattn_Wo).T), "bo": c(np.asarray(L0_xattn_bo)),
        "gate_w": c(L0_ffn_gate_w),
        "w0_t": c(np.asarray(L0_ffn_w0).T), "b0": c(np.asarray(L0_ffn_b0)),
        "w1_t": c(np.asarray(L0_ffn_w1).T), "b1": c(np.asarray(L0_ffn_b1)),
    }
    nc = bacc.Bacc("TRN2", target_bir_lowering=False, num_devices=1)
    t = {n: nc.dram_tensor(f"in_{n}", list(a.shape), F32, kind="ExternalInput").ap() for n, a in arrays.items()}
    for n in SCRATCH:
        t[n] = nc.dram_tensor(f"scratch_{n}", [BATCH, SEQ, DIM], F32, kind="Internal").ap()
    t["out"] = nc.dram_tensor("out", [BATCH, SEQ, DIM], F32, kind="ExternalOutput").ap()
    build(nc, t)
    r = run_bass_kernel_spmd(nc, [{f"in_{n}": a for n, a in arrays.items()}], core_ids=[0])
    return r.results[0]["out"]
```

```python
from contextlib import ExitStack

import numpy as np

import concourse.bass as bass
from concourse import mybir

F32 = mybir.dt.float32
F32R = mybir.dt.float32r
BF16 = mybir.dt.bfloat16
ALU = mybir.AluOpType
ACT = mybir.ActivationFunctionType
AX = mybir.AxisListType.X

BATCH, SEQ, DIM, HEADS, EXPERTS = 8, 512, 512, 16, 8
P = 128
HEAD_DIM = DIM // HEADS
TILES = SEQ // P
GROUPS = DIM // P
PER = P // HEAD_DIM
NG = BATCH * GROUPS
STEPS = GROUPS * TILES
SCALE_SELF = float(HEAD_DIM) ** -0.5
SCALE_CROSS = float(DIM) ** -0.5
LEAK = 0.02
EPS = 1e-5
NEG = -1.0e30
LEAD = 5
PAUSE = 400
LAG = 2


class Flag:

    def __init__(self, sem):
        self.sem, self.count = sem, 0


class Program:

    ENGINES = ("tensor", "vector", "scalar", "gpsimd", "sync")

    def __init__(self, nc, ctx):
        self.nc, self.ctx = nc, ctx
        self.queue = {e: [] for e in self.ENGINES}
        self.waited = {e: {} for e in self.ENGINES}

    def flag(self, name):
        return Flag(self.ctx.enter_context(self.nc.semaphore(name)))

    def put(self, engine, build, waits=(), flag=None, by=1):
        seen, need = self.waited[engine], {}
        for w in waits:
            if w is not None and seen.get(w[0], 0) < w[1]:
                need[w[0]] = max(need.get(w[0], 0), w[1])
        seen.update(need)
        self.queue[engine].append((list(need.items()), build, flag, by))
        if flag is None:
            return None
        flag.count += by
        return (flag, flag.count)

    def emit(self, engine, eng):
        for need, build, flag, by in self.queue[engine]:
            for f, value in need:
                eng.wait_ge(f.sem, value)
            ins = build(eng)
            if flag is not None:
                ins.then_inc(flag.sem, by)


def build(nc, t):
    sems = ExitStack()
    with sems:
        prog = Program(nc, sems)
        shared = Shared(nc, sems, prog)
        with ExitStack() as ctx:
            self_softmax_phase(nc, ctx, prog, shared, t)
        with ExitStack() as both:
            cross = CrossWeights(nc, both, prog)
            for phase in (self_memory_phase, cross_phase):
                with ExitStack() as ctx:
                    phase(nc, ctx, prog, shared, t, cross)
        prog.put("sync", lambda e: e.nop(), waits=shared.stores)
        with nc.Block() as block:
            for engine in Program.ENGINES:
                bind(block, prog, engine)


def bind(block, prog, engine):
    def body(eng):
        prog.emit(engine, eng)

    {"tensor": block.tensor, "vector": block.vector, "scalar": block.scalar,
     "gpsimd": block.gpsimd, "sync": block.sync}[engine](body)


class Shared:

    def __init__(self, nc, ctx, prog):
        def sb(name, shape, dt=F32):
            return ctx.enter_context(nc.sbuf_tensor(name, shape, dt))

        self.bank = [ctx.enter_context(nc.psum_tensor(f"bank{i}", [P, 512], F32)) for i in range(8)]
        self.bank_read = [None] * 8
        self.ident = sb("ident", [P, P])
        self.identb = sb("identb", [P, P], BF16)
        self.future = sb("future", [P, P], BF16)
        self.ones = sb("ones", [P, HEAD_DIM])
        self.prog, self.pool_last = prog, None
        self.wall = []
        self.stores = []
        names = ("scores", "scores_t", "pv", "dense", "small_t")
        self.pe = {n: prog.flag(f"pe_{n}") for n in names}
        self.dve = {n: prog.flag(f"dve_{n}") for n in ("max", "split", "norm", "ln", "misc", "ffn")}
        self.act = {n: prog.flag(f"act_{n}") for n in ("exp", "evac", "misc", "ln")}
        self.pool = {n: prog.flag(f"pool_{n}") for n in ("mask", "const", "add")}

        const = self.pool["const"]
        on_pool(self, lambda e: e.memset(self.ident[:, :], 0.0), [], const)
        on_pool(self, lambda e: e.memset(self.identb[:, :], 0.0), [], const)
        on_pool(self, lambda e: e.memset(self.future[:, :], 0.0), [], const)
        on_pool(self, lambda e: e.memset(self.ones[:, :], 1.0), [], const)
        for m in (self.ident, self.identb):
            on_pool(self, lambda e, m=m: e.affine_select(
                out=m[:, :], in_=m[:, :], compare_op=ALU.not_equal, fill=1.0, base=0,
                pattern=[[-1, P]], channel_multiplier=1), [], const)
        self.const = on_pool(self, lambda e: e.affine_select(
            out=self.future[:, :], in_=self.future[:, :], compare_op=ALU.is_ge, fill=NEG, base=0,
            pattern=[[-1, P]], channel_multiplier=1), [], const)


def weave(*tasks):
    live = [[gen, 0.0, float(total)] for gen, total in tasks if gen is not None]
    while live:
        task = min(live, key=lambda x: x[1] / x[2])
        try:
            task[1] += next(task[0])
        except StopIteration:
            live.remove(task)


def chain(*gens):
    for gen in gens:
        yield from gen


class Background:

    def __init__(self, *gens):
        self.gen, self.ahead = chain(*gens), 0.0

    def share(self, ns):
        self.ahead -= ns
        while self.ahead < 0:
            cost = next(self.gen, None)
            if cost is None:
                return
            self.ahead += cost
            yield cost

    def rest(self):
        return self.gen


def run(gen):
    for _ in gen:
        pass


def on_pool(sh, build, waits, flag):
    sh.pool_last = sh.prog.put("gpsimd", build, waits=[*waits, sh.pool_last], flag=flag)
    return sh.pool_last


def split(prog, engine_hi, hi, lo, x, waits, flag, act_flag=None):
    if engine_hi == "scalar":
        got = prog.put("scalar", lambda e: e.activation(hi, x, ACT.Copy), waits=waits, flag=act_flag)
    else:
        got = prog.put("vector", lambda e: e.tensor_copy(hi, x), waits=waits, flag=flag)
    return prog.put("vector", lambda e: e.tensor_tensor(lo, x, hi.bitcast(F32), ALU.subtract),
                    waits=[*waits, got], flag=flag)


class Banks:

    def __init__(self, *numbers):
        self.idle = list(numbers)

    def turn(self):
        self.idle.append(self.idle.pop(0))
        return self.idle[-1]

    def hold(self):
        return self.idle.pop(0)

    def release(self, bank):
        self.idle.append(bank)


BANDS = (slice(0, 3, 2), slice(1, 3, 1), slice(0, 4, 3))


class Stacks:

    def __init__(self, nc, ctx, prog, name, operands, ring):
        self.prog, self.ring = prog, ring
        self.tile = [ctx.enter_context(nc.sbuf_tensor(f"{name}{r}", [P, operands, PER, SEQ], F32R))
                     for r in range(ring)]
        self.landed = [[prog.flag(f"{name}_landed{r}_{j}") for j in range(PER)] for r in range(ring)]
        self.shift_landed = [prog.flag(f"{name}_shift_landed{r}") for r in range(ring)]
        self.ready = {}
        self.read = [None] * ring

    def flags(self):
        return [*(f for slot in self.landed for f in slot), *self.shift_landed]

    def load(self, group, stage, staged):
        slot = group % self.ring
        dst = self.tile[slot]
        h = HEAD_DIM
        for j in range(PER):
            rows = slice(h * j, h * j + h)
            for band, operands in enumerate(BANDS):
                src = stage[rows, operands, :]
                out = dst[h * band:h * band + h, :, j, :].bitcast(F32)
                self.ready[(group, j)] = self.prog.put(
                    "sync", lambda e, src=src, out=out: e.dma_start(out, src),
                    waits=[staged, self.read[slot]], flag=self.landed[slot][j], by=16)
        return [self.ready[(group, j)] for j in range(PER)]


def softmax_attention(sh, prog, stacks, group, kt, causal, scale, ptiles, p_free, p_ready):
    slot = group % stacks.ring
    first = kt * P if causal else 0
    q0 = min(first, SEQ - 256)
    ptile = ptiles[(group * TILES + kt) % (LAG + 1)]
    for j in range(PER):
        b = 2 + sh.st_next
        sh.st_next ^= 1
        bank = sh.bank[b]
        kq = stacks.tile[slot]
        done = prog.put("tensor", lambda e, bank=bank, j=j: e.matmul(
            bank[:, 0:SEQ - q0], kq[0:98, 1, j, kt * P:kt * P + P], kq[0:98, 0, j, q0:SEQ],
            start=True, stop=True),
            waits=[stacks.ready[(group, j)], sh.shift_ready[group], sh.bank_read[b]], flag=sh.pe["scores_t"])
        if kt == TILES - 1 and j == PER - 1:
            stacks.read[slot] = done
        got = prog.put("scalar", lambda e, bank=bank, j=j: e.activation(
            ptile[:, j, 0:SEQ - first], bank[:, first - q0:SEQ - q0], ACT.Exp, scale=scale),
            waits=[done, *p_free, *sh.wall], flag=sh.act["exp"])
        sh.bank_read[b] = got
        if j < PER - 1:
            yield (SEQ - q0) / 2.4
    if causal:
        got = on_pool(sh, lambda e: e.affine_select(
            out=ptile[:, :, 0:P], in_=ptile[:, :, 0:P], compare_op=ALU.is_ge, fill=0.0, base=0,
            pattern=[[0, PER], [1, P]], channel_multiplier=-1), [got], sh.pool["mask"])
    p_ready[(group, kt)] = got
    yield (SEQ - q0) / 2.4
    if kt > 0:
        add_weights(sh, group, kt, causal, ptiles, got)


def add_weights(sh, group, kt, causal, ptiles, ready):
    added, new = sh.added, ptiles[(group * TILES + kt) % (LAG + 1)]
    first = kt * P if causal else 0
    out = added[:, :, first:SEQ]
    old, waits = out, [ready]
    if kt == 1:
        start = ptiles[group * TILES % (LAG + 1)]
        old, waits = start[:, :, first:SEQ], [ready, sh.added_read, *sh.wall]
        if causal:
            sh.copied = sh.prog.put("scalar", lambda e: e.activation(
                added[:, :, 0:P], start[:, :, 0:P], ACT.Copy), waits=waits, flag=sh.act["misc"])
    sh.add_done[(group, kt)] = on_pool(sh, lambda e: e.tensor_tensor(out, old, new[:, :, 0:SEQ - first], ALU.add),
                                       waits, sh.pool["add"])


def weighted_sum(sh, prog, ptile, ready, v, v_ready, kt, causal, out_bank, flag):
    first = kt * P if causal else 0
    for j in range(PER):
        rows = slice(HEAD_DIM * j, HEAD_DIM * j + HEAD_DIM)
        got = prog.put("tensor", lambda e, j=j, rows=rows: e.matmul(
            sh.bank[out_bank][rows, first:SEQ], v(j), ptile[:, j, 0:SEQ - first],
            start=(kt == 0), stop=(kt == TILES - 1), skip_group_check=True),
            waits=[ready, v_ready, sh.bank_read[out_bank] if kt == 0 else None], flag=flag)
    return got


def head_max(sh, prog, stacks, maxima_banks, group, j, causal):
    slot, m = group % stacks.ring, sh.negmax[group % 2]
    kq = stacks.tile[slot]
    for qt in range(TILES):
        b = maxima_banks.turn()
        bank = sh.bank[b]
        keys = P * (qt + 1) if causal else SEQ
        done = prog.put("tensor", lambda e, bank=bank, qt=qt, keys=keys: e.matmul(
            bank[:, 0:max(keys, 256)], kq[0:96, 0, j, qt * P:qt * P + P], kq[0:96, 1, j, 0:max(keys, 256)],
            start=True, stop=not causal, skip_group_check=True),
            waits=[stacks.ready[(group, j)], sh.bank_read[b]], flag=sh.pe["scores"])
        if causal:
            done = prog.put("tensor", lambda e, bank=bank, qt=qt: e.matmul(
                bank[:, qt * P:qt * P + P], sh.identb[:, :], sh.future[:, :],
                start=False, stop=True, skip_group_check=True),
                waits=[sh.const], flag=sh.pe["scores"])
        col = j * TILES + qt
        got = prog.put("vector", lambda e, bank=bank, keys=keys, col=col: e.reduce_max(
            m[:, col:col + 1], bank[:, 0:keys], AX, negate=True),
            waits=[done, sh.negmax_read[group % 2]], flag=sh.dve["max"])
        sh.bank_read[b] = got
        yield max(keys, 256) / 2.4 + (60 if causal else 0)
    sh.maxed[group] = got


def shift_rows(sh, prog, stacks, group, maxed, bank):
    m, hl, slot = sh.negmax[group % 2], sh.shift[group % 2], group % stacks.ring
    n = PER * TILES
    done = prog.put("tensor", lambda e: e.transpose(sh.bank[bank][0:n, 0:P], m[:, :], sh.ident[:, :]),
                    waits=[maxed, sh.const, sh.bank_read[bank]], flag=sh.pe["small_t"])
    sh.negmax_read[group % 2] = done
    x = sh.bank[bank][0:n, 0:P]
    free = sh.shift_free[group % 2]
    hi = prog.put("scalar", lambda e: e.activation(hl[:, 0, :].bitcast(F32R), x, ACT.Copy),
                  waits=[done, free], flag=sh.act["misc"])
    lo = prog.put("vector", lambda e: e.tensor_tensor(hl[:, 1, :].bitcast(F32R), x, hl[:, 0, :], ALU.subtract),
                  waits=[hi, free], flag=sh.dve["misc"])
    sh.bank_read[bank] = lo
    for part in range(2):
        row = stacks.tile[slot][96 + part:97 + part, 0, :, :].rearrange("p j (t q) -> p (j t) q", q=P)
        got = prog.put("sync", lambda e, row=row, part=part: e.dma_start(row.bitcast(F32), hl[:, part, :]),
                       waits=[hi, lo, stacks.read[slot]], flag=stacks.shift_landed[slot], by=16)
    sh.shift_free[group % 2] = got
    sh.shift_ready[group] = got


def evacuate(sh, prog, tile, bank, ready):
    sh.bank_read[bank] = prog.put("scalar", lambda e: e.activation(tile[:, :], sh.bank[bank][:, :], ACT.Copy),
                                  waits=[ready, sh.norm["last"]], flag=sh.act["misc"])
    return sh.bank_read[bank]


def total_sums(sh, prog, group, bank):
    added = sh.added
    for j in range(PER):
        rows = slice(HEAD_DIM * j, HEAD_DIM * j + HEAD_DIM)
        sh.added_read = prog.put("tensor", lambda e, j=j, rows=rows: e.matmul(
            sh.bank[bank][rows, :], sh.ones[:, :], added[:, j, :], start=True, stop=True, skip_group_check=True),
            waits=[sh.add_done[(group, TILES - 1)], sh.copied, sh.const, sh.bank_read[bank]], flag=sh.pe["pv"])
    sh.total_ready[group] = evacuate(sh, prog, sh.norm["total"], bank, sh.added_read)


def normalise(sh, prog, norm, dense, out, ready, out_free):
    raw, total, inverse = norm["raw"], norm["total"], norm["inverse"]

    def transposed(bank, wait):
        for k in range(TILES):
            done = prog.put("tensor", lambda e, k=k: e.transpose(
                sh.bank[bank][:, k * P:k * P + P], total[:, k * P:k * P + P], sh.ident[:, :]),
                waits=[wait, sh.bank_read[bank]], flag=sh.pe["small_t"])
        return done

    bank = dense.turn()
    done = transposed(bank, ready[1])
    inv = prog.put("vector", lambda e: e.reciprocal(
        inverse[:, :], sh.bank[bank][:, :].rearrange("p (a r) -> p a r", r=HEAD_DIM)[:, :, 0]),
        waits=[done, norm["last"]], flag=sh.dve["norm"])
    sh.bank_read[bank] = inv
    wide = prog.put("vector", lambda e: e.tensor_copy(
        total[:, :].rearrange("p (a r) -> p a r", r=HEAD_DIM),
        inverse[:, :].unsqueeze(2).to_broadcast([P, TILES * PER, HEAD_DIM])), waits=[inv, done], flag=sh.dve["norm"])
    yield TILES * 53
    bank2 = dense.turn()
    done = transposed(bank2, wide)
    norm["last"] = sh.bank_read[bank2] = prog.put("vector", lambda e: e.tensor_tensor(
        out, sh.bank[bank2][:, :], raw[:, :], ALU.mult),
        waits=[done, ready[0], out_free], flag=sh.dve["norm"])
    yield TILES * 53


def open_softmax(nc, ctx, sh, stacks, name):
    sb = lambda n, shape: ctx.enter_context(nc.sbuf_tensor(f"{name}_{n}", shape, F32))
    sh.negmax = [sb(f"negmax{i}", [P, PER * TILES]) for i in range(2)]
    sh.shift = [sb(f"shift{i}", [PER * TILES, 2, P]) for i in range(2)]
    sh.added, sh.added_read, sh.add_done, sh.total_ready = sb("added", [P, PER, SEQ]), None, {}, {}
    sh.copied = None
    sh.negmax_read, sh.shift_free, sh.shift_ready = [None] * 2, [None] * 2, {}
    sh.st_next = 0
    sh.norm = {"raw": sb("y_raw", [P, SEQ]), "total": sb("row_sum", [P, SEQ]),
               "inverse": sb("inverse", [P, TILES * PER]), "last": None}
    sh.maxed = {}
    for r in range(stacks.ring):
        got = on_pool(sh, lambda e, r=r: e.memset(stacks.tile[r][96:128, 1, :, :].bitcast(F32), 1.0),
                      sh.wall, sh.pool["const"])
    return got


class LayerNorm:

    def __init__(self, nc, ctx, sh, prog, name):
        sb = lambda n, s: ctx.enter_context(nc.sbuf_tensor(f"{name}_{n}", s, F32))
        self.sh, self.prog = sh, prog
        self.stats, self.mv = sb("stats", [P, TILES, 6]), sb("mv", [P, TILES, 2])
        self.rstd, self.shift, self.power = sb("rstd", [P, TILES]), sb("shift", [P, TILES]), sb("power", [P, TILES])
        self.power_ready = on_pool(sh, lambda e: e.memset(self.power[:, :], -0.5), sh.wall, sh.pool["const"])
        self.applied = None

    def statistics(self, k, r, ready):
        put, flag = self.prog.put, self.sh.dve["ln"]
        g = put("vector", lambda e: e.bn_stats(self.stats[:, k, :], r), waits=[ready, self.applied, *self.sh.wall],
                flag=flag)
        self.last = put("vector", lambda e: e.bn_aggr(self.mv[:, k, :], self.stats[:, k, :]), waits=[g], flag=flag)

    def scales(self):
        put, flag = self.prog.put, self.sh.dve["ln"]
        g = put("vector", lambda e: e.tensor_scalar(self.rstd[:, :], self.mv[:, :, 1], EPS, None, ALU.add),
                waits=[self.last], flag=flag)
        g = on_pool(self.sh, lambda e: e.tensor_tensor(self.rstd[:, :], self.rstd[:, :], self.power[:, :], ALU.pow),
                    [g], self.sh.pool["mask"])
        yield 2 * PAUSE
        self.ready = put("vector", lambda e: e.scalar_tensor_tensor(
            out=self.shift[:, :], in0=self.mv[:, :, 0], scalar=-1.0, in1=self.rstd[:, :],
            op0=ALU.mult, op1=ALU.mult), waits=[g], flag=flag)

    def apply(self, k, out, r, waits=()):
        self.applied = self.prog.put("scalar", lambda e: e.activation(
            out, r, ACT.Identity, bias=self.shift[:, k:k + 1], scale=self.rstd[:, k:k + 1]),
            waits=[self.ready, *waits], flag=self.sh.act["ln"])
        return self.applied


def matmul3(prog, out, pairs, waits, flag, start=True, stop=True):
    passes = [(a[x], b[y]) for a, b in pairs for x, y in ((0, 0), (1, 0), (0, 1))]
    for i, (a, b) in enumerate(passes):
        got = prog.put("tensor", lambda e, a=a, b=b, i=i: e.matmul(
            out, a, b, start=start and i == 0, stop=stop and i == len(passes) - 1),
            waits=waits, flag=flag if i == len(passes) - 1 else None)
        if i % 3 == 2 and i < len(passes) - 1:
            yield 3 * SEQ / 2.4
    return got


def load_split_weights(prog, sh, raw, raw_flags, jobs, free):
    got = {}
    for i, (key, hi, lo, src) in enumerate(jobs):
        r = i % len(raw)
        n = hi.shape[-1]
        tile = raw[r][:, 0:n]
        landed = prog.put("sync", lambda e, tile=tile, src=src: e.dma_start(tile, src),
                          waits=[free[r], *sh.wall], flag=raw_flags[r], by=16)
        got[key] = split(prog, "vector", hi, lo, tile, [landed, *sh.wall], sh.dve["split"])
        free[r] = got[key]
    return got, free



def self_softmax_phase(nc, ctx, prog, sh, t):
    sb = lambda name, shape, dt=F32: ctx.enter_context(nc.sbuf_tensor(name, shape, dt))
    put = prog.put
    Q, K, K2 = range(3)
    w_hi, w_lo = sb("w_hi", [P, GROUPS, 3 * DIM], F32R), sb("w_lo", [P, GROUPS, 3 * DIM], F32R)
    bias = sb("bias", [P, 3 * GROUPS])
    xt_hi = [sb(f"xt_hi{i}", [P, GROUPS, SEQ], F32R) for i in range(2)]
    xt_lo = [sb(f"xt_lo{i}", [P, GROUPS, SEQ], F32R) for i in range(2)]
    raw = [sb(f"raw{i}", [P, SEQ]) for i in range(GROUPS)]
    raw_landed = [prog.flag(f"raw_landed{i}") for i in range(GROUPS)]
    stage = [sb(f"stage{i}", [P, 4, SEQ]) for i in range(2)]
    memory = sb("memory", [P, 4, SEQ])
    stacks = Stacks(nc, ctx, prog, "qk", 2, 3)
    pt = [sb(f"pt{i}", [P, PER, SEQ]) for i in range(LAG + 1)]
    v = [sb(f"v{i}", [P, TILES, P]) for i in range(2)]
    v_landed = [prog.flag(f"v_landed{i}") for i in range(2)]
    y_ar = [sb(f"y_ar{i}", [P, SEQ]) for i in range(2)]
    y_stored = [prog.flag(f"y_stored{i}") for i in range(2)]
    memory_stored = prog.flag("memory_stored")
    bias_landed = prog.flag("bqk_landed")
    ones_ready = open_softmax(nc, ctx, sh, stacks, "self")
    maxima_banks, Y, dense = Banks(0, 1, 5), 4, Banks(6, 7)

    put("sync", lambda e: e.dma_start(bias[:, 0:2 * GROUPS], t["b_attn"]), flag=bias_landed, by=16)
    landed = put("sync", lambda e: e.dma_start(bias[:, 2 * GROUPS:], t["b_k2"]), flag=bias_landed, by=16)
    kscale = 0.5 * LEAK * SCALE_SELF
    bias_ready = put("vector", lambda e: e.tensor_scalar(bias[:, 2 * GROUPS:], bias[:, 2 * GROUPS:], kscale, None,
                                                         ALU.mult), waits=[landed], flag=sh.dve["misc"])
    jobs = [((w, c), w_hi[:, c, w * DIM:(w + 1) * DIM], w_lo[:, c, w * DIM:(w + 1) * DIM],
             t["w_k2_t"][c * P:c * P + P, :] if w == K2 else t["w_attn_t"][c * P:c * P + P, w * DIM:(w + 1) * DIM])
            for w in (Q, K, K2) for c in range(GROUPS)]
    xt_ready, xt_landed, xt_free = {}, {}, [None, None]

    def fetch_xt(b, c):
        xt_landed[c] = put("sync", lambda e: e.dma_start(raw[c][:, :], t["x_t"][b, c * P:c * P + P, :]),
                           waits=[raw_free[c]], flag=raw_landed[c], by=16)

    def split_xt(b, c):
        xt_ready[b] = split(prog, "vector", xt_hi[b % 2][:, c, :], xt_lo[b % 2][:, c, :], raw[c][:, :],
                            [xt_landed[c], xt_free[b % 2]], sh.dve["split"])
        raw_free[c] = xt_ready[b]

    raw_free = [None] * GROUPS
    for c in range(GROUPS):
        fetch_xt(0, c)
        split_xt(0, c)
    w_ready, raw_free = load_split_weights(prog, sh, raw, raw_landed, jobs, raw_free)

    stage_free, memory_free = [(), ()], [None]

    def project(g, which):
        b, h = divmod(g, GROUPS)
        bank, st = dense.hold(), stage[g % 2]
        col = which * DIM + h * P
        pairs = [((w_hi[:, c, col:col + P], w_lo[:, c, col:col + P]),
                  (xt_hi[b % 2][:, c, :], xt_lo[b % 2][:, c, :])) for c in range(GROUPS)]
        done = yield from matmul3(prog, sh.bank[bank][:, :], pairs,
                                  [w_ready[(which, GROUPS - 1)], xt_ready[b], sh.bank_read[bank]], sh.pe["dense"])
        if which == K2 and h == GROUPS - 1:
            xt_free[b % 2] = done
        column = bias[:, which * GROUPS + h:which * GROUPS + h + 1]
        q_hi, q_lo, k_hi, k_lo = (memory[:, i, :] for i in range(4))
        if which == K2:
            th = put("scalar", lambda e: e.activation(k_lo, sh.bank[bank][:, :], ACT.Tanh, bias=column, scale=kscale),
                     waits=[done, bias_ready, memory_free[0]], flag=sh.act["evac"])
            sh.bank_read[bank] = th
            dense.release(bank)
            yield PAUSE
            hi = put("vector", lambda e: e.tensor_scalar(k_hi.bitcast(F32R), k_lo, 1.0, None, ALU.add),
                     waits=[th], flag=sh.dve["split"])
            staged = put("vector", lambda e: e.scalar_tensor_tensor(
                out=k_lo.bitcast(F32R), in0=k_lo, scalar=1.0, in1=k_hi, op0=ALU.add, op1=ALU.subtract),
                waits=[hi], flag=sh.dve["split"])
            memory_free[0] = put("sync", lambda e: e.dma_start(t["memory"][b, h], memory[:, :, :]), waits=[staged],
                                 flag=memory_stored, by=16)
            yield 3 * SEQ / 2.4
            return
        hi, lo = st[:, 2 * which, :], st[:, 2 * which + 1, :]
        x = put("scalar", lambda e: e.activation(lo, sh.bank[bank][:, :], ACT.Identity, bias=column),
                waits=[done, bias_ready, *stage_free[g % 2]], flag=sh.act["evac"])
        sh.bank_read[bank] = x
        dense.release(bank)
        yield PAUSE
        if which == Q:
            got = put("vector", lambda e: e.scalar_tensor_tensor(
                out=q_lo, in0=lo, scalar=LEAK, in1=lo, op0=ALU.mult, op1=ALU.min),
                waits=[x, memory_free[0]], flag=sh.dve["misc"])
            split(prog, "vector", q_hi.bitcast(F32R), q_lo.bitcast(F32R), q_lo, [got], sh.dve["split"])
        staged = split(prog, "vector", hi.bitcast(F32R), lo.bitcast(F32R), lo, [x], sh.dve["split"])
        if which == K:
            stage_free[g % 2] = stacks.load(g, st, staged)
        yield 3 * SEQ / 2.4

    v_ready, v_free = {}, [None, None]

    def load_v(g):
        b, h = divmod(g, GROUPS)
        src = t["x"][b].rearrange("(k p) d -> p k d", p=P)[:, :, h * P:h * P + P]
        v_ready[g] = put("sync", lambda e: e.dma_start(v[g % 2][:, :, :], src), waits=[v_free[g % 2]],
                         flag=v_landed[g % 2], by=16)

    p_free, p_ready = [()] * (LAG + 1), {}
    y_free = [None, None]

    y_raw_ready = {}

    def sums(g, kt):
        u = (g * TILES + kt) % (LAG + 1)
        rows = weighted_sum(sh, prog, pt[u], p_ready[(g, kt)],
                            lambda j: v[g % 2][:, kt, HEAD_DIM * j:HEAD_DIM * j + HEAD_DIM],
                            v_ready[g], kt, True, Y, sh.pe["pv"])
        p_free[u] = (rows, sh.add_done[(g, max(kt, 1))], sh.copied)
        if kt == TILES - 1:
            v_free[g % 2] = rows
            y_raw_ready[g] = evacuate(sh, prog, sh.norm["raw"], Y, rows)
        yield 4 * (SEQ - kt * P) / 2.4

    def outputs(g):
        b, h = divmod(g, GROUPS)
        yield from normalise(sh, prog, sh.norm, dense, y_ar[g % 2][:, :], (y_raw_ready[g], sh.total_ready[g]),
                             y_free[g % 2])
        y_free[g % 2] = put("sync", lambda e: e.dma_start(t["y_ar"][b, h * P:h * P + P, :], y_ar[g % 2][:, :]),
                            waits=[sh.norm["last"]], flag=y_stored[g % 2], by=16)

    def maxima(g, j):
        yield from head_max(sh, prog, stacks, maxima_banks, g, j, True)
        if j == PER - 1:
            yield PAUSE
            shift_rows(sh, prog, stacks, g, sh.maxed[g], dense.turn())
            yield 53

    projections = Background(*(project(g, which) for g in range(NG) for which in (Q, K, K2)))
    quarter = 3 * (3 * GROUPS * SEQ / 2.4 + PAUSE) / TILES
    load_v(0)
    load_v(1)
    run(projections.share(4 * quarter))
    weave((projections.share(6 * quarter), 6 * quarter),
          (chain(*(maxima(*divmod(n, PER)) for n in range(LEAD))), 5500))
    put("tensor", lambda e: e.nop(), waits=[ones_ready])
    pending = []
    for g in range(NG):
        for kt in range(TILES):
            u = (g * TILES + kt) % (LAG + 1)
            ahead = g * TILES + kt + LEAD
            b, step = g // GROUPS, g % GROUPS * TILES + kt
            if b + 1 < BATCH:
                if step < GROUPS:
                    fetch_xt(b + 1, step)
                if 2 <= step < 2 + GROUPS:
                    split_xt(b + 1, step - 2)
            if kt == LAG and 1 <= g and g + 1 < NG:
                load_v(g + 1)
            weave(
                (softmax_attention(sh, prog, stacks, g, kt, True, SCALE_SELF, pt, p_free[u], p_ready), 900),
                (sums(*pending.pop(0)) if len(pending) == LAG else None, 900),
                (normal.share(225) if kt >= 2 and g > 0 else None, 225),
                (maxima(*divmod(ahead, PER)) if ahead < NG * PER else None, 900),
                (projections.share(quarter), quarter),
            )
            if kt == 0 and g > 0:
                total_sums(sh, prog, g - 1, dense.turn())
                normal = Background(outputs(g - 1))
            pending.append((g, kt))
    for job in pending:
        run(sums(*job))
    total_sums(sh, prog, NG - 1, dense.turn())
    run(outputs(NG - 1))
    tail = [*y_free, memory_free[0]]
    sh.wall = [(f, f.count) for f in (*sh.pe.values(), *sh.dve.values(), *sh.act.values(), *sh.pool.values(),
                                      *stacks.flags(), *raw_landed, *v_landed) if f.count] + tail



class CrossWeights:

    def __init__(self, nc, ctx, prog):
        sb = lambda name, shape, dt=F32: ctx.enter_context(nc.sbuf_tensor(name, shape, dt))
        self.wo = sb("wo", [P, GROUPS, DIM])
        self.a_hi, self.a_lo = sb("a_hi", [P, P], F32R), sb("a_lo", [P, P], F32R)
        self.e_hi, self.e_lo = (sb(f"exp_{part}", [P, 2, GROUPS, DIM], F32R) for part in ("hi", "lo"))
        self.gate_hi, self.gate_lo = (sb(f"gate_{part}", [P, GROUPS, EXPERTS], F32R) for part in ("hi", "lo"))
        self.gate_raw = sb("gate_raw", [P, GROUPS, EXPERTS])
        self.bo, self.be = sb("bo", [P, DIM]), sb("bias_exp", [P, 2, DIM])
        self.small = prog.flag("c_small_landed")

    def prepare(self, prog, sh, t, raw, raw_landed, raw_free, fold, dense):
        put, small = prog.put, self.small
        zero = on_pool(sh, lambda e: e.memset(fold[:, :, :], 0.0), sh.wall, sh.pool["const"])
        for i, name in enumerate(("wq", "wk", "wv")):
            for j in range(PER):
                d = slice(HEAD_DIM * j, HEAD_DIM * j + HEAD_DIM)
                put("sync", lambda e, i=i, d=d, name=name: e.dma_start(fold[d, i, d], t[name]),
                    waits=[zero, *sh.wall], flag=small, by=16)
                yield PAUSE
        for out, name in ((self.bo[:, :], "bo"), (self.be[:, 0, :], "b0"), (self.be[:, 1, :], "b1")):
            put("sync", lambda e, out=out, name=name: e.dma_start(out, t[name].partition_broadcast(P)),
                waits=sh.wall, flag=small, by=16)
            yield PAUSE
        self.small_ready = put("sync", lambda e: e.dma_start(
            self.gate_raw[:, :, :], t["gate_w"].rearrange("(c p) n -> p c n", p=P)), flag=small, by=16)
        yield 10 * PAUSE
        bank = dense.turn()
        done = put("tensor", lambda e, bank=bank: e.matmul(sh.bank[bank][:, 0:P], fold[:, 0, :], fold[:, 1, :],
                                                           start=True, stop=True),
                   waits=[self.small_ready, sh.bank_read[bank]], flag=sh.pe["dense"])
        self.a_ready = split(prog, "vector", self.a_hi[:, :], self.a_lo[:, :], sh.bank[bank][:, 0:P], [done, *sh.wall],
                             sh.dve["split"])
        sh.bank_read[bank] = self.a_ready
        self.gate_ready = split(prog, "vector", self.gate_hi[:, :, :], self.gate_lo[:, :, :], self.gate_raw[:, :, :],
                                [self.small_ready], sh.dve["split"])
        yield PAUSE

        def fetch(i, src):
            r = i % len(raw)
            return r, put("sync", lambda e: e.dma_start(raw[r][:, :], src), waits=[raw_free[r]], flag=raw_landed[r],
                          by=16)

        for c in range(GROUPS):
            r, landed = fetch(c, t["wo_t"][c * P:c * P + P, :])
            yield 10 * PAUSE
            bank = dense.turn()
            done = put("tensor", lambda e, bank=bank, r=r: e.matmul(
                sh.bank[bank][:, :], fold[:, 2, :], raw[r][:, :], start=True, stop=True),
                waits=[landed, sh.bank_read[bank]], flag=sh.pe["dense"])
            raw_free[r] = done
            self.wo_ready = put("vector", lambda e, bank=bank, c=c: e.tensor_copy(
                self.wo[:, c, :], sh.bank[bank][:, :]), waits=[done], flag=sh.dve["misc"])
            sh.bank_read[bank] = self.wo_ready
            yield 4 * SEQ / 2.4
        for i in range(2):
            for c in range(GROUPS):
                r, landed = fetch(c, t[f"w{i}_t"][c * P:c * P + P, :])
                yield 10 * PAUSE
                self.exp_ready = raw_free[r] = split(prog, "vector", self.e_hi[:, i, c, :], self.e_lo[:, i, c, :],
                                                     raw[r][:, :], [landed], sh.dve["split"])
                yield PAUSE



def self_memory_phase(nc, ctx, prog, sh, t, cross):
    sb = lambda name, shape, dt=F32: ctx.enter_context(nc.sbuf_tensor(name, shape, dt))
    put = prog.put
    wp_hi, wp_lo = sb("wproj_hi", [P, GROUPS, DIM], F32R), sb("wproj_lo", [P, GROUPS, DIM], F32R)
    raw = [sb(f"mraw{i}", [P, SEQ]) for i in range(2)]
    raw_landed = [prog.flag(f"mraw_landed{i}") for i in range(2)]
    bproj = sb("bproj", [P, DIM])
    RING = 3
    stack = [sb(f"ma{r}", [P, 2, PER, SEQ], F32R) for r in range(RING)]
    stack_landed = [prog.flag(f"ma_landed{r}") for r in range(RING)]
    mt = [sb(f"mt{i}", [P, PER, SEQ]) for i in range(LAG + 1)]
    y_ar = [sb(f"my_ar{i}", [P, SEQ]) for i in range(3)]
    xs = [sb(f"x_next{i}", [P, TILES, P]) for i in range(2)]
    ev = [sb(f"e{i}", [P, TILES, P]) for i in range(2)]
    y_sum = sb("y_sum", [P, SEQ])
    y_hi, y_lo = ([sb(f"y_{part}{i}", [P, GROUPS, SEQ], F32R) for i in range(2)] for part in ("hi", "lo"))
    xr = sb("mxr", [P, TILES, DIM])
    fold = sb("fold", [P, 3, P])
    xr_ready = [None]
    ln = LayerNorm(nc, ctx, sh, prog, "ln1")
    small = prog.flag("m_small_landed")
    y_landed = [prog.flag(f"m_y_landed{i}") for i in range(3)]
    xs_landed = [prog.flag(f"m_xs_landed{i}") for i in range(2)]
    xr_landed, x1_stored = prog.flag("m_xr_landed"), prog.flag("x1_stored")
    Y2, dense = 4, Banks(5, 6, 7)

    wall = sh.wall
    small_ready = put("sync", lambda e: e.dma_start(bproj[:, :], t["b_proj"].partition_broadcast(P)), waits=wall,
                      flag=small, by=16)
    for i in range(2):
        xs_zero = on_pool(sh, lambda e, i=i: e.memset(xs[i][:, :, :], 0.0), wall, sh.pool["const"])
    stack_ready, stack_read = {}, [None] * RING

    def load_stack(g):
        b, h = divmod(g, GROUPS)
        r = g % RING
        src = t["memory"][b, h].rearrange("(j p) o q -> p o j q", p=HEAD_DIM)
        for band, operands in enumerate(BANDS):
            rows = slice(HEAD_DIM * band, HEAD_DIM * band + HEAD_DIM)
            for o in range(2):
                one = range(4)[operands][o]
                stack_ready[g] = put("sync", lambda e, rows=rows, o=o, one=one: e.dma_start(
                    stack[r][rows, o, :, :].bitcast(F32), src[:, one, :, :]),
                    waits=[stack_read[r], *wall], flag=stack_landed[r], by=16)

    y_ready, y_free, xs_ready, xs_free = {}, [None] * 3, {}, [None] * 2

    def load_y(g):
        b, h = divmod(g, GROUPS)
        ry = g % 3
        y_ready[g] = put("sync", lambda e: e.dma_start(y_ar[ry][:, :], t["y_ar"][b, h * P:h * P + P, :]),
                         waits=[y_free[ry], *wall], flag=y_landed[ry], by=16)
        r = g % 2
        cols = slice(h * P, h * P + P)
        body = t["x"][b, 1:1 + (TILES - 1) * P, cols].rearrange("(k p) d -> p k d", p=P)
        put("sync", lambda e: e.dma_start(xs[r][:, 0:TILES - 1, :], body),
            waits=[xs_free[r], xs_zero], flag=xs_landed[r], by=16)
        rest = t["x"][b, 1 + (TILES - 1) * P:SEQ, cols]
        xs_ready[g] = put("sync", lambda e: e.dma_start(xs[r][0:P - 1, TILES - 1, :], rest),
                          waits=[xs_free[r]], flag=xs_landed[r], by=16)

    e_ready, e_free = {}, [None] * 2

    def values(g):
        bank = dense.turn()
        for k in range(TILES):
            done = put("tensor", lambda e, k=k: e.transpose(
                sh.bank[bank][:, k * P:k * P + P], y_ar[g % 3][:, k * P:k * P + P], sh.ident[:, :]),
                waits=[y_ready[g], sh.bank_read[bank]], flag=sh.pe["small_t"])
        e_ready[g] = put("vector", lambda e: e.tensor_tensor(
            ev[g % 2][:, :, :].rearrange("p k d -> p (k d)"), xs[g % 2][:, :, :].rearrange("p k d -> p (k d)"),
            sh.bank[bank][:, :], ALU.subtract),
            waits=[done, xs_ready[g], e_free[g % 2], *wall], flag=sh.dve["misc"])
        sh.bank_read[bank] = xs_free[g % 2] = e_ready[g]
        yield TILES * 53

    m_ready, m_free = {}, [None] * (LAG + 1)
    st_next = [0]

    def memory_scores(g, kt):
        u, first = (g * TILES + kt) % (LAG + 1), kt * P
        q0 = min(first, SEQ - 256)
        kq = stack[g % RING]
        for j in range(PER):
            b = st_next[0]
            st_next[0] = (b + 1) % 4
            done = put("tensor", lambda e, b=b, j=j: e.matmul(
                sh.bank[b][:, 0:SEQ - q0], kq[0:96, 1, j, first:first + P], kq[0:96, 0, j, q0:SEQ],
                start=True, stop=True),
                waits=[stack_ready[g], sh.bank_read[b]], flag=sh.pe["scores_t"])
            got = put("scalar", lambda e, b=b, j=j: e.activation(
                mt[u][:, j, 0:SEQ - first], sh.bank[b][:, first - q0:SEQ - q0], ACT.Copy, scale=0.5 * SCALE_SELF),
                waits=[done, m_free[u], *wall], flag=sh.act["exp"])
            sh.bank_read[b] = got
            if j < PER - 1:
                yield (SEQ - q0) / 2.4
        if kt == TILES - 1:
            stack_read[g % RING] = done
        m_ready[(g, kt)] = on_pool(sh, lambda e: e.affine_select(
            out=mt[u][:, :, 0:P], in_=mt[u][:, :, 0:P], compare_op=ALU.is_ge, fill=0.0, base=-1,
            pattern=[[0, PER], [1, P]], channel_multiplier=-1), [got], sh.pool["mask"])
        yield (SEQ - q0) / 2.4

    ysum_ready, ysum_free = {}, [None] * 2

    def memory_sums(g, kt):
        yield PAUSE
        b, h = divmod(g, GROUPS)
        u = (g * TILES + kt) % (LAG + 1)
        got = weighted_sum(sh, prog, mt[u], m_ready[(g, kt)],
                           lambda j: ev[g % 2][:, kt, HEAD_DIM * j:HEAD_DIM * j + HEAD_DIM],
                           e_ready[g], kt, True, Y2, sh.pe["pv"])
        m_free[u] = got
        yield PER * (SEQ - kt * P) / 2.4
        if kt < TILES - 1:
            return
        e_free[g % 2] = got
        n = put("vector", lambda e: e.tensor_tensor(y_sum[:, :], sh.bank[Y2][:, :], y_ar[g % 3][:, :], ALU.add),
                waits=[got, y_ready[g], ysum_ready.get("last"), *wall], flag=sh.dve["norm"])
        sh.bank_read[Y2] = y_free[g % 3] = n
        ysum_ready[b] = ysum_ready["last"] = split(
            prog, "vector", y_hi[b % 2][:, h, :], y_lo[b % 2][:, h, :], y_sum[:, :],
            [n, ysum_free[b % 2], *wall], sh.dve["split"])

    xr_free = [None]

    def fetch_residual(b):
        xr_ready[0] = put("sync", lambda e: e.dma_start(xr[:, :, :], t["x"][b].rearrange("(k p) d -> p k d", p=P)),
                          waits=[xr_free[0], *wall], flag=xr_landed, by=16)

    def project_out(b, k):
        bank = dense.hold()
        x = xr[:, k, :]
        pairs = [((y_hi[b % 2][:, c, k * P:k * P + P], y_lo[b % 2][:, c, k * P:k * P + P]),
                  (wp_hi[:, c, :], wp_lo[:, c, :])) for c in range(GROUPS)]
        done = yield from matmul3(prog, sh.bank[bank][:, :], pairs, [ysum_ready[b], wp_ready, sh.bank_read[bank]],
                                  sh.pe["dense"])
        if k == TILES - 1:
            ysum_free[b % 2] = done
        got = put("vector", lambda e: e.scalar_tensor_tensor(
            out=x, in0=bproj[:, :], scalar=2.0, in1=x, op0=ALU.mult, op1=ALU.add),
            waits=[xr_ready[0], small_ready], flag=sh.dve["misc"])
        got = put("vector", lambda e: e.tensor_tensor(x, sh.bank[bank][:, :], x, ALU.add),
                  waits=[done, got], flag=sh.dve["misc"])
        sh.bank_read[bank] = got
        dense.release(bank)
        ln.statistics(k, x, got)
        yield 3 * SEQ / 2.4
        if k < TILES - 1:
            return
        yield from ln.scales()
        yield PAUSE
        for i in range(TILES):
            got = ln.apply(i, xr[:, i, :], xr[:, i, :])
            yield 1
        xr_free[0] = put("sync", lambda e: e.dma_start(t["x1"][b].rearrange("(k p) d -> p k d", p=P), xr[:, :, :]),
                         waits=[got], flag=x1_stored, by=16)

    SETUP_SHARE = 500
    OUTPUT_SHARE = (TILES * GROUPS * 3 * SEQ / 2.4 + 3 * PAUSE + TILES) / (STEPS - 2)
    load_y(0)
    load_stack(0)
    load_stack(1)
    run(values(0))
    jobs = [(c, wp_hi[:, c, :], wp_lo[:, c, :], t["w_proj_t"][c * P:c * P + P, :]) for c in range(GROUPS)]
    w_ready, raw_free = load_split_weights(prog, sh, raw, raw_landed, jobs, [None, None])
    wp_ready = w_ready[GROUPS - 1]
    setup = Background(cross.prepare(prog, sh, t, raw, raw_landed, raw_free, fold, dense))
    pending = []
    for g in range(NG):
        b, h = divmod(g, GROUPS)
        for kt in range(TILES):
            if kt == 0 and g + 1 < NG:
                load_y(g + 1)
            if kt == 0 and g + 2 < NG:
                load_stack(g + 2)
            step = h * TILES + kt
            if step == 1 and b > 0:
                fetch_residual(b - 1)
                outputs = Background(*(project_out(b - 1, k) for k in range(TILES)))
            weave(
                (memory_scores(g, kt), 700),
                (memory_sums(*pending.pop(0)) if len(pending) == LAG else None, 1300),
                (values(g + 1) if kt == 3 and g + 1 < NG else None, 200),
                (None if step < 2 or b == 0 else outputs.rest() if step == STEPS - 1 else
                 outputs.share(OUTPUT_SHARE), OUTPUT_SHARE),
                (setup.share(SETUP_SHARE) if b > 0 else None, SETUP_SHARE),
            )
            pending.append((g, kt))
    for job in pending:
        run(memory_sums(*job))
    run(setup.rest())
    fetch_residual(BATCH - 1)
    for k in range(TILES):
        run(project_out(BATCH - 1, k))
    sh.wall = [(f, f.count) for f in (*sh.pe.values(), *sh.dve.values(), *sh.act.values(), *sh.pool.values(),
                                      *stack_landed, *raw_landed, *y_landed, *xs_landed, xr_landed, x1_stored,
                                      small) if f.count]



def cross_phase(nc, ctx, prog, sh, t, cross):
    sb = lambda name, shape, dt=F32: ctx.enter_context(nc.sbuf_tensor(name, shape, dt))
    put = prog.put
    wall = sh.wall
    stacks = Stacks(nc, ctx, prog, "cqk", 2, 3)
    stage = sb("cstage", [P, 4, SEQ])
    pt = [sb(f"cpt{i}", [P, PER, SEQ]) for i in range(LAG + 1)]
    v = [sb(f"cv{i}", [P, TILES, P]) for i in range(2)]
    v_landed = [prog.flag(f"cv_landed{i}") for i in range(2)]
    y = sb("cy", [P, GROUPS, SEQ])
    x1 = [sb(f"cx1_{i}", [P, TILES, DIM]) for i in range(2)]
    x1_landed = [prog.flag(f"cx1_landed{i}") for i in range(2)]
    x1t = sb("x1t", [P, 2, SEQ], F32R)
    x2 = sb("x2", [P, TILES, DIM])
    x2t_hi, x2t_lo = sb("x2t_hi", [P, GROUPS, SEQ], F32R), sb("x2t_lo", [P, GROUPS, SEQ], F32R)
    zt = sb("z", [P, DIM])
    tanh = [sb(f"tanh{i}", [P, DIM]) for i in range(2)]
    lt = sb("logits_t", [EXPERTS, SEQ])
    lg = sb("logits", [P, TILES, EXPERTS])
    gs = {n: sb(f"gate_{n}", [P, TILES]) for n in ("max", "sum", "rest", "keep0", "keep1", "w0", "w1")}
    ge = sb("gate_exp", [P, TILES, EXPERTS])
    gb = sb("gate_beats", [P, TILES, EXPERTS])
    ln2 = LayerNorm(nc, ctx, sh, prog, "ln2")
    ln3 = LayerNorm(nc, ctx, sh, prog, "ln3")
    out_stored = prog.flag("out_stored")
    k_landed = prog.flag("c_keys_landed")
    ones_ready = open_softmax(nc, ctx, sh, stacks, "cross")
    maxima_banks, Y, dense = Banks(0, 1), 4, Banks(5, 6, 7)

    wo, a_hi, a_lo, e_hi, e_lo, bo, be = cross.wo, cross.a_hi, cross.a_lo, cross.e_hi, cross.e_lo, cross.bo, cross.be
    gate_hi, gate_lo = cross.gate_hi, cross.gate_lo
    small_ready, a_ready, wo_ready, gate_ready, exp_ready = (
        cross.small_ready, cross.a_ready, cross.wo_ready, cross.gate_ready, cross.exp_ready)

    x1_ready, x1_used, x1_free = {}, {}, [None, None]

    def load_x1(b):
        x1_ready[b] = put("sync", lambda e: e.dma_start(
            x1[b % 2][:, :, :], t["x1"][b].rearrange("(k p) d -> p k d", p=P)),
            waits=[x1_free[b % 2], *wall], flag=x1_landed[b % 2], by=16)

    stage_free, x1t_free, keys_here = [()], [None], {}
    v_ready, v_free = {}, [None, None]

    def fetch_keys(g):
        b, h = divmod(g, GROUPS)
        keys_here[g] = put("sync", lambda e: e.dma_start(stage[:, 3, :], t["ctx_t"][b, h * P:h * P + P, :]),
                           waits=[*stage_free[0], *wall], flag=k_landed, by=16)

    def load_values(g):
        b, h = divmod(g, GROUPS)
        src = t["ctx"][b].rearrange("(k p) d -> p k d", p=P)[:, :, h * P:h * P + P]
        v_ready[g] = put("sync", lambda e: e.dma_start(v[g % 2][:, :, :], src), waits=[v_free[g % 2], *wall],
                         flag=v_landed[g % 2], by=16)

    def queries(g):
        b, h = divmod(g, GROUPS)
        bank = dense.turn()
        for k in range(TILES):
            done = put("tensor", lambda e, k=k: e.transpose(
                sh.bank[bank][:, k * P:k * P + P], x1[b % 2][:, k, h * P:h * P + P], sh.ident[:, :]),
                waits=[x1_ready[b], sh.bank_read[bank]], flag=sh.pe["small_t"])
        x1_used[b] = done
        got = put("scalar", lambda e: e.activation(x1t[:, 0, :], sh.bank[bank][:, :], ACT.Copy),
                  waits=[done, x1t_free[0], *wall], flag=sh.act["evac"])
        got = put("vector", lambda e: e.tensor_tensor(x1t[:, 1, :], sh.bank[bank][:, :],
                                                      x1t[:, 0, :].bitcast(F32), ALU.subtract),
                  waits=[got, x1t_free[0]], flag=sh.dve["split"])
        sh.bank_read[bank] = got
        yield 450
        bank2 = dense.turn()
        pairs = [((a_hi[:, :], a_lo[:, :]), (x1t[:, 0, :], x1t[:, 1, :]))]
        done = yield from matmul3(prog, sh.bank[bank2][:, :], pairs, [a_ready, got, sh.bank_read[bank2]],
                                  sh.pe["dense"])
        x1t_free[0] = done
        q_hi, q_lo, k_hi, k_lo = (stage[:, i, :] for i in range(4))
        split(prog, "scalar", k_hi.bitcast(F32R), k_lo.bitcast(F32R), k_lo, [keys_here[g]], sh.dve["split"],
              sh.act["evac"])
        hi = put("scalar", lambda e: e.activation(q_hi.bitcast(F32R), sh.bank[bank2][:, :], ACT.Copy),
                 waits=[done, *stage_free[0]], flag=sh.act["evac"])
        staged = put("vector", lambda e: e.tensor_tensor(q_lo.bitcast(F32R), sh.bank[bank2][:, :], q_hi, ALU.subtract),
                     waits=[hi, *stage_free[0]], flag=sh.dve["split"])
        sh.bank_read[bank2] = staged
        stage_free[0] = stacks.load(g, stage, staged)
        yield 3 * SEQ / 2.4

    p_free, p_ready = [()] * (LAG + 1), {}
    y_ready, y_free, y_raw_ready = {}, [None], {}

    def sums(g, kt):
        u = (g * TILES + kt) % (LAG + 1)
        rows = weighted_sum(sh, prog, pt[u], p_ready[(g, kt)],
                            lambda j: v[g % 2][:, kt, HEAD_DIM * j:HEAD_DIM * j + HEAD_DIM],
                            v_ready[g], kt, False, Y, sh.pe["pv"])
        p_free[u] = (rows, sh.add_done[(g, max(kt, 1))])
        if kt == TILES - 1:
            v_free[g % 2] = rows
            y_raw_ready[g] = evacuate(sh, prog, sh.norm["raw"], Y, rows)
        yield 4 * SEQ / 2.4

    def outputs(g):
        b, h = divmod(g, GROUPS)
        yield from normalise(sh, prog, sh.norm, dense, y[:, h, :], (y_raw_ready[g], sh.total_ready[g]), y_free[0])
        y_ready[b] = sh.norm["last"]

    def maxima(g, j):
        yield from head_max(sh, prog, stacks, maxima_banks, g, j, False)
        if j == PER - 1:
            yield PAUSE
            shift_rows(sh, prog, stacks, g, sh.maxed[g], dense.turn())
            yield 53

    x2_ready, x2_free, x2t_ready, x2t_free = {}, [None], {}, [None]

    def project_out(b, k):
        bank = dense.hold()
        x = x1[b % 2][:, k, :]
        biased = on_pool(sh, lambda e: e.tensor_tensor(x, x, bo[:, :], ALU.add), [small_ready, x1_used[b]],
                         sh.pool["mask"])
        for c in range(GROUPS):
            done = put("tensor", lambda e, c=c: e.matmul(
                sh.bank[bank][:, :], y[:, c, k * P:k * P + P], wo[:, c, :],
                start=(c == 0), stop=(c == GROUPS - 1)),
                waits=[y_ready[b], wo_ready, sh.bank_read[bank]], flag=sh.pe["dense"])
            if c < GROUPS - 1:
                yield 4 * SEQ / 2.4
        if k == TILES - 1:
            y_free[0] = done
        got = put("vector", lambda e: e.tensor_tensor(x, sh.bank[bank][:, :], x, ALU.add),
                  waits=[done, biased], flag=sh.dve["misc"])
        sh.bank_read[bank] = got
        dense.release(bank)
        ln2.statistics(k, x, got)
        yield 4 * SEQ / 2.4
        if k < TILES - 1:
            return
        yield from ln2.scales()
        yield PAUSE
        for i in range(TILES):
            got = ln2.apply(i, x2[:, i, :], x1[b % 2][:, i, :], [x2_free[0]])
            yield 1
        x2_ready[b] = x1_free[b % 2] = got

    def transpose_x2(b, c):
        bank = dense.turn()
        for k in range(TILES):
            done = put("tensor", lambda e, k=k: e.transpose(
                sh.bank[bank][:, k * P:k * P + P], x2[:, k, c * P:c * P + P], sh.ident[:, :]),
                waits=[x2_ready[b], sh.bank_read[bank]], flag=sh.pe["small_t"])
        hi = put("scalar", lambda e: e.activation(x2t_hi[:, c, :], sh.bank[bank][:, :], ACT.Copy),
                 waits=[done, x2t_free[0], *wall], flag=sh.act["evac"])
        x2t_ready[b] = put("vector", lambda e: e.tensor_tensor(
            x2t_lo[:, c, :], sh.bank[bank][:, :], x2t_hi[:, c, :].bitcast(F32), ALU.subtract),
            waits=[hi, x2t_free[0]], flag=sh.dve["split"])
        sh.bank_read[bank] = x2t_ready[b]
        yield TILES * 53 + PAUSE

    gates_done = {}
    gate_last, gate_used = [None], [None]

    def gates(b):
        bank = dense.hold()
        pairs = [((gate_hi[:, c, :], gate_lo[:, c, :]), (x2t_hi[:, c, :], x2t_lo[:, c, :])) for c in range(GROUPS)]
        done = yield from matmul3(prog, sh.bank[bank][0:EXPERTS, :], pairs,
                                  [gate_ready, x2t_ready[b], sh.bank_read[bank]], sh.pe["dense"])
        got = put("scalar", lambda e: e.activation(lt[:, :], sh.bank[bank][0:EXPERTS, :], ACT.Copy),
                  waits=[done, gate_last[0], *wall], flag=sh.act["evac"])
        sh.bank_read[bank] = got
        dense.release(bank)
        yield 2 * PAUSE
        bank2 = dense.turn()
        for k in range(TILES):
            done = put("tensor", lambda e, k=k: e.transpose(
                sh.bank[bank2][:, k * EXPERTS:(k + 1) * EXPERTS], lt[:, k * P:k * P + P],
                sh.ident[0:EXPERTS, 0:EXPERTS]),
                waits=[got, sh.bank_read[bank2]], flag=sh.pe["small_t"])
        dv = lambda f, *w: put("vector", f, waits=w, flag=sh.dve["ffn"])
        g = dv(lambda e: e.tensor_copy(lg[:, :, :].rearrange("p k x -> p (k x)"),
                                       sh.bank[bank2][:, 0:TILES * EXPERTS]), done, gate_used[0])
        sh.bank_read[bank2] = g
        col = lambda n: gs[n][:, :]
        wide = lambda ap, n=EXPERTS: ap.unsqueeze(2).to_broadcast([P, TILES, n])
        g = dv(lambda e: e.reduce_max(col("max"), lg[:, :, :], AX), g)
        g = dv(lambda e: e.tensor_tensor(ge[:, :, :], lg[:, :, :], wide(col("max")), ALU.subtract), g)
        yield 2 * PAUSE
        x = put("scalar", lambda e: e.activation(ge[:, :, :], ge[:, :, :], ACT.Exp), waits=[g], flag=sh.act["misc"])
        yield 2 * PAUSE
        g = dv(lambda e: e.reduce_sum(col("rest"), ge[:, :, :], AX), x)
        g = dv(lambda e: e.reciprocal(col("sum"), col("rest")), g)
        g = dv(lambda e: e.reduce_max(col("rest"), lg[:, :, 1:EXPERTS], AX), g)
        g = dv(lambda e: e.tensor_tensor(col("keep0"), lg[:, :, 0], col("rest"), ALU.is_ge), g)
        g = dv(lambda e: e.tensor_tensor(gb[:, :, :], lg[:, :, :], wide(lg[:, :, 1]), ALU.is_gt), g)
        g = dv(lambda e: e.tensor_tensor(gb[:, :, 0], lg[:, :, 0], lg[:, :, 1], ALU.is_ge), g)
        g = dv(lambda e: e.reduce_sum(col("rest"), gb[:, :, :], AX), g)
        g = dv(lambda e: e.tensor_scalar(col("keep1"), col("rest"), 1.0, 0.5, ALU.is_equal, ALU.mult), g)
        g = dv(lambda e: e.tensor_scalar(col("keep0"), col("keep0"), 0.5, None, ALU.mult), g)
        for i in (0, 1):
            g = dv(lambda e, i=i: e.tensor_tensor(col(f"w{i}"), ge[:, :, i], col("sum"), ALU.mult), g)
            g = dv(lambda e, i=i: e.tensor_tensor(col(f"w{i}"), col(f"w{i}"), col(f"keep{i}"), ALU.mult), g)
        gates_done[b] = gate_last[0] = g
        yield 3 * SEQ / 2.4

    z_free, tanh_free, x2_added = [None], [None, None], {}

    def expert(b, k, i):
        bank = dense.hold()
        pairs = [((x2t_hi[:, c, k * P:k * P + P], x2t_lo[:, c, k * P:k * P + P]),
                  (e_hi[:, i, c, :], e_lo[:, i, c, :])) for c in range(GROUPS)]
        done = yield from matmul3(prog, sh.bank[bank][:, :], pairs, [exp_ready, x2t_ready[b], sh.bank_read[bank]],
                                  sh.pe["dense"])
        if k == TILES - 1 and i == 1:
            x2t_free[0] = done
        z, r = zt[:, :], i
        g = put("vector", lambda e: e.tensor_tensor(z, sh.bank[bank][:, :], be[:, i, :], ALU.add),
                waits=[done, small_ready, z_free[0]], flag=sh.dve["ffn"])
        sh.bank_read[bank] = g
        dense.release(bank)
        yield PAUSE
        a = put("scalar", lambda e: e.activation(tanh[r][:, :], z, ACT.Tanh, scale=0.5), waits=[g, tanh_free[r]],
                flag=sh.act["evac"])
        yield 2 * PAUSE
        g = put("vector", lambda e: e.scalar_tensor_tensor(out=tanh[r][:, :], in0=tanh[r][:, :], scalar=1.0, in1=z,
                                                           op0=ALU.add, op1=ALU.mult), waits=[a], flag=sh.dve["ffn"])
        z_free[0] = g
        yield 2 * PAUSE
        w = gs[f"w{i}"][:, k:k + 1]
        g = put("scalar", lambda e: e.activation(tanh[r][:, :], tanh[r][:, :], ACT.Copy, scale=w),
                waits=[g, gates_done[b]], flag=sh.act["evac"])
        gate_used[0] = g
        yield PAUSE
        tanh_free[r] = g = on_pool(sh, lambda e: e.tensor_tensor(x2[:, k, :], x2[:, k, :], tanh[r][:, :], ALU.add),
                                   [g, x2t_ready[b]], sh.pool["mask"])
        yield 3 * SEQ / 2.4
        if i == 0 and k > 0:
            ln3.statistics(k - 1, x2[:, k - 1, :], x2_added[k - 1])
        x2_added[k] = g
        if i == 0 or k < TILES - 1:
            return
        yield 4 * PAUSE
        ln3.statistics(k, x2[:, k, :], g)
        yield from ln3.scales()
        yield PAUSE
        for n in range(TILES):
            got = ln3.apply(n, x2[:, n, :], x2[:, n, :])
            yield 1
        x2_free[0] = put("sync", lambda e: e.dma_start(t["out"][b].rearrange("(k p) d -> p k d", p=P), x2[:, :, :]),
                         waits=[got], flag=out_stored, by=16)

    PROJECT_SHARE, FEED_SHARE = 4900, 3900
    projected, fed = {}, {}

    def after(b, step):
        if step == 4:
            projected[b] = Background(*(project_out(b, k) for k in range(TILES)))
            fed[b] = Background(*(transpose_x2(b, c) for c in range(GROUPS)), gates(b),
                                *(expert(b, k, i) for k in range(TILES) for i in (0, 1)))
        if 4 <= step < 6:
            return projected[b].share(PROJECT_SHARE), PROJECT_SHARE
        if step == 6:
            return projected[b].rest(), PROJECT_SHARE
        if 8 <= step < STEPS + 4:
            return fed[b].share(FEED_SHARE), FEED_SHARE
        if step == STEPS + 4:
            return fed[b].rest(), FEED_SHARE
        return None, 0

    load_x1(0)
    for g in range(2):
        load_values(g)
        fetch_keys(g)
        run(queries(g))
    fetch_keys(2)
    for n in range(LEAD):
        run(maxima(*divmod(n, PER)))
    put("tensor", lambda e: e.nop(), waits=[ones_ready])
    pending = []
    for g in range(NG):
        b, h = divmod(g, GROUPS)
        for kt in range(TILES):
            step, ahead = h * TILES + kt, g * TILES + kt + LEAD
            u = (g * TILES + kt) % (LAG + 1)
            if kt == LAG and g >= 1 and g + 1 < NG:
                load_values(g + 1)
            if kt == 1 and g + 3 < NG:
                fetch_keys(g + 3)
            if step == 7 and b + 1 < BATCH:
                load_x1(b + 1)
            weave(
                (softmax_attention(sh, prog, stacks, g, kt, False, SCALE_CROSS, pt, p_free[u], p_ready), 1100),
                (sums(*pending.pop(0)) if len(pending) == LAG else None, 950),
                (maxima(*divmod(ahead, PER)) if ahead < NG * PER else None, 900),
                (queries(g + 2) if kt == 0 and g + 2 < NG else None, 900),
                (normal.share(225) if kt >= 2 and g > 0 else None, 225),
                after(b - 1, step) if b > 0 else (None, 0),
                after(b - 2, step + STEPS) if b > 1 else (None, 0),
            )
            if kt == 0 and g > 0:
                total_sums(sh, prog, g - 1, dense.turn())
                normal = Background(outputs(g - 1))
            pending.append((g, kt))
    for job in pending:
        run(sums(*job))
    total_sums(sh, prog, NG - 1, dense.turn())
    run(outputs(NG - 1))
    for b in (BATCH - 2, BATCH - 1):
        if b == BATCH - 1:
            after(b, 4)
            run(projected[b].rest())
        run(fed[b].rest())
    sh.stores = [(out_stored, out_stored.count)]



SCRATCH = {"y_ar": [BATCH, DIM, SEQ], "memory": [BATCH, GROUPS, P, 4, SEQ], "x1": [BATCH, SEQ, DIM]}


def kernel(x, ctx_1024, L0_attn_w_attn, L0_attn_b_attn, L0_attn_w_k2, L0_attn_b_k2, L0_attn_w_proj,
           L0_attn_b_proj, L0_xattn_Wv, L0_xattn_Wk, L0_xattn_Wq, L0_xattn_Wo, L0_xattn_bo,
           L0_ffn_gate_w, L0_ffn_w0, L0_ffn_b0, L0_ffn_w1, L0_ffn_b1):
    import concourse.bacc as bacc
    from concourse.bass_utils import run_bass_kernel_spmd

    def c(a):
        return np.ascontiguousarray(a)

    def columns(bias):
        return c(np.asarray(bias).reshape(-1, P).T)

    x, ctx_1024 = np.asarray(x), np.asarray(ctx_1024)
    arrays = {
        "x": c(x), "x_t": c(x.transpose(0, 2, 1)),
        "ctx": c(ctx_1024), "ctx_t": c(ctx_1024.transpose(0, 2, 1)),
        "w_attn_t": c(np.asarray(L0_attn_w_attn).T), "b_attn": columns(L0_attn_b_attn),
        "w_k2_t": c(np.asarray(L0_attn_w_k2).T), "b_k2": columns(L0_attn_b_k2),
        "w_proj_t": c(np.asarray(L0_attn_w_proj).T), "b_proj": c(np.asarray(L0_attn_b_proj)),
        "wv": c(L0_xattn_Wv), "wk": c(L0_xattn_Wk), "wq": c(L0_xattn_Wq),
        "wo_t": c(np.asarray(L0_xattn_Wo).T), "bo": c(np.asarray(L0_xattn_bo)),
        "gate_w": c(L0_ffn_gate_w),
        "w0_t": c(np.asarray(L0_ffn_w0).T), "b0": c(np.asarray(L0_ffn_b0)),
        "w1_t": c(np.asarray(L0_ffn_w1).T), "b1": c(np.asarray(L0_ffn_b1)),
    }
    nc = bacc.Bacc("TRN2", target_bir_lowering=False, num_devices=1)
    t = {n: nc.dram_tensor(f"in_{n}", list(a.shape), F32, kind="ExternalInput").ap() for n, a in arrays.items()}
    for n, shape in SCRATCH.items():
        t[n] = nc.dram_tensor(f"scratch_{n}", shape, F32, kind="Internal").ap()
    t["out"] = nc.dram_tensor("out", [BATCH, SEQ, DIM], F32, kind="ExternalOutput").ap()
    build(nc, t)
    r = run_bass_kernel_spmd(nc, [{f"in_{n}": a for n, a in arrays.items()}], core_ids=[0])
    return r.results[0]["out"]
```
